# Optimizing a Trainium2 kernel written in Bass

```python
import numpy as np
import jax
import jax.numpy as jnp

def _softmax(x, axis=-1):
    return jax.nn.softmax(x, axis=axis)

def _gelu(x):
    return jax.nn.gelu(x, approximate=True)

def _silu(x):
    return jax.nn.silu(x)

def _sigmoid(x):
    return jax.nn.sigmoid(x)

def _layernorm(x, axis=-1, eps=1e-05):
    m = jnp.mean(x, axis=axis, keepdims=True)
    v = jnp.var(x, axis=axis, keepdims=True)
    return (x - m) / jnp.sqrt(v + eps)

def _scatter_add(tgt, idx, src, axis=0):
    return tgt.at[idx].add(src)

def _segment_sum(src, seg, n):
    return jax.ops.segment_sum(src, seg, n)
kernel_name = 'mk_seq_preln_d1_jaxref_r4_dde111'

def setup_inputs(seed: int=0):
    np.random.seed(seed)
    _w = jnp.asarray

    def _L0_attn_setup():
        import jax, jax.numpy as jnp
        import numpy as np
        B, S, D, H = (2, 512, 256, 16)
        HD = D // H
        key = jax.random.key(seed)
        ks = jax.random.split(key, 16)
        sc = 0.02
        return {'hidden_states': jax.random.normal(ks[0], (B, S, D), jnp.float32), 'Wq': jax.random.normal(ks[1], (D, D), jnp.float32) * sc, 'bq': jnp.zeros((D,), jnp.float32), 'Wk': jax.random.normal(ks[2], (D, D), jnp.float32) * sc, 'bk': jnp.zeros((D,), jnp.float32), 'Wv': jax.random.normal(ks[3], (D, D), jnp.float32) * sc, 'bv': jnp.zeros((D,), jnp.float32), 'Wo': jax.random.normal(ks[4], (D, D), jnp.float32) * sc, 'bo': jnp.zeros((D,), jnp.float32), 'rel_W': jax.random.normal(ks[5], (3, 2 * D), jnp.float32) * sc, 'rel_b': jnp.zeros((3,), jnp.float32), 'logical_bias': jax.random.normal(ks[6], (H, 3), jnp.float32) * sc, 'gate_W': jax.random.normal(ks[7], (H, D), jnp.float32) * sc, 'gate_b': jnp.zeros((H,), jnp.float32)}
    _L0_attn_in = _L0_attn_setup()

    def _L0_ffn_setup():
        import jax, jax.numpy as jnp
        import numpy as np
        D_MODEL, D_FF, N_EXPERTS, TOP_K = (256, 1024, 8, 2)
        key = jax.random.key(seed)
        k0, k1, k2, k3 = jax.random.split(key, 4)
        x = jax.random.normal(k0, (2, 512, D_MODEL), dtype=jnp.float32)
        Wg = jax.random.normal(k1, (D_MODEL, N_EXPERTS), dtype=jnp.float32) * 0.02
        W1 = jax.random.normal(k2, (N_EXPERTS, D_MODEL, D_FF), dtype=jnp.float32) * 0.02
        b1 = jnp.zeros((N_EXPERTS, D_FF), dtype=jnp.float32)
        W2 = jax.random.normal(k3, (N_EXPERTS, D_FF, D_MODEL), dtype=jnp.float32) * 0.02
        b2 = jnp.zeros((N_EXPERTS, D_MODEL), dtype=jnp.float32)
        return {'x': x, 'Wg': Wg, 'W1': W1, 'b1': b1, 'W2': W2, 'b2': b2}
    _L0_ffn_in = _L0_ffn_setup()
    _d = {'L0_attn_hidden_states': _L0_attn_in['hidden_states'], 'L0_attn_Wq': _L0_attn_in['Wq'], 'L0_attn_bq': _L0_attn_in['bq'], 'L0_attn_Wk': _L0_attn_in['Wk'], 'L0_attn_bk': _L0_attn_in['bk'], 'L0_attn_Wv': _L0_attn_in['Wv'], 'L0_attn_bv': _L0_attn_in['bv'], 'L0_attn_Wo': _L0_attn_in['Wo'], 'L0_attn_bo': _L0_attn_in['bo'], 'L0_attn_rel_W': _L0_attn_in['rel_W'], 'L0_attn_rel_b': _L0_attn_in['rel_b'], 'L0_attn_logical_bias': _L0_attn_in['logical_bias'], 'L0_attn_gate_W': _L0_attn_in['gate_W'], 'L0_attn_gate_b': _L0_attn_in['gate_b'], 'L0_ffn_Wg': _L0_ffn_in['Wg'], 'L0_ffn_W1': _L0_ffn_in['W1'], 'L0_ffn_b1': _L0_ffn_in['b1'], 'L0_ffn_W2': _L0_ffn_in['W2'], 'L0_ffn_b2': _L0_ffn_in['b2']}
    _x0 = _d['L0_attn_hidden_states']
    _d['L0_attn_hidden_states'] = jax.random.normal(jax.random.fold_in(jax.random.key(seed), 1), (1, 4096, 256), dtype=_x0.dtype)
    del _x0
    return _d

def reference(L0_attn_hidden_states, L0_attn_Wq, L0_attn_bq, L0_attn_Wk, L0_attn_bk, L0_attn_Wv, L0_attn_bv, L0_attn_Wo, L0_attn_bo, L0_attn_rel_W, L0_attn_rel_b, L0_attn_logical_bias, L0_attn_gate_W, L0_attn_gate_b, L0_ffn_Wg, L0_ffn_W1, L0_ffn_b1, L0_ffn_W2, L0_ffn_b2):

    def _L0_attn_ref(hidden_states, Wq, bq, Wk, bk, Wv, bv, Wo, bo, rel_W, rel_b, logical_bias, gate_W, gate_b):
        import jax, jax.numpy as jnp
        import numpy as np
        B, S, D, H = (2, 512, 256, 16)
        HD = D // H
        x = hidden_states
        b, s, d = x.shape
        h = gate_W.shape[0]
        hd = d // h
        scale = hd ** 0.5
        q = (x @ Wq.T + bq).reshape(b, s, h, hd)
        k = (x @ Wk.T + bk).reshape(b, s, h, hd)
        v = (x @ Wv.T + bv).reshape(b, s, h, hd)
        attn_scores = jnp.einsum('bihd,bjhd->bhij', q, k) / scale
        li = x @ rel_W[:, :d].T
        lj = x @ rel_W[:, d:].T
        logits = li[:, :, None, :] + lj[:, None, :, :] + rel_b
        relation_probs = jax.nn.softmax(logits, axis=-1)
        bias = jnp.einsum('bijk,hk->bhij', relation_probs, logical_bias)
        gate = jax.nn.sigmoid(x @ gate_W.T + gate_b)
        gate = jnp.transpose(gate, (0, 2, 1))[..., None]
        attn_scores = attn_scores + gate * bias
        attn_weights = jax.nn.softmax(attn_scores, axis=-1)
        out = jnp.einsum('bhij,bjhd->bihd', attn_weights, v).reshape(b, s, d)
        return out @ Wo.T + bo

    def _L0_ffn_ref(x, Wg, W1, b1, W2, b2):
        import jax, jax.numpy as jnp
        import numpy as np
        D_MODEL, D_FF, N_EXPERTS, TOP_K = (256, 1024, 8, 2)
        B = x.shape[:-1]
        xs = x.reshape(-1, x.shape[-1])
        T = xs.shape[0]
        gate_logits = xs @ Wg
        weights, sel = jax.lax.top_k(gate_logits, TOP_K)
        weights = jax.nn.softmax(weights.astype(jnp.float32), axis=1).astype(x.dtype)
        h = jax.nn.relu(jnp.einsum('td,edf->etf', xs, W1) + b1[:, None, :])
        out_e = jnp.einsum('etf,efd->etd', h, W2) + b2[:, None, :]
        tok = jnp.arange(T)
        picked = out_e[sel, tok[:, None]]
        out = jnp.einsum('tk,tkd->td', weights, picked)
        return out.reshape(*B, x.shape[-1])
    x = L0_attn_hidden_states
    x = x + _L0_attn_ref(_layernorm(x, axis=-1), L0_attn_Wq, L0_attn_bq, L0_attn_Wk, L0_attn_bk, L0_attn_Wv, L0_attn_bv, L0_attn_Wo, L0_attn_bo, L0_attn_rel_W, L0_attn_rel_b, L0_attn_logical_bias, L0_attn_gate_W, L0_attn_gate_b)
    x = x + _L0_ffn_ref(_layernorm(x, axis=-1), L0_ffn_Wg, L0_ffn_W1, L0_ffn_b1, L0_ffn_W2, L0_ffn_b2)
    return x

_drawn_inputs = setup_inputs


def setup_inputs(seed=0):
    import zlib

    import numpy as np

    out = dict(_drawn_inputs(seed))
    spreads = {'L0_attn_bq': (0.0, 0.8),
     'L0_attn_bk': (0.0, 2.0),
     'L0_attn_bv': (0.0, 0.1),
     'L0_attn_bo': (0.0, 0.1),
     'L0_attn_rel_b': (0.0, 2.0),
     'L0_attn_gate_b': (0.0, 2.0),
     'L0_ffn_b1': (0.0, 0.286),
     'L0_ffn_b2': (0.0, 0.1)}
    factors = {'L0_attn_Wq': 8.0,
     'L0_attn_Wk': 8.0,
     'L0_attn_Wv': 8.0,
     'L0_attn_rel_W': 33.634,
     'L0_attn_logical_bias': 31.77,
     'L0_attn_gate_W': 53.621}
    for name, (base, spread) in spreads.items():
        noise = np.random.default_rng([zlib.crc32(name.encode()), seed]).standard_normal(out[name].shape)
        drawn = base * np.exp(spread * noise) if base else spread * noise
        out[name] = jnp.asarray(drawn.astype(out[name].dtype))
    for name, factor in factors.items():
        out[name] = (out[name] * factor).astype(out[name].dtype)
    return out
```

```python
from contextlib import ExitStack

import concourse.bass as bass
from concourse import mybir

F32 = mybir.dt.float32
F16 = mybir.dt.float16
U32 = mybir.dt.uint32
ALU = mybir.AluOpType
ACT = mybir.ActivationFunctionType
AX = mybir.AxisListType

P = 128
S, D, H, HD = 4096, 256, 16, 16
NT = S // P
KC = D // P
PAIRS = H // 2
HH = H // 2
NB, BI = 8, 16
JU = 512
UNITS = S // JU
SPU = 2 * JU // P
STEPS = 2 * NT
VW = HD + 1
VPAD = H * VW + 15
E, F, TOP = 8, 1024, 2
FT = F // P
TB = 512
NTB = S // TB
EPS = 1e-5
EXP_MAX = 43.0
ROWS = 6 * BI
MX_FIRST, MX_LAST = 4, 60


def mx_units(m):
    m = min(max(m - MX_FIRST, 0), MX_LAST - MX_FIRST)
    return m * STEPS // (MX_LAST - MX_FIRST)


def bank_owner(jobs, n, ring=8):
    if n < ring:
        return None
    eng = jobs[n - ring]
    return eng, sum(1 for e in jobs[:n - ring + 1] if e == eng)


def identity_into(nc, pool, t, zeroed, made):
    nc.gpsimd.memset(t, 0.0).then_inc(zeroed, 1)
    pool.wait_ge(zeroed, 1)
    nc.gpsimd.affine_select(out=t, in_=t, compare_op=ALU.not_equal, fill=1.0, base=0,
                            pattern=[[-1, P]], channel_multiplier=1).then_inc(made, 1)


def project_inputs(nc, kst, vp, hidden, wqT, bq, wkT, bk, wvT, bv, relT, rel_b, lbT, gwT, gate_b,
                   q_dram, c_dram, const_dram, dj_dram):
    with ExitStack() as ctx:
        def sb(name, shape, dt=F32):
            return ctx.enter_context(nc.sbuf_tensor("a_" + name, shape, dt))

        def sem(name):
            return ctx.enter_context(nc.semaphore("a_" + name))

        ps = ctx.enter_context(nc.psum_tensor("a_ps", [P, 8, 512], F32))
        x_room = sb("x_room", [P, NT * D])
        x = x_room[:, :].rearrange("p (t d) -> p t d", t=NT)
        part_lo = x_room[:, :].bitcast(F16).rearrange("p (m s) -> p m s", m=4)
        part_hi = sb("part_hi", [P, 2, S], F16)
        xnT = sb("xnT", [P, KC, S])
        stats = sb("stats", [P, 2, 6])
        mv = sb("mv", [P, NT, 2])
        std = sb("std", [P, NT])
        rstd = sb("rstd", [P, NT])
        ident = sb("ident", [P, P])
        wq = sb("wq", [P, 2, KC, D])
        wv = sb("wv", [P, KC, D])
        rel = sb("rel", [P, 2, KC, 3])
        gw = sb("gw", [P, KC, H + 4])
        wdj = sb("wdj", [P, KC, 3])
        bqk = sb("bqk", [P, 4])
        bvb = sb("bvb", [P, D])
        gb = sb("gb", [P, H + 4])
        rb = sb("rb", [P, 3])
        lb = sb("lb", [P, 3, H])
        lbd = sb("lbd", [P, 2, H])
        mb = sb("mb", [P, H])
        qk32 = sb("qk32", [P, 2, 512])
        g = sb("g", [P, NT, H + 4])
        gate = sb("gate", [P, NT, H])
        consts = sb("consts", [P, NT, H + 4])
        chi = sb("chi", [P, 2, NT, H], F16)
        clo = sb("clo", [P, 2, NT, H], F16)
        zero16 = sb("zero16", [BI, PAIRS * P], F16)

        x_in, w_in, zeroed, ident_made, zero_made = (sem(n) for n in (
            "x_in", "w_in", "zeroed", "ident_made", "zero_made"))
        dve_step, act_step = sem("dve_step"), sem("act_step")
        var_done, std_done, xn_done, wts_done = (sem(n) for n in ("var_done", "std_done", "xn_done", "wts_done"))
        pe_job, act_job, dve_job = sem("pe_job"), sem("act_job"), sem("dve_job")
        qk_split = sem("qk_split")
        dj_out = [sem("dj_out0"), sem("dj_out1")]
        ez_done, consts_done, c_done = sem("ez_done"), sem("consts_done"), sem("c_done")
        stored, k_filled, g_ready = sem("stored"), sem("k_filled"), sem("g_ready")

        kinds = ([("T", j) for j in range(16)] + [("G", j) for j in range(2)]
                 + [("QK", j) for j in range(32)] + [("DJ", j) for j in range(8)]
                 + [("V", j) for j in range(16)])
        jobs = ["act" if k == "T" and j % 2 or k in ("QK", "DJ") else "dve" for k, j in kinds]
        freed = {"act": act_job, "dve": dve_job}
        first_qk = next(n for n, (k, _) in enumerate(kinds) if k == "QK")
        last_t = 16
        N_W = 14

        block = ctx.enter_context(nc.Block())

        def act_before(n):
            return sum(1 for e in jobs[:n] if e == "act")

        def dve_before(n):
            return sum(1 for e in jobs[:n] if e == "dve")

        @block.sync
        def _(sp):
            for q in range(4):
                sp.dma_start(x[:, 8 * q:8 * q + 8, :],
                             hidden.rearrange("o (t p) d -> p (o t) d", p=P)[:, 8 * q:8 * q + 8, :]).then_inc(x_in, 16)
            for dst, src in ((wq[:, 0], wqT.rearrange("(c p) n -> p c n", p=P)),
                             (wq[:, 1], wkT.rearrange("(c p) n -> p c n", p=P)),
                             (wv[:, :, :], wvT.rearrange("(c p) n -> p c n", p=P)),
                             (rel[:, 0], relT.rearrange("(two c p) k -> two p c k", p=P, two=2)[0]),
                             (rel[:, 1], relT.rearrange("(two c p) k -> two p c k", p=P, two=2)[1]),
                             (gw[:, :, 0:H], gwT.rearrange("(c p) n -> p c n", p=P)),
                             (bqk[:, 0:2], bq.rearrange("(c p) -> p c", p=P)),
                             (bqk[:, 2:4], bk.rearrange("(c p) -> p c", p=P)),
                             (bvb[:, :], bv.partition_broadcast(P)),
                             (gb[:, 0:H], gate_b.partition_broadcast(P)),
                             (rb[:, :], rel_b.partition_broadcast(P)),
                             (lb[:, 0, :], lbT[0].partition_broadcast(P)),
                             (lb[:, 1, :], lbT[1].partition_broadcast(P)),
                             (lb[:, 2, :], lbT[2].partition_broadcast(P))):
                sp.dma_start(dst, src, allow_slow_non_contiguous=True).then_inc(w_in, 16)
            sp.wait_ge(zero_made, 1)
            for xc in range(NT):
                for ab in range(2):
                    sp.dma_start(q_dram[xc, ab, 32:48], zero16[:, :].rearrange("r (q t) -> r q t", q=PAIRS)).then_inc(stored, 16)
            for m in range(4):
                sp.wait_ge(qk_split, 16 * (m + 1))
                for pp in range(4):
                    for ab in range(2):
                        r = 32 * pp + 16 * ab
                        pair = 4 * (m % 2) + pp
                        for row, part in ((0, "hi"), (16, "hi" if m < 2 else "lo"), (48, "lo" if m < 2 else "hi")):
                            src = part_hi[r:r + 16, m % 2, :] if part == "hi" else part_lo[r:r + 16, m, :]
                            if m < 2:
                                sp.dma_start(q_dram[:, ab, row:row + 16, pair, :].rearrange("x r t -> r x t"),
                                             src.rearrange("r (x t) -> r x t", t=P)).then_inc(stored, 16)
                            else:
                                sp.dma_start(kst[64 * ab + row:64 * ab + row + 16, pair, :], src).then_inc(k_filled, 16)
            first_dj = next(n for n, (k, _) in enumerate(kinds) if k == "DJ")
            for j in range(8):
                sp.wait_ge(act_job, act_before(first_dj + j) + 1)
                sp.dma_start(dj_dram[:, j * 512:j * 512 + 512], qk32[0:3, j % 2, :]).then_inc(dj_out[j % 2], 16)
            for q in dj_out:
                sp.wait_ge(q, 64)
            sp.wait_ge(consts_done, 2)
            sp.dma_start(const_dram.rearrange("x p n -> p x n"), consts[:, :, :]).then_inc(stored, 16)
            sp.wait_ge(c_done, 2)
            for part, t in ((0, chi), (1, chi), (2, clo)):
                for k in range(2):
                    sp.dma_start(c_dram[:, part, k].rearrange("x p h -> p x h"), t[:, k]).then_inc(stored, 16)
            sp.wait_ge(k_filled, 16 * 48)
            sp.wait_ge(stored, 16 * (64 + 48 + 1 + 6))

        @block.gpsimd
        def _(pool):
            nc.gpsimd.memset(zero16[:, :], 0.0).then_inc(zero_made, 1)
            identity_into(nc, pool, ident[:, :], zeroed, ident_made)

        @block.vector
        def _(dve):
            chain = [0]

            def link(ins):
                chain[0] += 1
                ins.then_inc(dve_step, 1)
                dve.wait_ge(dve_step, chain[0])

            nc.vector.memset(vp[:, :, :], 1.0).then_inc(wts_done, 1)
            for r in (32, 96):
                nc.vector.memset(kst[r:r + 16, :, :], 1.0).then_inc(wts_done, 1)
            dve.wait_ge(w_in, 16 * N_W)
            for n, (a, b) in enumerate(((1, 0), (2, 0), (0, 1), (2, 1))):
                nc.vector.tensor_tensor(gw[:, :, H + n:H + n + 1], rel[:, 0, :, a:a + 1], rel[:, 0, :, b:b + 1],
                                        ALU.subtract).then_inc(wts_done, 1)
                nc.vector.tensor_tensor(gb[:, H + n:H + n + 1], rb[:, a:a + 1], rb[:, b:b + 1],
                                        ALU.subtract).then_inc(wts_done, 1)
            for n, (a, b) in enumerate(((1, 0), (2, 0), (2, 1))):
                link(nc.vector.tensor_tensor(wdj[:, :, n:n + 1], rel[:, 1, :, a:a + 1], rel[:, 1, :, b:b + 1],
                                             ALU.subtract))
            for k in range(2):
                nc.vector.tensor_tensor(lbd[:, k], lb[:, k], lb[:, 2], ALU.subtract).then_inc(wts_done, 1)
            dve.wait_ge(wts_done, 13)
            link(nc.vector.tensor_tensor(mb[:, :], lbd[:, 0], lbd[:, 1], ALU.max))
            link(nc.vector.tensor_scalar(mb[:, :], mb[:, :], 0.0, None, ALU.max))
            dve.wait_ge(x_in, 64)
            for t in range(NT):
                link(nc.vector.bn_stats(stats[:, t % 2], x[:, t]))
                link(nc.vector.bn_aggr(mv[:, t], stats[:, t % 2]))
            nc.vector.tensor_scalar(rstd[:, :], mv[:, :, 1], EPS, None, ALU.add).then_inc(var_done, 1)
            dve.wait_ge(std_done, 1)
            link(nc.vector.reciprocal(rstd[:, :], std[:, :]))
            for t in range(NT):
                nc.vector.tensor_scalar(x[:, t], x[:, t], mv[:, t, 0:1], rstd[:, t:t + 1], ALU.subtract,
                                        ALU.mult).then_inc(xn_done, 1)
            for n, (kind, j) in enumerate(kinds):
                if kind == "QK":
                    m, tb = j // 8, j % 8
                    dve.wait_ge(act_job, act_before(n) + 1)
                    if n == first_qk:
                        dve.wait_ge(pe_job, last_t)
                    if m == 2 and tb == 0:
                        dve.wait_ge(stored, 16 * (2 * NT + 48))
                    cols = slice(tb * 512, tb * 512 + 512)
                    nc.vector.tensor_copy(part_hi[:, m % 2, cols], qk32[:, j % 2, :]).then_inc(qk_split, 1)
                    dve.wait_ge(qk_split, 2 * j + 1)
                    nc.vector.tensor_tensor(part_lo[:, m, cols], qk32[:, j % 2, :], part_hi[:, m % 2, cols],
                                            ALU.subtract).then_inc(qk_split, 1)
                if jobs[n] != "dve":
                    continue
                dve.wait_ge(pe_job, n + 1)
                if kind == "T":
                    nc.vector.tensor_copy(xnT[:, j % 2, (j // 2) * 512:(j // 2) * 512 + 512], ps[:, n % 8, :]).then_inc(dve_job, 1)
                if kind == "V":
                    dst = vp[:, 2 * j:2 * j + 2, 0:H * VW].rearrange("p t (h w) -> p t h w", w=VW)
                    for t in range(2):
                        ins = nc.vector.tensor_tensor(dst[:, t, :, 0:HD],
                                                      ps[:, n % 8, t * D:t * D + D].rearrange("p (h w) -> p h w", w=HD),
                                                      bvb[:, :].rearrange("p (h w) -> p h w", w=HD), ALU.add)
                    ins.then_inc(dve_job, 1)
                if kind == "G":
                    w = NT // 2 * (H + 4)
                    ins = nc.vector.tensor_tensor(g[:, j * 16:j * 16 + 16, :],
                                                  ps[:, n % 8, 0:w].rearrange("p (t n) -> p t n", n=H + 4),
                                                  gb[:, :].unsqueeze(1).broadcast_to([P, 16, H + 4]), ALU.add)
                    ins.then_inc(dve_job, 1)
            dve.wait_ge(ez_done, 1)
            link(nc.vector.tensor_scalar(gate[:, :, :], gate[:, :, :], 1.0, None, ALU.add))
            link(nc.vector.reciprocal(gate[:, :, :], gate[:, :, :]))
            nc.vector.tensor_copy(consts[:, :, 0:4], g[:, :, H:H + 4]).then_inc(consts_done, 1)
            nc.vector.tensor_tensor(consts[:, :, 4:4 + H], gate[:, :, :],
                                    mb[:, :].unsqueeze(1).broadcast_to([P, NT, H]), ALU.mult).then_inc(consts_done, 1)
            for k in range(2):
                link(nc.vector.tensor_tensor(g[:, :, 0:H], gate[:, :, :],
                                             lbd[:, k].unsqueeze(1).broadcast_to([P, NT, H]), ALU.mult))
                link(nc.vector.tensor_copy(chi[:, k], g[:, :, 0:H]))
                nc.vector.tensor_tensor(clo[:, k], g[:, :, 0:H], chi[:, k], ALU.subtract).then_inc(c_done, 1)
                dve.wait_ge(c_done, k + 1)

        @block.scalar
        def _(act):
            act.wait_ge(w_in, 16 * N_W)
            nc.scalar.mul(bqk[:, 0:2], bqk[:, 0:2], HD ** -0.5).then_inc(act_step, 1)
            act.wait_ge(act_step, 1)
            act.wait_ge(var_done, 1)
            nc.scalar.activation(std[:, :], rstd[:, :], ACT.Sqrt).then_inc(std_done, 1)
            for n, (kind, j) in enumerate(kinds):
                if jobs[n] != "act":
                    continue
                act.wait_ge(pe_job, n + 1)
                if kind == "T":
                    nc.scalar.copy(xnT[:, j % 2, (j // 2) * 512:(j // 2) * 512 + 512], ps[:, n % 8, :]).then_inc(act_job, 1)
                if kind == "DJ":
                    if j == 0:
                        act.wait_ge(qk_split, 64)
                    if j >= 2:
                        act.wait_ge(dj_out[j % 2], 16 * (j // 2))
                    nc.scalar.copy(qk32[0:3, j % 2, :], ps[0:3, n % 8, :]).then_inc(act_job, 1)
                if kind == "QK":
                    if j >= 2:
                        act.wait_ge(qk_split, 2 * (j - 1))
                    m = j // 8
                    nc.scalar.activation(qk32[:, j % 2, :], ps[:, n % 8, :], ACT.Identity, bias=bqk[:, m:m + 1],
                                         scale=HD ** -0.5 if m < 2 else 1.0).then_inc(act_job, 1)
            act.wait_ge(dve_job, dve_before(first_qk))
            nc.scalar.activation(gate[:, :, :], g[:, :, 0:H], ACT.Exp, scale=-1.0).then_inc(ez_done, 1)

        @block.tensor
        def _(pe):
            pe.wait_ge(w_in, 16 * N_W)
            pe.wait_ge(ident_made, 1)
            pe.wait_ge(wts_done, 13)
            for n, (kind, j) in enumerate(kinds):
                own = bank_owner(jobs, n)
                if own:
                    pe.wait_ge(freed[own[0]], own[1])
                if kind == "T":
                    c, tb = j % 2, j // 2
                    pe.wait_ge(xn_done, 4 * tb + 4)
                    for t in range(4):
                        ins = pe.transpose(ps[:, n % 8, t * P:t * P + P], x[:, 4 * tb + t, c * P:c * P + P], ident[:, :])
                if n == last_t:
                    pe.wait_ge(act_job, act_before(n))
                    pe.wait_ge(dve_job, dve_before(n))
                if kind == "G":
                    for t in range(16):
                        tile = 16 * j + t
                        for c in range(KC):
                            ins = pe.matmul(ps[:, n % 8, t * (H + 4):(t + 1) * (H + 4)], xnT[:, c, tile * P:tile * P + P],
                                            gw[:, c, :], start=(c == 0), stop=(c == KC - 1))
                if kind == "QK":
                    m, tb = j // 8, j % 8
                    for c in range(KC):
                        ins = pe.matmul(ps[:, n % 8, :], wq[:, m // 2, c, (m % 2) * P:(m % 2) * P + P],
                                        xnT[:, c, tb * 512:tb * 512 + 512], start=(c == 0), stop=(c == KC - 1))
                if kind == "DJ":
                    for c in range(KC):
                        ins = pe.matmul(ps[0:3, n % 8, :], wdj[:, c, :], xnT[:, c, j * 512:j * 512 + 512],
                                        start=(c == 0), stop=(c == KC - 1))
                if kind == "V":
                    for t in range(2):
                        tile = 2 * j + t
                        for c in range(KC):
                            ins = pe.matmul(ps[:, n % 8, t * D:t * D + D], xnT[:, c, tile * P:tile * P + P],
                                            wv[:, c, :], start=(c == 0), stop=(c == KC - 1))
                ins.then_inc(pe_job, 1)


def attend(nc, kst, vp, dj_dram, q_dram, c_dram, const_dram, r_dram, m_dram, att_dram):
    with ExitStack() as ctx:
        def sb(name, shape, dt=F32):
            return ctx.enter_context(nc.sbuf_tensor("b_" + name, shape, dt))

        def sem(name):
            return ctx.enter_context(nc.semaphore("b_" + name))

        sc = ctx.enter_context(nc.psum_tensor("b_sc", [P, 2, 2, 512], F32))
        mx = ctx.enter_context(nc.psum_tensor("b_mx", [P, 2 * 512], F32))
        acc = ctx.enter_context(nc.psum_tensor("b_acc", [P, 4, P], F32))
        tail = ctx.enter_context(nc.psum_tensor("b_tail", [P, 4, P], F32))

        dj = sb("dj", [P, 3, S])
        rst = sb("rst", [ROWS, 2, NB, JU], F16)
        pr = sb("pr", [P, 2, HH * P])
        qx = sb("qx", [P, PAIRS, 2, P], F16)
        qm = sb("qm", [P, PAIRS, 2, P], F16)
        cx = sb("cx", [ROWS, 2, NB, HH, BI], F16)
        cm = sb("cm", [ROWS, 2, NB, HH, BI], F16)
        cval = sb("cval", [ROWS, NB, H], F16)
        eye = sb("eye", [ROWS, BI], F16)
        ident = sb("ident", [P, P])
        const = sb("const", [P, H + 4])
        ex = sb("ex", [P, 2, 2, JU])
        rhi = sb("rhi", [P, 2, JU], F16)
        rlo = sb("rlo", [P, 2, JU], F16)
        mxp = sb("mxp", [P, H, 4])
        mrow = sb("mrow", [P, H])
        mT = sb("mT", [H, P])
        mparts = sb("mparts", [H, 3, P], F16)
        oT = sb("oT", [P, 4, P])
        rl = sb("rl", [P, H])
        att = sb("att", [P, H, HD])

        names = ("zeroed", "ident_made", "eye_made", "dj_in", "q_zeroed", "qx_in", "qxm_in", "const_in", "cval_in", "cx_made",
                 "turn0", "turn1", "scores_ready", "p_ready", "pv_done", "mx_ready", "mx_used", "m_step",
                 "m_neg", "m_turned", "m_parts", "m_out", "e_ready", "r_ready", "hi_ready", "lo_ready",
                 "r_out0", "r_out1", "r_in0", "r_in1", "acc_read", "o_turned", "att_step", "att_made", "att_out", "att_free", "att_zeroed", "sp_waited", "pool_waited", "d_ready", "sum_ready", "ln_ready")
        s = {n: sem(n) for n in names}

        block = ctx.enter_context(nc.Block())

        def waited(sp):
            sp.sem_inc(s["sp_waited"], 1)

        def sp_begin(sp, x):
            for ab in range(2):
                sp.dma_start(qx[64 * ab:64 * ab + 64, :, ab, :],
                             q_dram[bass.ds(x, 1), ab].rearrange("o r q t -> r (o q) t")).then_inc(s["qx_in"], 16)
            sp.dma_start(cval[:, :, :].rearrange("r b h -> r (b h)"),
                         c_dram[bass.ds(x, 1)].rearrange("o a k (i b) h -> (o a k i) (b h)", b=NB)).then_inc(s["cval_in"], 16)
            sp.dma_start(const[:, :], const_dram[bass.ds(x, 1)].rearrange("o p n -> (o p) n")).then_inc(s["const_in"], 16)

        def sp_write_r(sp, x, u):
            for k in range(2):
                sp.wait_ge(s["lo_ready"], 16 * x + 2 * u + k + 1)
                waited(sp)
                for part, t in ((0, rhi), (1, rlo)):
                    sp.dma_start(r_dram[bass.ds(x, 1), u, part, k].rearrange("o i j -> (o i) j"), t[:, k]).then_inc(
                        s[f"r_out{k}"], 16)

        def sp_read_r(sp, x, u, written):
            sp.wait_ge(s["r_out0"], 32 * written)
            sp.wait_ge(s["r_out1"], 32 * written)
            waited(sp)
            src = r_dram[bass.ds(x, 1), u].rearrange("o a k (i b) j -> (o a k i) (b j)", b=NB)
            dst = rst[:, u % 2].rearrange("r b j -> r (b j)")
            sp.dma_start(dst[0:64], src).then_inc(s[f"r_in{u % 2}"], 16)
            sp.dma_start(dst[64:96], src[0:32]).then_inc(s[f"r_in{u % 2}"], 16)

        def sp_m(sp, x):
            sp.wait_ge(s["m_parts"], 3 * x + 3)
            sp.dma_start(m_dram[:, :, :], mparts[:, :, :]).then_inc(s["m_out"], 16)
            sp.wait_ge(s["m_out"], 16 * x + 16)
            for ab in range(2):
                sp.dma_start(qx[64 * ab + 32:64 * ab + 35, :, ab, :],
                             m_dram.rearrange("(q ab) s i -> ab s q i", ab=2)[ab]).then_inc(s["qxm_in"], 16)

        def sp_turn(sp, x, half):
            if half == 0:
                sp.wait_ge(s["qxm_in"], 32 * x + 32)
                sp.wait_ge(s["cx_made"], 2 * x + 2)
            sp.dma_start(qm[:, 4 * half:4 * half + 4], qx[:, 4 * half:4 * half + 4]).then_inc(s[f"turn{half}"], 16)
            sp.dma_start(cm[:, half], cx[:, half]).then_inc(s[f"turn{half}"], 16)

        @block.sync
        def _(sp):
            for d in range(3):
                sp.dma_start(dj[:, d, :], dj_dram[d].partition_broadcast(P)).then_inc(s["dj_in"], 16)
            sp.wait_ge(s["q_zeroed"], 1)
            sp_begin(sp, 0)
            sp.wait_ge(s["att_zeroed"], 1)
            sp.dma_start(att_dram[0], att[:, :, :].rearrange("p h w -> p (h w)")).then_inc(s["att_out"], 16)
            for u in range(UNITS):
                sp_write_r(sp, 0, u)
            sp_m(sp, 0)
            sp_turn(sp, 0, 0)
            sp_turn(sp, 0, 1)
            sp_read_r(sp, 0, 0, UNITS)

            def chunk(c, last):
                if not last:
                    sp.wait_ge(s["turn0"], 32 * c + 32)
                    sp.wait_ge(s["turn1"], 32 * c + 32)
                    waited(sp)
                    sp_begin(sp, c + 1)
                for u in range(UNITS):
                    if u == UNITS - 1:
                        sp.wait_ge(s["att_out"], 16 * c + 16)
                        sp.sem_inc(s["att_free"], 1)
                    if u + 1 < UNITS:
                        if u > 0:
                            sp.wait_ge(s["scores_ready"], STEPS * c + SPU * u)
                        sp_read_r(sp, c, u + 1, UNITS * (c + 1) + (0 if last else u))
                    if not last:
                        sp_write_r(sp, c + 1, u)
                if not last:
                    sp_m(sp, c + 1)
                    sp.wait_ge(s["scores_ready"], STEPS * c + SPU * (UNITS - 1))
                    sp_read_r(sp, c + 1, 0, UNITS * (c + 2))
                    sp.wait_ge(s["scores_ready"], STEPS * c + STEPS - 1)
                    sp_turn(sp, c + 1, 0)
                    sp.wait_ge(s["scores_ready"], STEPS * c + STEPS)
                    sp_turn(sp, c + 1, 1)
                sp.wait_ge(s["att_made"], c + 1)
                waited(sp)
                sp.dma_start(att_dram[bass.ds(c, 1)].rearrange("o p n -> (o p) n"),
                             att[:, :, :].rearrange("p h w -> p (h w)")).then_inc(s["att_out"], 16)

            with sp.Fori(0, NT - 1) as c:
                chunk(c, False)
            chunk(NT - 1, True)
            sp.wait_ge(s["att_out"], 16 * NT + 16)

        def pool_c(pool, x):
            pool.wait_ge(s["cval_in"], 16 * x + 16)
            for half in range(2):
                nc.gpsimd.tensor_tensor(cx[:, half],
                                        cval[:, :, HH * half:HH * half + HH].unsqueeze(3).broadcast_to([ROWS, NB, HH, BI]),
                                        eye[:, :].unsqueeze(1).unsqueeze(1).broadcast_to([ROWS, NB, HH, BI]),
                                        ALU.mult).then_inc(s["cx_made"], 1)

        def pool_r(pool, x):
            pool.wait_ge(s["const_in"], 16 * x + 16)
            for u in range(UNITS):
                for k in range(2):
                    g = 16 * x + 2 * u + k
                    if not (isinstance(g, int) and g < 2):
                        pool.wait_ge(s["lo_ready"], g - 1)
                    pool.sem_inc(s["pool_waited"], 1)
                    cols = slice(u * JU, u * JU + JU)
                    for n, (d, b, limit, op) in enumerate((((0, 0, EXP_MAX, ALU.min), (1, 1, EXP_MAX, ALU.min)),
                                                           ((0, 0, -EXP_MAX, ALU.max), (2, 3, EXP_MAX, ALU.min)))[k]):
                        nc.gpsimd.tensor_scalar(ex[:, k, n], dj[:, d, cols], const[:, b:b + 1], limit, ALU.add,
                                                op).then_inc(s["d_ready"], 1)

        @block.gpsimd
        def _(pool):
            identity_into(nc, pool, ident[:, :], s["zeroed"], s["ident_made"])
            nc.gpsimd.memset(qx[:, :, :, :], 0.0).then_inc(s["q_zeroed"], 1)
            nc.gpsimd.memset(att[:, :, :], 0.0).then_inc(s["att_zeroed"], 1)
            nc.gpsimd.memset(eye[:, :], 0.0).then_inc(s["eye_made"], 1)
            for n in range(ROWS // BI):
                pool.wait_ge(s["eye_made"], n + 1)
                nc.gpsimd.affine_select(out=eye[:, :], in_=eye[:, :], compare_op=ALU.not_equal, fill=1.0,
                                        base=-BI * n, pattern=[[-1, BI]], channel_multiplier=1).then_inc(s["eye_made"], 1)
            pool.wait_ge(s["eye_made"], ROWS // BI + 1)
            pool.wait_ge(s["dj_in"], 48)
            pool_c(pool, 0)
            pool_r(pool, 0)
            with pool.Fori(0, NT - 1) as c:
                pool_c(pool, c + 1)
                pool_r(pool, c + 1)

        def act_r_exp(act, x, u, k):
            act.wait_ge(s["d_ready"], 2 * (16 * x + 2 * u + k) + 2)
            for n, sign in enumerate(((1.0, 1.0), (-1.0, 1.0))[k]):
                nc.scalar.activation(ex[:, k, n], ex[:, k, n], ACT.Exp, scale=sign).then_inc(s["e_ready"], 1)

        def act_r_inv(act, x, u, k):
            g = 16 * x + 2 * u + k
            act.wait_ge(s["sum_ready"], g + 1)
            nc.scalar.activation(ex[:, k, 0], ex[:, k, 0], ACT.Ln, bias=1.0).then_inc(s["ln_ready"], 1)
            act.wait_ge(s["ln_ready"], g + 1)
            nc.scalar.activation(ex[:, k, 0], ex[:, k, 0], ACT.Exp, scale=-1.0).then_inc(s["r_ready"], 1)

        @block.scalar
        def _(act):
            nc.scalar.preload_act_table_set("natural_log_exp_and_others")
            for u in range(UNITS):
                for k in range(2):
                    act_r_exp(act, 0, u, k)
                    act_r_inv(act, 0, u, k)

            def chunk(c, last):
                for m in range(STEPS):
                    act.wait_ge(s["scores_ready"], STEPS * c + m + 1)
                    if m >= 2:
                        act.wait_ge(s["pv_done"], STEPS * c + m - 1)
                    nc.scalar.activation(pr[:, m % 2, :], sc[:, m % 2].rearrange("p a b -> p (a b)"),
                                         ACT.Exp).then_inc(s["p_ready"], 1)
                    if not last:
                        u, k, at = m // SPU, m % SPU // 4, m % 4
                        if at == 0:
                            act_r_exp(act, c + 1, u, k)
                        if at == 2:
                            act_r_inv(act, c + 1, u, k)

            with act.Fori(0, NT - 1) as c:
                chunk(c, False)
            chunk(NT - 1, True)

        def dve_max(dve, x, n):
            dve.wait_ge(s["mx_ready"], STEPS * x + n + 1)
            nc.vector.tensor_reduce(mxp[:, n // 4, n % 4:n % 4 + 1], mx[:, :], AX.X, ALU.max).then_inc(s["mx_used"], 1)

        def dve_r_sum(dve, x, u, k):
            g = 16 * x + 2 * u + k
            dve.wait_ge(s["e_ready"], 2 * g + 2)
            nc.vector.tensor_tensor(ex[:, k, 0], ex[:, k, 0], ex[:, k, 1], ALU.add).then_inc(s["sum_ready"], 1)

        def dve_r_split(dve, x, u, k):
            g = 16 * x + 2 * u + k
            dve.wait_ge(s["r_ready"], g + 1)
            if not (isinstance(g, int) and g < 2):
                dve.wait_ge(s[f"r_out{k}"], 32 * (UNITS * x + u))
            nc.vector.tensor_copy(rhi[:, k], ex[:, k, 0]).then_inc(s["hi_ready"], 1)
            dve.wait_ge(s["hi_ready"], g + 1)
            nc.vector.tensor_tensor(rlo[:, k], ex[:, k, 0], rhi[:, k], ALU.subtract).then_inc(s["lo_ready"], 1)

        def dve_m(dve, x):
            dve.wait_ge(s["mx_used"], STEPS * x + STEPS)
            nc.vector.tensor_reduce(mrow[:, :], mxp[:, :, :], AX.X, ALU.max).then_inc(s["m_step"], 1)
            dve.wait_ge(s["m_step"], 4 * x + 1)
            dve.wait_ge(s["const_in"], 16 * x + 16)
            nc.vector.scalar_tensor_tensor(out=mrow[:, :], in0=mrow[:, :], scalar=-1.0, in1=const[:, 4:4 + H],
                                           op0=ALU.mult, op1=ALU.subtract).then_inc(s["m_neg"], 1)
            dve.wait_ge(s["m_turned"], x + 1)
            nc.vector.tensor_copy(mT[:, :], tail[0:H, 0, :]).then_inc(s["m_step"], 1)
            dve.wait_ge(s["m_step"], 4 * x + 2)
            if not (isinstance(x, int) and x == 0):
                dve.wait_ge(s["m_out"], 16 * x)
            nc.vector.tensor_copy(mparts[:, 0], mT[:, :]).then_inc(s["m_parts"], 1)
            dve.wait_ge(s["m_parts"], 3 * x + 1)
            nc.vector.tensor_tensor(mT[:, :], mT[:, :], mparts[:, 0], ALU.subtract).then_inc(s["m_step"], 1)
            dve.wait_ge(s["m_step"], 4 * x + 3)
            nc.vector.tensor_copy(mparts[:, 1], mT[:, :]).then_inc(s["m_parts"], 1)
            dve.wait_ge(s["m_parts"], 3 * x + 2)
            nc.vector.tensor_tensor(mT[:, :], mT[:, :], mparts[:, 1], ALU.subtract).then_inc(s["m_step"], 1)
            dve.wait_ge(s["m_step"], 4 * x + 4)
            nc.vector.tensor_copy(mparts[:, 2], mT[:, :]).then_inc(s["m_parts"], 1)
            dve.wait_ge(s["m_parts"], 3 * x + 3)

        def dve_out(dve, c):
            dve.wait_ge(s["pv_done"], STEPS * c + STEPS)
            nc.vector.tensor_copy(oT[:, :, :], acc[:, :, :]).then_inc(s["acc_read"], 1)
            dve.wait_ge(s["o_turned"], c + 1)
            t = tail[:, :, :].rearrange("p g (c w) -> p (g c) w", w=32)
            nc.vector.reciprocal(rl[:, :], t[:, :, HD]).then_inc(s["att_step"], 1)
            dve.wait_ge(s["att_step"], c + 1)
            dve.wait_ge(s["att_free"], c + 1)
            nc.vector.tensor_tensor(att[:, :, :], t[:, :, 0:HD], rl[:, :].unsqueeze(2).broadcast_to([P, H, HD]),
                                    ALU.mult).then_inc(s["att_made"], 1)

        @block.vector
        def _(dve):
            for n in range(STEPS):
                dve_max(dve, 0, n)
                u, k, at = n // SPU, n % SPU // 4, n % 4
                if at == 1:
                    dve_r_sum(dve, 0, u, k)
                if at == 3:
                    dve_r_split(dve, 0, u, k)
            dve_m(dve, 0)

            def chunk(c, last):
                for m in range(STEPS):
                    if last:
                        break
                    for n in range(mx_units(m), mx_units(m + 1)):
                        dve_max(dve, c + 1, n)
                    u, k, at = m // SPU, m % SPU // 4, m % 4
                    if at == 1:
                        dve_r_sum(dve, c + 1, u, k)
                    if at == 3:
                        dve_r_split(dve, c + 1, u, k)
                    if m == MX_LAST:
                        dve_m(dve, c + 1)
                dve_out(dve, c)

            with dve.Fori(0, NT - 1) as c:
                chunk(c, False)
            chunk(NT - 1, True)

        def pe_scores(pe, c, m):
            jt, half = m // 2, m % 2
            if m < 2:
                pe.wait_ge(s[f"turn{half}"], 32 * c + 32)
            if m % SPU == 0:
                u = m // SPU
                pe.wait_ge(s[f"r_in{u % 2}"], 32 * (UNITS // 2 * c + u // 2 + 1))
            if m >= 2:
                pe.wait_ge(s["p_ready"], STEPS * c + m - 1)
            u, j0 = m // SPU, jt % 4 * P
            for p in range(4):
                pair = 4 * half + p
                pe.matmul(sc[:, half, p // 2, (p % 2) * 256:(p % 2) * 256 + 256], kst[:, pair, jt * P:jt * P + P],
                          qm[:, pair].rearrange("r a t -> r (a t)"), start=(p % 2 == 0), stop=False,
                          skip_group_check=True)
            for b in range(NB):
                for bank in range(2):
                    out = sc[:, half, bank, :].rearrange("p (h i b) -> p h i b", h=4, b=NB)[:, :, :, b]
                    ins = pe.matmul(out, rst[:, u % 2, b, j0:j0 + P], cm[:, half, b, 4 * bank:4 * bank + 4, :],
                                    start=False, stop=(b == NB - 1), skip_group_check=True)
            ins.then_inc(s["scores_ready"], 1)

        def pe_max(pe, x, n, first):
            head = n // 4
            if not first:
                pe.wait_ge(s["mx_used"], STEPS * x + n)
            for i in range(2):
                j0 = (n % 4 * 2 + i) * 512
                ins = pe.matmul(mx[:, i * 512:i * 512 + 512], qx[:, head // 2, head % 2, :],
                                kst[:, head // 2, j0:j0 + 512], start=True, stop=True)
            ins.then_inc(s["mx_ready"], 1)

        def pe_pv(pe, c, m):
            jt, half = m // 2, m % 2
            pe.wait_ge(s["p_ready"], STEPS * c + m + 1)
            for k in range(HH):
                h = HH * half + k
                ins = pe.matmul(acc[32 * (h % 4):32 * (h % 4) + 32, h // 4, :], vp[:, jt, VW * h:VW * h + 32],
                                pr[:, half, k * P:k * P + P], start=(m == 0 and k < 4), stop=(jt == NT - 1),
                                skip_group_check=True)
            ins.then_inc(s["pv_done"], 1)

        def pe_m(pe, x):
            pe.wait_ge(s["m_neg"], x + 1)
            pe.transpose(tail[0:H, 0, :], mrow[:, :], ident[:, :]).then_inc(s["m_turned"], 1)

        @block.tensor
        def _(pe):
            pe.wait_ge(s["ident_made"], 1)
            pe.wait_ge(s["qx_in"], 32)
            for n in range(STEPS):
                pe_max(pe, 0, n, n == 0)
            pe_m(pe, 0)

            def chunk(c, last):
                for m in range(STEPS):
                    pe_scores(pe, c, m)
                    if not last:
                        for n in range(mx_units(m), mx_units(m + 1)):
                            if n == 0:
                                pe.wait_ge(s["qx_in"], 32 * c + 64)
                            pe_max(pe, c + 1, n, False)
                    if m > 0:
                        pe_pv(pe, c, m - 1)
                    if m == MX_LAST + 1 and not last:
                        pe_m(pe, c + 1)
                pe_pv(pe, c, STEPS - 1)
                pe.wait_ge(s["acc_read"], c + 1)
                for g in range(4):
                    ins = pe.transpose(tail[:, g, :], oT[:, g, :], ident[:, :])
                ins.then_inc(s["o_turned"], 1)

            with pe.Fori(0, NT - 1) as c:
                chunk(c, False)
            chunk(NT - 1, True)


def experts(nc, hidden, woT, bo, wg, w1, b1, w2, b2, att_dram, out):
    with ExitStack() as ctx:
        def sb(name, shape, dt=F32):
            return ctx.enter_context(nc.sbuf_tensor("c_" + name, shape, dt))

        def sem(name):
            return ctx.enter_context(nc.semaphore("c_" + name))

        ps = ctx.enter_context(nc.psum_tensor("c_ps", [P, 8, 512], F32))
        x1 = sb("x1", [P, NT, D])
        a_room = sb("a", [P, NT * D])
        a = a_room[:, :].rearrange("p (t d) -> p t d", t=NT)
        hT = a_room[:, :].bitcast(F16).rearrange("p (o v f t) -> p o v f t", o=2, v=2, f=FT)
        aT = sb("aT", [P, KC, S])
        xT = [sb("xT_hi", [P, KC, S], F16), sb("xT_lo", [P, KC, S], F16)]
        wo = sb("wo", [P, KC, D])
        wgs = sb("wgs", [P, KC, E])
        bob = sb("bob", [P, D])
        b2s = sb("b2s", [E, D])
        b1s = sb("b1s", [P, E, FT])
        ident = sb("ident", [P, P])
        stats = sb("stats", [P, 2, 6])
        mv = sb("mv", [P, NT, 2])
        std = sb("std", [P, NT])
        rstd = sb("rstd", [P, NT])
        lg = sb("lg", [P, NT, E])
        top = sb("top", [P, NT, 8])
        topi = sb("topi", [P, NT, 8], U32)
        topf = sb("topf", [P, NT, TOP])
        iota_i = sb("iota_i", [P, E], mybir.dt.int32)
        iota_f = sb("iota_f", [P, E])
        pw = sb("pw", [P, TOP, NT])
        w = sb("w", [P, NT, E])
        w_b = sb("w_b", [P, NT, E])
        wT = sb("wT", [E, S])
        w32 = sb("w32", [P, 2048])
        w1p = [sb(f"w1p{n}", [P, 2, KC, F], F16) for n in range(2)]
        w2p = [sb(f"w2p{n}", [P, 2, FT, D], F16) for n in range(2)]
        h32 = sb("h32", [P, 2, TB])

        names = ("x_in", "w_in", "zeroed", "ident_made", "iota_made", "dve_step", "var_done", "std_done", "xn_done",
                 "pe_job", "act_job", "dve_job", "xT_done", "top_done", "exp_done", "w_done",
                 "w32_in", "w_split", "relu_done", "h_split", "up_done", "down_done", "added", "stored")
        s = {n: sem(n) for n in names}

        kinds = ([("AT", j) for j in range(16)] + [("O", j) for j in range(16)] + [("XT", j) for j in range(16)]
                 + [("G", 0)] + [("WT", j) for j in range(8)] + [("B2", j) for j in range(16)])
        jobs = ["act" if k in ("AT", "XT") and j % 2 and k == "AT" else "dve" for k, j in kinds]
        freed = {"act": s["act_job"], "dve": s["dve_job"]}
        start = {k: next(n for n, (kk, _) in enumerate(kinds) if kk == k) for k, _ in kinds}

        def act_before(n):
            return sum(1 for e in jobs[:n] if e == "act")

        def dve_before(n):
            return sum(1 for e in jobs[:n] if e == "dve")

        N_W = 6
        block = ctx.enter_context(nc.Block())

        @block.sync
        def _(sp):
            for q in range(4):
                t = slice(8 * q, 8 * q + 8)
                sp.dma_start(a[:, t, :], att_dram.rearrange("t p d -> p t d")[:, t, :]).then_inc(s["x_in"], 16)
                sp.dma_start(x1[:, t, :], hidden.rearrange("o (t p) d -> p (o t) d", p=P)[:, t, :]).then_inc(s["x_in"], 16)
            for dst, src in ((wo[:, :, :], woT.rearrange("(c p) n -> p c n", p=P)),
                             (wgs[:, :, :], wg.rearrange("(c p) n -> p c n", p=P)),
                             (bob[:, :], bo.partition_broadcast(P)),
                             (b2s[:, :], b2),
                             (b1s[:, 0:E // 2, :], b1.rearrange("e (p f) -> p e f", f=FT)[:, 0:E // 2]),
                             (b1s[:, E // 2:E, :], b1.rearrange("e (p f) -> p e f", f=FT)[:, E // 2:E])):
                sp.dma_start(dst, src).then_inc(s["w_in"], 16)
            for e in range(E):
                for n, (dst, src) in enumerate(((w32[:, :].rearrange("p (c f) -> p c f", c=KC),
                                                 w1[e].rearrange("(c p) f -> p c f", p=P)),
                                                (w32[:, :].rearrange("p (f d) -> p f d", f=FT),
                                                 w2[e].rearrange("(p f) d -> p f d", f=FT)))):
                    if e + n > 0:
                        sp.wait_ge(s["w_split"], 2 * (2 * e + n))
                    sp.dma_start(dst, src).then_inc(s["w32_in"], 16)
            for t in range(4):
                sp.wait_ge(s["added"], (E - 1) * NT + 8 * t + 8)
                sp.dma_start(out.rearrange("o (t p) d -> p (o t) d", p=P)[:, 8 * t:8 * t + 8, :],
                             x1[:, 8 * t:8 * t + 8, :]).then_inc(s["stored"], 16)
            sp.wait_ge(s["stored"], 64)

        @block.gpsimd
        def _(pool):
            identity_into(nc, pool, ident[:, :], s["zeroed"], s["ident_made"])
            nc.gpsimd.iota(iota_i[:, :], pattern=[[1, E]], base=0, channel_multiplier=0).then_inc(s["iota_made"], 1)

        def add_result(dve, d):
            e, t = d // NT, d % NT
            dve.wait_ge(s["down_done"], d + 1)
            if e > 0:
                dve.wait_ge(s["added"], d - NT + 1)
            nc.vector.scalar_tensor_tensor(out=x1[:, t], in0=ps[:, 4 + d % 4, 0:D], scalar=w[:, t, e:e + 1],
                                           in1=x1[:, t], op0=ALU.mult, op1=ALU.add).then_inc(s["added"], 1)

        def split_weights(dve, e):
            for n, dst in enumerate((w1p[e % 2], w2p[e % 2])):
                dve.wait_ge(s["w32_in"], 16 * (2 * e + n + 1))
                hi = dst[:, 0].rearrange("p a b -> p (a b)")
                lo = dst[:, 1].rearrange("p a b -> p (a b)")
                nc.vector.tensor_copy(hi, w32[:, :]).then_inc(s["w_split"], 1)
                dve.wait_ge(s["w_split"], 2 * (2 * e + n) + 1)
                nc.vector.tensor_tensor(lo, w32[:, :], hi, ALU.subtract).then_inc(s["w_split"], 1)

        @block.vector
        def _(dve):
            chain = [0]

            def link(ins):
                chain[0] += 1
                ins.then_inc(s["dve_step"], 1)
                dve.wait_ge(s["dve_step"], chain[0])

            split_weights(dve, 0)
            dve.wait_ge(s["x_in"], 128)
            dve.wait_ge(s["w_in"], 16 * N_W)
            for n, (kind, j) in enumerate(kinds):
                if jobs[n] != "dve":
                    continue
                if n == start["XT"]:
                    dve.wait_ge(s["pe_job"], start["O"])
                    for t in range(NT):
                        link(nc.vector.bn_stats(stats[:, t % 2], x1[:, t]))
                        link(nc.vector.bn_aggr(mv[:, t], stats[:, t % 2]))
                    nc.vector.tensor_scalar(rstd[:, :], mv[:, :, 1], EPS, None, ALU.add).then_inc(s["var_done"], 1)
                    dve.wait_ge(s["std_done"], 1)
                    link(nc.vector.reciprocal(rstd[:, :], std[:, :]))
                    for t in range(NT):
                        nc.vector.tensor_scalar(a[:, t], x1[:, t], mv[:, t, 0:1], rstd[:, t:t + 1], ALU.subtract,
                                                ALU.mult).then_inc(s["xn_done"], 1)
                if n == start["WT"]:
                    for t in range(NT):
                        nc.vector.max(out=top[:, t], in_=lg[:, t]).then_inc(s["top_done"], 1)
                        dve.wait_ge(s["top_done"], 2 * t + 1)
                        nc.vector.max_index(topi[:, t], top[:, t], lg[:, t]).then_inc(s["top_done"], 1)
                    dve.wait_ge(s["top_done"], 2 * NT)
                    link(nc.vector.tensor_copy(topf[:, :, :], topi[:, :, 0:TOP]))
                    dve.wait_ge(s["iota_made"], 1)
                    link(nc.vector.tensor_copy(iota_f[:, :], iota_i[:, :]))
                    link(nc.vector.tensor_tensor(pw[:, 1], top[:, :, 1], top[:, :, 0], ALU.subtract))
                    dve.wait_ge(s["exp_done"], 1)
                    link(nc.vector.tensor_scalar(pw[:, 1], pw[:, 0], 1.0, None, ALU.add))
                    link(nc.vector.reciprocal(rstd[:, :], pw[:, 1]))
                    link(nc.vector.tensor_tensor(pw[:, 1], pw[:, 0], rstd[:, :], ALU.mult))
                    iota_b = iota_f[:, :].unsqueeze(1).broadcast_to([P, NT, E])
                    for r, dst, weight in ((0, w, rstd[:, :]), (1, w_b, pw[:, 1])):
                        link(nc.vector.tensor_tensor(dst[:, :, :], iota_b, topf[:, :, r:r + 1].broadcast_to([P, NT, E]),
                                                     ALU.is_equal))
                        link(nc.vector.tensor_tensor(dst[:, :, :], dst[:, :, :],
                                                     weight.unsqueeze(2).broadcast_to([P, NT, E]), ALU.mult))
                    nc.vector.tensor_tensor(w[:, :, :], w[:, :, :], w_b[:, :, :], ALU.add).then_inc(s["w_done"], 1)
                    dve.wait_ge(s["w_done"], 1)
                dve.wait_ge(s["pe_job"], n + 1)
                bank = ps[:, n % 8, :]
                if kind == "AT":
                    nc.vector.tensor_copy(aT[:, j % 2, (j // 2) * 512:(j // 2) * 512 + 512], bank).then_inc(s["dve_job"], 1)
                if kind == "O":
                    link(nc.vector.tensor_tensor(x1[:, 2 * j:2 * j + 2, :], x1[:, 2 * j:2 * j + 2, :],
                                                 bank.rearrange("p (t d) -> p t d", t=2), ALU.add))
                    nc.vector.tensor_tensor(x1[:, 2 * j:2 * j + 2, :], x1[:, 2 * j:2 * j + 2, :],
                                            bob[:, :].unsqueeze(1).broadcast_to([P, 2, D]), ALU.add).then_inc(s["dve_job"], 1)
                    dve.wait_ge(s["dve_job"], dve_before(n) + 1)
                if kind == "XT":
                    cols = slice((j // 2) * 512, (j // 2) * 512 + 512)
                    link(nc.vector.tensor_copy(aT[:, j % 2, cols], bank))
                    nc.vector.tensor_copy(xT[0][:, j % 2, cols], aT[:, j % 2, cols]).then_inc(s["dve_job"], 1)
                    dve.wait_ge(s["dve_job"], dve_before(n) + 1)
                    nc.vector.tensor_tensor(xT[1][:, j % 2, cols], aT[:, j % 2, cols], xT[0][:, j % 2, cols],
                                            ALU.subtract).then_inc(s["xT_done"], 1)
                if kind == "G":
                    nc.vector.tensor_copy(lg[:, :, :], bank[:, 0:NT * E].rearrange("p (t e) -> p t e", e=E)).then_inc(s["dve_job"], 1)
                    dve.wait_ge(s["dve_job"], dve_before(n) + 1)
                if kind == "WT":
                    nc.vector.tensor_copy(wT[:, j * 512:j * 512 + 512], ps[0:E, n % 8, :]).then_inc(s["dve_job"], 1)
                if kind == "B2":
                    nc.vector.tensor_tensor(x1[:, 2 * j:2 * j + 2, :], x1[:, 2 * j:2 * j + 2, :],
                                            bank.rearrange("p (t d) -> p t d", t=2), ALU.add).then_inc(s["dve_job"], 1)
            dve.wait_ge(s["dve_job"], dve_before(len(kinds)))
            for i in range(E * NTB + 1):
                if i < E * NTB:
                    e, tb = i // NTB, i % NTB
                    for f in range(FT):
                        n = i * FT + f
                        dve.wait_ge(s["relu_done"], n + 1)
                        if f == 0 and i >= 2:
                            dve.wait_ge(s["down_done"], 4 * (i - 1))
                        nc.vector.tensor_copy(hT[:, i % 2, 0, f], h32[:, n % 2]).then_inc(s["h_split"], 1)
                        dve.wait_ge(s["h_split"], 2 * n + 1)
                        nc.vector.tensor_tensor(hT[:, i % 2, 1, f], h32[:, n % 2], hT[:, i % 2, 0, f],
                                                ALU.subtract).then_inc(s["h_split"], 1)
                        if i >= 1 and f % 2:
                            d = 4 * (i - 1) + f // 2
                            add_result(dve, d)
                    if tb == 4 and e + 1 < E:
                        if e > 0:
                            dve.wait_ge(s["down_done"], 4 * (e * NTB))
                        split_weights(dve, e + 1)
                else:
                    for d in range(4 * (i - 1), 4 * i):
                        add_result(dve, d)

        @block.scalar
        def _(act):
            for n, (kind, j) in enumerate(kinds):
                if n == start["XT"]:
                    act.wait_ge(s["var_done"], 1)
                    nc.scalar.activation(std[:, :], rstd[:, :], ACT.Sqrt).then_inc(s["std_done"], 1)
                if n == start["WT"]:
                    act.wait_ge(s["dve_step"], 2 * NT + 1 + 16 + 16 + 3)
                    nc.scalar.activation(pw[:, 0], pw[:, 1], ACT.Exp).then_inc(s["exp_done"], 1)
                if jobs[n] != "act":
                    continue
                act.wait_ge(s["pe_job"], n + 1)
                nc.scalar.copy(aT[:, j % 2, (j // 2) * 512:(j // 2) * 512 + 512], ps[:, n % 8, :]).then_inc(s["act_job"], 1)
            for i in range(E * NTB):
                e = i // NTB
                for f in range(FT):
                    n = i * FT + f
                    act.wait_ge(s["up_done"], n + 1)
                    if n >= 2:
                        act.wait_ge(s["h_split"], 2 * (n - 1))
                    nc.scalar.activation(h32[:, n % 2], ps[:, n % 4, :], ACT.Relu, bias=b1s[:, e, f:f + 1]).then_inc(
                        s["relu_done"], 1)

        @block.tensor
        def _(pe):
            pe.wait_ge(s["w_in"], 16 * N_W)
            pe.wait_ge(s["x_in"], 128)
            pe.wait_ge(s["ident_made"], 1)
            for n, (kind, j) in enumerate(kinds):
                own = bank_owner(jobs, n)
                if own:
                    pe.wait_ge(freed[own[0]], own[1])
                if n in (start["O"], start["G"], start["B2"]):
                    if act_before(n):
                        pe.wait_ge(s["act_job"], act_before(n))
                    pe.wait_ge(s["dve_job"], dve_before(n))
                if kind in ("AT", "XT"):
                    c, tb = j % 2, j // 2
                    if kind == "XT":
                        pe.wait_ge(s["xn_done"], 4 * tb + 4)
                    for t in range(4):
                        ins = pe.transpose(ps[:, n % 8, t * P:t * P + P], a[:, 4 * tb + t, c * P:c * P + P], ident[:, :])
                if kind == "O":
                    for t in range(2):
                        tile = 2 * j + t
                        for c in range(KC):
                            ins = pe.matmul(ps[:, n % 8, t * D:t * D + D], aT[:, c, tile * P:tile * P + P], wo[:, c, :],
                                            start=(c == 0), stop=(c == KC - 1))
                if kind == "G":
                    for t in range(NT):
                        for c in range(KC):
                            ins = pe.matmul(ps[:, n % 8, t * E:t * E + E], aT[:, c, t * P:t * P + P], wgs[:, c, :],
                                            start=(c == 0), stop=(c == KC - 1))
                if kind == "WT":
                    pe.wait_ge(s["w_done"], 1)
                    for t in range(4):
                        ins = pe.transpose(ps[0:E, n % 8, t * P:t * P + P], w[:, 4 * j + t, :], ident[:, :])
                if kind == "B2":
                    for t in range(2):
                        tile = 2 * j + t
                        ins = pe.matmul(ps[:, n % 8, t * D:t * D + D], wT[:, tile * P:tile * P + P], b2s[:, :],
                                        start=True, stop=True)
                ins.then_inc(s["pe_job"], 1)
            pe.wait_ge(s["dve_job"], dve_before(len(kinds)))
            pe.wait_ge(s["xT_done"], 16)
            parts = ((0, 0), (1, 0), (0, 1))
            for i in range(E * NTB + 1):
                if i < E * NTB:
                    e, tb = i // NTB, i % NTB
                    if tb == 0:
                        pe.wait_ge(s["w_split"], 4 * e + 4)
                    for f in range(FT):
                        n = i * FT + f
                        if n >= 4:
                            pe.wait_ge(s["relu_done"], n - 3)
                        first = True
                        for c in range(KC):
                            for wp, xp in parts:
                                ins = pe.matmul(ps[:, n % 4, :], w1p[e % 2][:, wp, c, f:F:FT],
                                                xT[xp][:, c, tb * TB:tb * TB + TB], start=first,
                                                stop=(c == KC - 1 and xp == 1))
                                first = False
                        ins.then_inc(s["up_done"], 1)
                if i > 0:
                    e = (i - 1) // NTB
                    for t in range(4):
                        d = 4 * (i - 1) + t
                        if t == 0:
                            pe.wait_ge(s["h_split"], 2 * FT * i)
                        if d >= 4:
                            pe.wait_ge(s["added"], d - 3)
                        for f in range(FT):
                            for hp, wp in parts:
                                ins = pe.matmul(ps[:, 4 + d % 4, 0:D], hT[:, (i - 1) % 2, hp, f, t * P:t * P + P],
                                                w2p[e % 2][:, wp, f, :], start=(f == 0 and hp == 0 and wp == 0),
                                                stop=(f == FT - 1 and wp == 1))
                        ins.then_inc(s["down_done"], 1)


def preln_attention_moe_kernel(nc, hidden, wqT, bq, wkT, bk, wvT, bv, woT, bo, relT, rel_b, lbT, gwT, gate_b,
                               wg, w1, b1, w2, b2, out):
    with ExitStack() as ctx:
        def dram(name, shape, dt=F32):
            return nc.dram_tensor(name, shape, dt, kind="Internal").ap()

        q_dram = dram("q_stacks", (NT, 2, 64, PAIRS, P), F16)
        c_dram = dram("c_values", (NT, 3, 2, P, H), F16)
        dj_dram = dram("key_logits", (3, S))
        const_dram = dram("query_consts", (NT, P, H + 4))
        r_dram = dram("relation_parts", (NT, UNITS, 2, 2, P, JU), F16)
        m_dram = dram("row_maxima", (H, 3, P), F16)
        att_dram = dram("attention_out", (NT, P, D))
        with ExitStack() as attention:
            kst = attention.enter_context(nc.sbuf_tensor("kst", [P, PAIRS, S], F16))
            vp = attention.enter_context(nc.sbuf_tensor("vp", [P, NT, VPAD], F32))
            project_inputs(nc, kst, vp, hidden, wqT, bq, wkT, bk, wvT, bv, relT, rel_b, lbT, gwT, gate_b,
                           q_dram, c_dram, const_dram, dj_dram)
            attend(nc, kst, vp, dj_dram, q_dram, c_dram, const_dram, r_dram, m_dram, att_dram)
        experts(nc, hidden, woT, bo, wg, w1, b1, w2, b2, att_dram, out)


_INS = [("L0_attn_hidden_states", False), ("L0_attn_Wq", True), ("L0_attn_bq", False), ("L0_attn_Wk", True),
        ("L0_attn_bk", False), ("L0_attn_Wv", True), ("L0_attn_bv", False), ("L0_attn_Wo", True),
        ("L0_attn_bo", False), ("L0_attn_rel_W", True), ("L0_attn_rel_b", False), ("L0_attn_logical_bias", True),
        ("L0_attn_gate_W", True), ("L0_attn_gate_b", False), ("L0_ffn_Wg", False), ("L0_ffn_W1", False),
        ("L0_ffn_b1", False), ("L0_ffn_W2", False), ("L0_ffn_b2", False)]


def kernel(**inputs):
    import numpy as _np
    import concourse.bacc as _bacc
    from concourse import mybir as _mybir
    from concourse.bass_utils import run_bass_kernel_spmd as _run

    nc = _bacc.Bacc("TRN2", target_bir_lowering=False, num_devices=1)
    arrays, args = {}, []
    for name, turned in _INS:
        a = _np.asarray(inputs[name])
        a = _np.ascontiguousarray(a.T if turned else a)
        arrays[f"in_{name}_dram"] = a
        args.append(nc.dram_tensor(f"in_{name}_dram", a.shape, _mybir.dt.from_np(a.dtype), kind="ExternalInput").ap())
    args.append(nc.dram_tensor("out_0_dram", (1, S, D), _mybir.dt.float32, kind="ExternalOutput").ap())
    preln_attention_moe_kernel(nc, *args)
    r = _run(nc, [arrays], core_ids=[0])
    return r.results[0]["out_0_dram"]
```

```python
from contextlib import ExitStack

import concourse.bass as bass
from concourse import mybir

F32 = mybir.dt.float32
F16 = mybir.dt.float16
U32 = mybir.dt.uint32
ALU = mybir.AluOpType
ACT = mybir.ActivationFunctionType
AX = mybir.AxisListType

P = 128
S, D, H, HD = 4096, 256, 16, 16
NT = S // P
KC = D // P
PAIRS = H // 2
HH = H // 2
NB, BI = 8, 16
JU = 512
UNITS = S // JU
SPU = 2 * JU // P
STEPS = 2 * NT
VW = HD + 1
VPAD = H * VW + 15
E, F, TOP = 8, 1024, 2
FT = F // P
TB = 512
NTB = S // TB
EPS = 1e-5
EXP_MAX = 43.0
ROWS = 6 * BI
MX_FIRST, MX_LAST = 2, 57
MXU = S // 512
MXN = H * MXU


def mx_units(m):
    m = min(max(m - MX_FIRST, 0), MX_LAST - MX_FIRST)
    return m * MXN // (MX_LAST - MX_FIRST)


def in_chunks(eng, chunk):
    with eng.Fori(0, (NT - 2) // 2) as pair:
        chunk(pair * 2, 0, pair + 1, False)
        chunk(pair * 2 + 1, 1, pair + 1, False)
    chunk(NT - 2, 0, NT // 2, False)
    chunk(NT - 1, 1, NT // 2, True)


def bank_owner(jobs, n, ring=8):
    if n < ring:
        return None
    eng = jobs[n - ring]
    return eng, sum(1 for e in jobs[:n - ring + 1] if e == eng)


def identity_into(nc, pool, t, zeroed, made):
    nc.gpsimd.memset(t, 0.0).then_inc(zeroed, 1)
    pool.wait_ge(zeroed, 1)
    nc.gpsimd.affine_select(out=t, in_=t, compare_op=ALU.not_equal, fill=1.0, base=0,
                            pattern=[[-1, P]], channel_multiplier=1).then_inc(made, 1)


def project_inputs(nc, kst, vp, hidden, wqT, bq, wkT, bk, wvT, bv, relT, rel_b, lbT, gwT, gate_b,
                   q_dram, c_dram, const_dram, dj_dram):
    with ExitStack() as ctx:
        def sb(name, shape, dt=F32):
            return ctx.enter_context(nc.sbuf_tensor("a_" + name, shape, dt))

        def sem(name):
            return ctx.enter_context(nc.semaphore("a_" + name))

        ps = ctx.enter_context(nc.psum_tensor("a_ps", [P, 8, 512], F32))
        x_room = sb("x_room", [P, NT * D])
        x = x_room[:, :].rearrange("p (t d) -> p t d", t=NT)
        part_lo = x_room[:, :].bitcast(F16).rearrange("p (m s) -> p m s", m=4)
        part_hi = sb("part_hi", [P, 2, S], F16)
        xnT = sb("xnT", [P, KC, S])
        stats = sb("stats", [P, 2, 6])
        mv = sb("mv", [P, NT, 2])
        std = sb("std", [P, NT])
        rstd = sb("rstd", [P, NT])
        ident = sb("ident", [P, P])
        wq = sb("wq", [P, 2, KC, D])
        wv = sb("wv", [P, KC, D])
        rel = sb("rel", [P, 2, KC, 3])
        gw = sb("gw", [P, KC, H + 4])
        wdj = sb("wdj", [P, KC, 3])
        bqk = sb("bqk", [P, 4])
        bvb = sb("bvb", [P, D])
        gb = sb("gb", [P, H + 4])
        rb = sb("rb", [P, 3])
        lb = sb("lb", [P, 3, H])
        lbd = sb("lbd", [P, 2, H])
        mb = sb("mb", [P, H])
        qk32 = sb("qk32", [P, 2, 512])
        g = sb("g", [P, NT, H + 4])
        gate = sb("gate", [P, NT, H])
        consts = sb("consts", [P, NT, H + 4])
        chi = sb("chi", [P, 2, NT, H], F16)
        clo = sb("clo", [P, 2, NT, H], F16)
        zero16 = sb("zero16", [BI, PAIRS * P], F16)

        x_in, w_in, zeroed, ident_made, zero_made = (sem(n) for n in (
            "x_in", "w_in", "zeroed", "ident_made", "zero_made"))
        dve_step, act_step = sem("dve_step"), sem("act_step")
        var_done, std_done, xn_done, wts_done = (sem(n) for n in ("var_done", "std_done", "xn_done", "wts_done"))
        pe_job, act_job, dve_job = sem("pe_job"), sem("act_job"), sem("dve_job")
        qk_split = sem("qk_split")
        dj_out = [sem("dj_out0"), sem("dj_out1")]
        ez_done, consts_done, c_done = sem("ez_done"), sem("consts_done"), sem("c_done")
        stored, k_filled, g_ready = sem("stored"), sem("k_filled"), sem("g_ready")

        kinds = ([("T", j) for j in range(16)] + [("G", j) for j in range(2)]
                 + [("QK", j) for j in range(32)] + [("DJ", j) for j in range(8)]
                 + [("V", j) for j in range(16)])
        jobs = ["act" if k == "T" and j % 2 or k in ("QK", "DJ") else "dve" for k, j in kinds]
        freed = {"act": act_job, "dve": dve_job}
        first_qk = next(n for n, (k, _) in enumerate(kinds) if k == "QK")
        last_t = 16
        N_W = 14

        block = ctx.enter_context(nc.Block())

        def act_before(n):
            return sum(1 for e in jobs[:n] if e == "act")

        def dve_before(n):
            return sum(1 for e in jobs[:n] if e == "dve")

        @block.sync
        def _(sp):
            for q in range(4):
                sp.dma_start(x[:, 8 * q:8 * q + 8, :],
                             hidden.rearrange("o (t p) d -> p (o t) d", p=P)[:, 8 * q:8 * q + 8, :]).then_inc(x_in, 16)
            for dst, src in ((wq[:, 0], wqT.rearrange("(c p) n -> p c n", p=P)),
                             (wq[:, 1], wkT.rearrange("(c p) n -> p c n", p=P)),
                             (wv[:, :, :], wvT.rearrange("(c p) n -> p c n", p=P)),
                             (rel[:, 0], relT.rearrange("(two c p) k -> two p c k", p=P, two=2)[0]),
                             (rel[:, 1], relT.rearrange("(two c p) k -> two p c k", p=P, two=2)[1]),
                             (gw[:, :, 0:H], gwT.rearrange("(c p) n -> p c n", p=P)),
                             (bqk[:, 0:2], bq.rearrange("(c p) -> p c", p=P)),
                             (bqk[:, 2:4], bk.rearrange("(c p) -> p c", p=P)),
                             (bvb[:, :], bv.partition_broadcast(P)),
                             (gb[:, 0:H], gate_b.partition_broadcast(P)),
                             (rb[:, :], rel_b.partition_broadcast(P)),
                             (lb[:, 0, :], lbT[0].partition_broadcast(P)),
                             (lb[:, 1, :], lbT[1].partition_broadcast(P)),
                             (lb[:, 2, :], lbT[2].partition_broadcast(P))):
                sp.dma_start(dst, src, allow_slow_non_contiguous=True).then_inc(w_in, 16)
            sp.wait_ge(zero_made, 1)
            for xc in range(NT):
                for ab in range(2):
                    sp.dma_start(q_dram[xc, ab, 32:48], zero16[:, :].rearrange("r (q t) -> r q t", q=PAIRS)).then_inc(stored, 16)
            for m in range(4):
                sp.wait_ge(qk_split, 16 * (m + 1))
                for pp in range(4):
                    for ab in range(2):
                        r = 32 * pp + 16 * ab
                        pair = 4 * (m % 2) + pp
                        for row, part in ((0, "hi"), (16, "hi" if m < 2 else "lo"), (48, "lo" if m < 2 else "hi")):
                            src = part_hi[r:r + 16, m % 2, :] if part == "hi" else part_lo[r:r + 16, m, :]
                            if m < 2:
                                sp.dma_start(q_dram[:, ab, row:row + 16, pair, :].rearrange("x r t -> r x t"),
                                             src.rearrange("r (x t) -> r x t", t=P)).then_inc(stored, 16)
                            else:
                                sp.dma_start(kst[64 * ab + row:64 * ab + row + 16, pair, :], src).then_inc(k_filled, 16)
            first_dj = next(n for n, (k, _) in enumerate(kinds) if k == "DJ")
            for j in range(8):
                sp.wait_ge(act_job, act_before(first_dj + j) + 1)
                sp.dma_start(dj_dram[:, j * 512:j * 512 + 512], qk32[0:3, j % 2, :]).then_inc(dj_out[j % 2], 16)
            for q in dj_out:
                sp.wait_ge(q, 64)
            sp.wait_ge(consts_done, 2)
            sp.dma_start(const_dram.rearrange("x p n -> p x n"), consts[:, :, :]).then_inc(stored, 16)
            sp.wait_ge(c_done, 2)
            for part, t in ((0, chi), (1, chi), (2, clo)):
                for k in range(2):
                    sp.dma_start(c_dram[:, part, k].rearrange("x p h -> p x h"), t[:, k]).then_inc(stored, 16)
            sp.wait_ge(k_filled, 16 * 48)
            sp.wait_ge(stored, 16 * (64 + 48 + 1 + 6))

        @block.gpsimd
        def _(pool):
            nc.gpsimd.memset(zero16[:, :], 0.0).then_inc(zero_made, 1)
            identity_into(nc, pool, ident[:, :], zeroed, ident_made)

        @block.vector
        def _(dve):
            chain = [0]

            def link(ins):
                chain[0] += 1
                ins.then_inc(dve_step, 1)
                dve.wait_ge(dve_step, chain[0])

            nc.vector.memset(vp[:, :, :], 1.0).then_inc(wts_done, 1)
            for r in (32, 96):
                nc.vector.memset(kst[r:r + 16, :, :], 1.0).then_inc(wts_done, 1)
            dve.wait_ge(w_in, 16 * N_W)
            for n, (a, b) in enumerate(((1, 0), (2, 0), (0, 1), (2, 1))):
                nc.vector.tensor_tensor(gw[:, :, H + n:H + n + 1], rel[:, 0, :, a:a + 1], rel[:, 0, :, b:b + 1],
                                        ALU.subtract).then_inc(wts_done, 1)
                nc.vector.tensor_tensor(gb[:, H + n:H + n + 1], rb[:, a:a + 1], rb[:, b:b + 1],
                                        ALU.subtract).then_inc(wts_done, 1)
            for n, (a, b) in enumerate(((1, 0), (2, 0), (2, 1))):
                link(nc.vector.tensor_tensor(wdj[:, :, n:n + 1], rel[:, 1, :, a:a + 1], rel[:, 1, :, b:b + 1],
                                             ALU.subtract))
            for k in range(2):
                nc.vector.tensor_tensor(lbd[:, k], lb[:, k], lb[:, 2], ALU.subtract).then_inc(wts_done, 1)
            dve.wait_ge(wts_done, 13)
            link(nc.vector.tensor_tensor(mb[:, :], lbd[:, 0], lbd[:, 1], ALU.max))
            link(nc.vector.tensor_scalar(mb[:, :], mb[:, :], 0.0, None, ALU.max))
            dve.wait_ge(x_in, 64)
            for t in range(NT):
                link(nc.vector.bn_stats(stats[:, t % 2], x[:, t]))
                link(nc.vector.bn_aggr(mv[:, t], stats[:, t % 2]))
            nc.vector.tensor_scalar(rstd[:, :], mv[:, :, 1], EPS, None, ALU.add).then_inc(var_done, 1)
            dve.wait_ge(std_done, 1)
            link(nc.vector.reciprocal(rstd[:, :], std[:, :]))
            for t in range(NT):
                nc.vector.tensor_scalar(x[:, t], x[:, t], mv[:, t, 0:1], rstd[:, t:t + 1], ALU.subtract,
                                        ALU.mult).then_inc(xn_done, 1)
            for n, (kind, j) in enumerate(kinds):
                if kind == "QK":
                    m, tb = j // 8, j % 8
                    dve.wait_ge(act_job, act_before(n) + 1)
                    if n == first_qk:
                        dve.wait_ge(pe_job, last_t)
                    if m == 2 and tb == 0:
                        dve.wait_ge(stored, 16 * (2 * NT + 48))
                    cols = slice(tb * 512, tb * 512 + 512)
                    nc.vector.tensor_copy(part_hi[:, m % 2, cols], qk32[:, j % 2, :]).then_inc(qk_split, 1)
                    dve.wait_ge(qk_split, 2 * j + 1)
                    nc.vector.tensor_tensor(part_lo[:, m, cols], qk32[:, j % 2, :], part_hi[:, m % 2, cols],
                                            ALU.subtract).then_inc(qk_split, 1)
                if jobs[n] != "dve":
                    continue
                dve.wait_ge(pe_job, n + 1)
                if kind == "T":
                    nc.vector.tensor_copy(xnT[:, j % 2, (j // 2) * 512:(j // 2) * 512 + 512], ps[:, n % 8, :]).then_inc(dve_job, 1)
                if kind == "V":
                    dst = vp[:, 2 * j:2 * j + 2, 0:H * VW].rearrange("p t (h w) -> p t h w", w=VW)
                    for t in range(2):
                        ins = nc.vector.tensor_tensor(dst[:, t, :, 0:HD],
                                                      ps[:, n % 8, t * D:t * D + D].rearrange("p (h w) -> p h w", w=HD),
                                                      bvb[:, :].rearrange("p (h w) -> p h w", w=HD), ALU.add)
                    ins.then_inc(dve_job, 1)
                if kind == "G":
                    w = NT // 2 * (H + 4)
                    ins = nc.vector.tensor_tensor(g[:, j * 16:j * 16 + 16, :],
                                                  ps[:, n % 8, 0:w].rearrange("p (t n) -> p t n", n=H + 4),
                                                  gb[:, :].unsqueeze(1).broadcast_to([P, 16, H + 4]), ALU.add)
                    ins.then_inc(dve_job, 1)
            dve.wait_ge(ez_done, 1)
            link(nc.vector.tensor_scalar(gate[:, :, :], gate[:, :, :], 1.0, None, ALU.add))
            link(nc.vector.reciprocal(gate[:, :, :], gate[:, :, :]))
            nc.vector.tensor_copy(consts[:, :, 0:4], g[:, :, H:H + 4]).then_inc(consts_done, 1)
            nc.vector.tensor_tensor(consts[:, :, 4:4 + H], gate[:, :, :],
                                    mb[:, :].unsqueeze(1).broadcast_to([P, NT, H]), ALU.mult).then_inc(consts_done, 1)
            for k in range(2):
                link(nc.vector.tensor_tensor(g[:, :, 0:H], gate[:, :, :],
                                             lbd[:, k].unsqueeze(1).broadcast_to([P, NT, H]), ALU.mult))
                link(nc.vector.tensor_copy(chi[:, k], g[:, :, 0:H]))
                nc.vector.tensor_tensor(clo[:, k], g[:, :, 0:H], chi[:, k], ALU.subtract).then_inc(c_done, 1)
                dve.wait_ge(c_done, k + 1)

        @block.scalar
        def _(act):
            act.wait_ge(w_in, 16 * N_W)
            nc.scalar.mul(bqk[:, 0:2], bqk[:, 0:2], HD ** -0.5).then_inc(act_step, 1)
            act.wait_ge(act_step, 1)
            act.wait_ge(var_done, 1)
            nc.scalar.activation(std[:, :], rstd[:, :], ACT.Sqrt).then_inc(std_done, 1)
            for n, (kind, j) in enumerate(kinds):
                if jobs[n] != "act":
                    continue
                act.wait_ge(pe_job, n + 1)
                if kind == "T":
                    nc.scalar.copy(xnT[:, j % 2, (j // 2) * 512:(j // 2) * 512 + 512], ps[:, n % 8, :]).then_inc(act_job, 1)
                if kind == "DJ":
                    if j == 0:
                        act.wait_ge(qk_split, 64)
                    if j >= 2:
                        act.wait_ge(dj_out[j % 2], 16 * (j // 2))
                    nc.scalar.copy(qk32[0:3, j % 2, :], ps[0:3, n % 8, :]).then_inc(act_job, 1)
                if kind == "QK":
                    if j >= 2:
                        act.wait_ge(qk_split, 2 * (j - 1))
                    m = j // 8
                    nc.scalar.activation(qk32[:, j % 2, :], ps[:, n % 8, :], ACT.Identity, bias=bqk[:, m:m + 1],
                                         scale=HD ** -0.5 if m < 2 else 1.0).then_inc(act_job, 1)
            act.wait_ge(dve_job, dve_before(first_qk))
            nc.scalar.activation(gate[:, :, :], g[:, :, 0:H], ACT.Exp, scale=-1.0).then_inc(ez_done, 1)

        @block.tensor
        def _(pe):
            pe.wait_ge(w_in, 16 * N_W)
            pe.wait_ge(ident_made, 1)
            pe.wait_ge(wts_done, 13)
            for n, (kind, j) in enumerate(kinds):
                own = bank_owner(jobs, n)
                if own:
                    pe.wait_ge(freed[own[0]], own[1])
                if kind == "T":
                    c, tb = j % 2, j // 2
                    pe.wait_ge(xn_done, 4 * tb + 4)
                    for t in range(4):
                        ins = pe.transpose(ps[:, n % 8, t * P:t * P + P], x[:, 4 * tb + t, c * P:c * P + P], ident[:, :])
                if n == last_t:
                    pe.wait_ge(act_job, act_before(n))
                    pe.wait_ge(dve_job, dve_before(n))
                if kind == "G":
                    for t in range(16):
                        tile = 16 * j + t
                        for c in range(KC):
                            ins = pe.matmul(ps[:, n % 8, t * (H + 4):(t + 1) * (H + 4)], xnT[:, c, tile * P:tile * P + P],
                                            gw[:, c, :], start=(c == 0), stop=(c == KC - 1))
                if kind == "QK":
                    m, tb = j // 8, j % 8
                    for c in range(KC):
                        ins = pe.matmul(ps[:, n % 8, :], wq[:, m // 2, c, (m % 2) * P:(m % 2) * P + P],
                                        xnT[:, c, tb * 512:tb * 512 + 512], start=(c == 0), stop=(c == KC - 1))
                if kind == "DJ":
                    for c in range(KC):
                        ins = pe.matmul(ps[0:3, n % 8, :], wdj[:, c, :], xnT[:, c, j * 512:j * 512 + 512],
                                        start=(c == 0), stop=(c == KC - 1))
                if kind == "V":
                    for t in range(2):
                        tile = 2 * j + t
                        for c in range(KC):
                            ins = pe.matmul(ps[:, n % 8, t * D:t * D + D], xnT[:, c, tile * P:tile * P + P],
                                            wv[:, c, :], start=(c == 0), stop=(c == KC - 1))
                ins.then_inc(pe_job, 1)


def attend(nc, kst, vp, dj_dram, q_dram, c_dram, const_dram, r_dram, m_dram, att_dram):
    with ExitStack() as ctx:
        def sb(name, shape, dt=F32):
            return ctx.enter_context(nc.sbuf_tensor("b_" + name, shape, dt))

        def sem(name):
            return ctx.enter_context(nc.semaphore("b_" + name))

        sc = ctx.enter_context(nc.psum_tensor("b_sc", [P, 2, 2, 512], F32))
        mx = ctx.enter_context(nc.psum_tensor("b_mx", [P, 2, 512], F32))
        acc = ctx.enter_context(nc.psum_tensor("b_acc", [P, 4, P], F32))
        tail = ctx.enter_context(nc.psum_tensor("b_tail", [P, 4, P], F32))

        dj = sb("dj", [P, 3, S])
        rst = sb("rst", [ROWS, 2, NB, JU], F16)
        pr = sb("pr", [P, 2, HH * P])
        qm = sb("qm", [P, 2, PAIRS, 2, P], F16)
        cm = sb("cm", [ROWS, 2, 2, NB, HH, BI], F16)
        cval = sb("cval", [ROWS, 2, NB, H], F16)
        eye = sb("eye", [ROWS, BI], F16)
        ident = sb("ident", [P, P])
        const = sb("const", [P, 2, H + 4])
        ex = sb("ex", [P, 2, 2, JU])
        rhi = sb("rhi", [P, 2, JU], F16)
        rlo = sb("rlo", [P, 2, JU], F16)
        mxp = sb("mxp", [P, H, MXU])
        mrow = sb("mrow", [P, H])
        mT = sb("mT", [H, P])
        mparts = sb("mparts", [H, 3, P], F16)
        oT = sb("oT", [P, 4, P])
        rl = sb("rl", [P, H])
        att = sb("att", [P, H, HD])

        names = ("zeroed", "ident_made", "eye_made", "dj_in", "q_zeroed", "att_zeroed",
                 "q_in", "m_in", "const_in0", "const_in1", "cval_in0", "cval_in1", "c_made",
                 "scores_ready", "p_ready", "pv_done", "mx_ready", "mx_used", "m_step", "m_neg", "m_turned", "m_parts",
                 "m_out", "d_ready", "e_ready", "sum_ready", "ln_ready", "r_ready", "hi_ready", "lo_ready",
                 "r_out00", "r_out01", "r_out10", "r_out11", "r_in0", "r_in1",
                 "acc_read", "o_turned", "att_step", "att_made", "att_out", "att_free", "sp_waited")
        s = {n: sem(n) for n in names}

        block = ctx.enter_context(nc.Block())

        def r_stored(eng, x, u, k):
            if u >= 0:
                eng.wait_ge(s[f"r_out{k}{u % 2}"], 32 * (UNITS // 2 * x + u // 2 + 1))
            elif not (isinstance(x, int) and x == 0):
                eng.wait_ge(s[f"r_out{k}1"], 32 * (UNITS // 2 * x))

        def waited(sp):
            sp.sem_inc(s["sp_waited"], 1)

        def sp_q(sp, x, par):
            for ab in range(2):
                sp.dma_start(qm[64 * ab:64 * ab + 64, par, :, ab, :],
                             q_dram[bass.ds(x, 1), ab].rearrange("o r q t -> r (o q) t")).then_inc(s["q_in"], 16)

        def sp_consts(sp, x, par):
            sp.dma_start(cval[:, par].rearrange("r b h -> r (b h)"),
                         c_dram[bass.ds(x, 1)].rearrange("o a k (i b) h -> (o a k i) (b h)", b=NB)).then_inc(s[f"cval_in{par}"], 16)
            sp.dma_start(const[:, par], const_dram[bass.ds(x, 1)].rearrange("o p n -> (o p) n")).then_inc(s[f"const_in{par}"], 16)

        def sp_write_r(sp, x, u):
            for k in range(2):
                sp.wait_ge(s["lo_ready"], 16 * x + 2 * u + k + 1)
                waited(sp)
                for part, t in ((0, rhi), (1, rlo)):
                    sp.dma_start(r_dram[bass.ds(x, 1), u, part, k].rearrange("o i j -> (o i) j"), t[:, k]).then_inc(
                        s[f"r_out{k}{u % 2}"], 16)

        def sp_read_r(sp, x, u, written):
            for k in range(2):
                sp.wait_ge(s[f"r_out{k}{u % 2}"], 32 * written)
            waited(sp)
            src = r_dram[bass.ds(x, 1), u].rearrange("o a k (i b) j -> (o a k i) (b j)", b=NB)
            dst = rst[:, u % 2].rearrange("r b j -> r (b j)")
            sp.dma_start(dst[0:64], src).then_inc(s[f"r_in{u % 2}"], 16)
            sp.dma_start(dst[64:96], src[0:32]).then_inc(s[f"r_in{u % 2}"], 16)

        def sp_m(sp, x, par):
            sp.wait_ge(s["m_parts"], 3 * x + 3)
            waited(sp)
            if not (isinstance(x, int) and x == 0):
                sp.wait_ge(s["m_in"], 32 * x)
            sp.dma_start(m_dram[:, :, :], mparts[:, :, :]).then_inc(s["m_out"], 16)
            sp.wait_ge(s["m_out"], 16 * x + 16)
            for ab in range(2):
                sp.dma_start(qm[64 * ab + 32:64 * ab + 35, par, :, ab, :],
                             m_dram.rearrange("(q ab) s i -> ab s q i", ab=2)[ab]).then_inc(s["m_in"], 16)

        @block.sync
        def _(sp):
            for d in range(3):
                sp.dma_start(dj[:, d, :], dj_dram[d].partition_broadcast(P)).then_inc(s["dj_in"], 16)
            sp.wait_ge(s["q_zeroed"], 1)
            for x in range(2):
                sp_consts(sp, x, x)
            sp_q(sp, 0, 0)
            sp.wait_ge(s["att_zeroed"], 1)
            sp.dma_start(att_dram[0], att[:, :, :].rearrange("p h w -> p (h w)")).then_inc(s["att_out"], 16)
            for u in range(UNITS):
                sp_write_r(sp, 0, u)
            sp_read_r(sp, 0, 0, UNITS // 2)
            sp_m(sp, 0, 0)
            sp_q(sp, 1, 1)

            def chunk(c, par, nth, last):
                more = not last and not (isinstance(c, int) and c + 2 >= NT)
                if more:
                    sp_consts(sp, c + 2, par)
                for u in range(UNITS):
                    if u + 1 < UNITS:
                        if u > 0:
                            sp.wait_ge(s["scores_ready"], STEPS * c + SPU * u)
                        sp_read_r(sp, c, u + 1, UNITS // 2 * (c + 1) + (0 if last else len(range((u + 1) % 2, u, 2))))
                    else:
                        sp.wait_ge(s["att_out"], 16 * c + 16)
                        sp.sem_inc(s["att_free"], 1)
                        if not last:
                            sp.wait_ge(s["scores_ready"], STEPS * c + SPU * u)
                            sp_read_r(sp, c + 1, 0, UNITS // 2 * (c + 2))
                    if not last:
                        if u + 1 == UNITS:
                            sp_m(sp, c + 1, 1 - par)
                        sp_write_r(sp, c + 1, u)
                if more:
                    sp.wait_ge(s["scores_ready"], STEPS * c + STEPS)
                    waited(sp)
                    sp_q(sp, c + 2, par)
                sp.wait_ge(s["att_made"], c + 1)
                waited(sp)
                sp.dma_start(att_dram[bass.ds(c, 1)].rearrange("o p n -> (o p) n"),
                             att[:, :, :].rearrange("p h w -> p (h w)")).then_inc(s["att_out"], 16)

            in_chunks(sp, chunk)
            sp.wait_ge(s["att_out"], 16 * NT + 16)

        def pool_c(pool, x, par, nth):
            pool.wait_ge(s[f"cval_in{par}"], 16 * nth)
            if not (isinstance(x, int) and x < 2):
                pool.wait_ge(s["scores_ready"], STEPS * (x - 1))
            for half in range(2):
                nc.gpsimd.tensor_tensor(cm[:, par, half],
                                        cval[:, par, :, HH * half:HH * half + HH].unsqueeze(3).broadcast_to([ROWS, NB, HH, BI]),
                                        eye[:, :].unsqueeze(1).unsqueeze(1).broadcast_to([ROWS, NB, HH, BI]),
                                        ALU.mult).then_inc(s["c_made"], 1)

        def pool_r(pool, x):
            for u in range(UNITS):
                for k in range(2):
                    g = 16 * x + 2 * u + k
                    pool.wait_ge(s["e_ready"], 2 * g + 2)
                    nc.gpsimd.tensor_tensor(ex[:, k, 0], ex[:, k, 0], ex[:, k, 1], ALU.add).then_inc(s["sum_ready"], 1)
                    pool.wait_ge(s["hi_ready"], g + 1)
                    nc.gpsimd.tensor_tensor(rlo[:, k], ex[:, k, 0], rhi[:, k], ALU.subtract).then_inc(s["lo_ready"], 1)

        @block.gpsimd
        def _(pool):
            identity_into(nc, pool, ident[:, :], s["zeroed"], s["ident_made"])
            nc.gpsimd.memset(qm[:, :, :, :, :], 0.0).then_inc(s["q_zeroed"], 1)
            nc.gpsimd.memset(att[:, :, :], 0.0).then_inc(s["att_zeroed"], 1)
            nc.gpsimd.memset(eye[:, :], 0.0).then_inc(s["eye_made"], 1)
            for n in range(ROWS // BI):
                pool.wait_ge(s["eye_made"], n + 1)
                nc.gpsimd.affine_select(out=eye[:, :], in_=eye[:, :], compare_op=ALU.not_equal, fill=1.0,
                                        base=-BI * n, pattern=[[-1, BI]], channel_multiplier=1).then_inc(s["eye_made"], 1)
            pool.wait_ge(s["eye_made"], ROWS // BI + 1)
            pool_c(pool, 0, 0, 1)
            pool_r(pool, 0)
            pool_c(pool, 1, 1, 1)

            def chunk(c, par, nth, last):
                if not last:
                    pool_r(pool, c + 1)
                if not last and not (isinstance(c, int) and c + 2 >= NT):
                    pool_c(pool, c + 2, par, nth + 1)

            in_chunks(pool, chunk)

        def act_r_exp(act, x, u, k):
            act.wait_ge(s["d_ready"], 2 * (16 * x + 2 * u + k) + 2)
            for n, sign in enumerate(((1.0, 1.0), (-1.0, 1.0))[k]):
                nc.scalar.activation(ex[:, k, n], ex[:, k, n], ACT.Exp, scale=sign).then_inc(s["e_ready"], 1)

        def act_r_inv(act, x, u, k):
            g = 16 * x + 2 * u + k
            act.wait_ge(s["sum_ready"], g + 1)
            nc.scalar.activation(ex[:, k, 0], ex[:, k, 0], ACT.Ln, bias=1.0).then_inc(s["ln_ready"], 1)
            act.wait_ge(s["ln_ready"], g + 1)
            nc.scalar.activation(ex[:, k, 0], ex[:, k, 0], ACT.Exp, scale=-1.0).then_inc(s["r_ready"], 1)

        @block.scalar
        def _(act):
            nc.scalar.preload_act_table_set("natural_log_exp_and_others")
            for u in range(UNITS):
                for k in range(2):
                    act_r_exp(act, 0, u, k)
                    act_r_inv(act, 0, u, k)

            def chunk(c, par, nth, last):
                for m in range(STEPS):
                    act.wait_ge(s["scores_ready"], STEPS * c + m + 1)
                    if m >= 2:
                        act.wait_ge(s["pv_done"], STEPS * c + m - 1)
                    nc.scalar.activation(pr[:, m % 2, :], sc[:, m % 2].rearrange("p a b -> p (a b)"),
                                         ACT.Exp).then_inc(s["p_ready"], 1)
                    if not last:
                        u, k, at = m // SPU, m % SPU // 4, m % 4
                        if at == 0:
                            act_r_exp(act, c + 1, u, k)
                        if at == 2:
                            act_r_inv(act, c + 1, u, k)

            in_chunks(act, chunk)

        def dve_max(dve, x, n):
            dve.wait_ge(s["mx_ready"], MXN * x + n + 1)
            nc.vector.tensor_reduce(mxp[:, n // MXU, n % MXU:n % MXU + 1], mx[:, n % 2, :], AX.X, ALU.max).then_inc(s["mx_used"], 1)

        def dve_r_diff(dve, x, par, nth, u, k):
            g = 16 * x + 2 * u + k
            if u == 0 and k == 0:
                dve.wait_ge(s[f"const_in{par}"], 16 * nth)
            if not (isinstance(g, int) and g < 2):
                dve.wait_ge(s["lo_ready"], g - 1)
            cols = slice(u * JU, u * JU + JU)
            for n, (d, b, limit, op) in enumerate((((0, 0, EXP_MAX, ALU.min), (1, 1, EXP_MAX, ALU.min)),
                                                   ((0, 0, -EXP_MAX, ALU.max), (2, 3, EXP_MAX, ALU.min)))[k]):
                nc.vector.tensor_scalar(ex[:, k, n], dj[:, d, cols], const[:, par, b:b + 1], limit, ALU.add,
                                        op).then_inc(s["d_ready"], 1)

        def dve_r_hi(dve, x, u, k):
            g = 16 * x + 2 * u + k
            dve.wait_ge(s["r_ready"], g + 1)
            r_stored(dve, x, u - 1, k)
            nc.vector.tensor_copy(rhi[:, k], ex[:, k, 0]).then_inc(s["hi_ready"], 1)

        def dve_m(dve, x, par):
            dve.wait_ge(s["mx_used"], MXN * x + MXN)
            nc.vector.tensor_reduce(mrow[:, :], mxp[:, :, :], AX.X, ALU.max).then_inc(s["m_step"], 1)
            dve.wait_ge(s["m_step"], 4 * x + 1)
            nc.vector.scalar_tensor_tensor(out=mrow[:, :], in0=mrow[:, :], scalar=-1.0, in1=const[:, par, 4:4 + H],
                                           op0=ALU.mult, op1=ALU.subtract).then_inc(s["m_neg"], 1)
            dve.wait_ge(s["m_turned"], x + 1)
            nc.vector.tensor_copy(mT[:, :], tail[0:H, 0, :]).then_inc(s["m_step"], 1)
            dve.wait_ge(s["m_step"], 4 * x + 2)
            if not (isinstance(x, int) and x == 0):
                dve.wait_ge(s["m_out"], 16 * x)
            nc.vector.tensor_copy(mparts[:, 0], mT[:, :]).then_inc(s["m_parts"], 1)
            dve.wait_ge(s["m_parts"], 3 * x + 1)
            nc.vector.tensor_tensor(mT[:, :], mT[:, :], mparts[:, 0], ALU.subtract).then_inc(s["m_step"], 1)
            dve.wait_ge(s["m_step"], 4 * x + 3)
            nc.vector.tensor_copy(mparts[:, 1], mT[:, :]).then_inc(s["m_parts"], 1)
            dve.wait_ge(s["m_parts"], 3 * x + 2)
            nc.vector.tensor_tensor(mT[:, :], mT[:, :], mparts[:, 1], ALU.subtract).then_inc(s["m_step"], 1)
            dve.wait_ge(s["m_step"], 4 * x + 4)
            nc.vector.tensor_copy(mparts[:, 2], mT[:, :]).then_inc(s["m_parts"], 1)
            dve.wait_ge(s["m_parts"], 3 * x + 3)

        def dve_out(dve, c):
            dve.wait_ge(s["pv_done"], STEPS * c + STEPS)
            nc.vector.tensor_copy(oT[:, :, :], acc[:, :, :]).then_inc(s["acc_read"], 1)
            dve.wait_ge(s["o_turned"], c + 1)
            t = tail[:, :, :].rearrange("p g (c w) -> p (g c) w", w=32)
            nc.vector.reciprocal(rl[:, :], t[:, :, HD]).then_inc(s["att_step"], 1)
            dve.wait_ge(s["att_step"], c + 1)
            dve.wait_ge(s["att_free"], c + 1)
            nc.vector.tensor_tensor(att[:, :, :], t[:, :, 0:HD], rl[:, :].unsqueeze(2).broadcast_to([P, H, HD]),
                                    ALU.mult).then_inc(s["att_made"], 1)

        @block.vector
        def _(dve):
            dve.wait_ge(s["dj_in"], 48)
            for m in range(STEPS):
                u, k, at = m // SPU, m % SPU // 4, m % 4
                if at == 0:
                    dve_r_diff(dve, 0, 0, 1, u, k)
                for n in range(2 * m, 2 * m + 2):
                    dve_max(dve, 0, n)
                if at == 3:
                    dve_r_hi(dve, 0, u, k)
            dve_m(dve, 0, 0)

            def chunk(c, par, nth, last):
                for m in range(STEPS):
                    if last:
                        break
                    u, k, at = m // SPU, m % SPU // 4, m % 4
                    if at == 0:
                        dve_r_diff(dve, c + 1, 1 - par, nth + par, u, k)
                    for n in range(mx_units(m), mx_units(m + 1)):
                        dve_max(dve, c + 1, n)
                    if at == 3:
                        dve_r_hi(dve, c + 1, u, k)
                    if m == MX_LAST:
                        dve_m(dve, c + 1, 1 - par)
                dve_out(dve, c)

            in_chunks(dve, chunk)

        def pe_scores(pe, c, par, m, between=lambda: None):
            jt, half = m // 2, m % 2
            if m == 0:
                pe.wait_ge(s["m_in"], 32 * c + 32)
                pe.wait_ge(s["c_made"], 2 * c + 2)
            if m % SPU == 0:
                u = m // SPU
                pe.wait_ge(s[f"r_in{u % 2}"], 32 * (UNITS // 2 * c + u // 2 + 1))
            if m >= 2:
                pe.wait_ge(s["p_ready"], STEPS * c + m - 1)
            u, j0 = m // SPU, jt % 4 * P
            for p in range(4):
                pair = 4 * half + p
                pe.matmul(sc[:, half, p // 2, (p % 2) * 256:(p % 2) * 256 + 256], kst[:, pair, jt * P:jt * P + P],
                          qm[:, par, pair].rearrange("r a t -> r (a t)"), start=(p % 2 == 0), stop=False,
                          skip_group_check=True)
            between()
            for b in range(NB):
                for bank in range(2):
                    out = sc[:, half, bank, :].rearrange("p (h i b) -> p h i b", h=4, b=NB)[:, :, :, b]
                    ins = pe.matmul(out, rst[:, u % 2, b, j0:j0 + P], cm[:, par, half, b, 4 * bank:4 * bank + 4, :],
                                    start=False, stop=(b == NB - 1), skip_group_check=True)
            ins.then_inc(s["scores_ready"], 1)

        def pe_max(pe, x, par, n):
            head, j0 = n // MXU, n % MXU * 512
            if not (isinstance(x, int) and x == 0 and n < 2):
                pe.wait_ge(s["mx_used"], MXN * x + n - 1)
            pe.matmul(mx[:, n % 2, :], qm[:, par, head // 2, head % 2, :], kst[:, head // 2, j0:j0 + 512],
                      start=True, stop=True).then_inc(s["mx_ready"], 1)

        def pe_pv(pe, c, m):
            jt, half = m // 2, m % 2
            pe.wait_ge(s["p_ready"], STEPS * c + m + 1)
            for k in range(HH):
                h = HH * half + k
                ins = pe.matmul(acc[32 * (h % 4):32 * (h % 4) + 32, h // 4, :], vp[:, jt, VW * h:VW * h + 32],
                                pr[:, half, k * P:k * P + P], start=(m == 0 and k < 4), stop=(jt == NT - 1),
                                skip_group_check=True)
            ins.then_inc(s["pv_done"], 1)

        def pe_m(pe, x):
            pe.wait_ge(s["m_neg"], x + 1)
            pe.transpose(tail[0:H, 0, :], mrow[:, :], ident[:, :]).then_inc(s["m_turned"], 1)

        @block.tensor
        def _(pe):
            pe.wait_ge(s["ident_made"], 1)
            pe.wait_ge(s["q_in"], 32)
            for n in range(MXN):
                pe_max(pe, 0, 0, n)
            pe_m(pe, 0)
            pe_scores(pe, 0, 0, 0)

            def chunk(c, par, nth, last):
                for m in range(STEPS):
                    units = [] if last else list(range(mx_units(m), mx_units(m + 1)))

                    def max_unit():
                        if units:
                            if units[0] == 0:
                                pe.wait_ge(s["q_in"], 32 * c + 64)
                            pe_max(pe, c + 1, 1 - par, units.pop(0))

                    if m + 1 < STEPS:
                        pe_scores(pe, c, par, m + 1, max_unit)
                    elif not last:
                        pe_scores(pe, c + 1, 1 - par, 0)
                    max_unit()
                    pe_pv(pe, c, m)
                    max_unit()
                    if m == MX_LAST and not last:
                        pe_m(pe, c + 1)
                pe.wait_ge(s["acc_read"], c + 1)
                for g in range(4):
                    ins = pe.transpose(tail[:, g, :], oT[:, g, :], ident[:, :])
                ins.then_inc(s["o_turned"], 1)

            in_chunks(pe, chunk)


def experts(nc, hidden, woT, bo, wg, w1, b1, w2, b2, att_dram, out):
    with ExitStack() as ctx:
        def sb(name, shape, dt=F32):
            return ctx.enter_context(nc.sbuf_tensor("c_" + name, shape, dt))

        def sem(name):
            return ctx.enter_context(nc.semaphore("c_" + name))

        ps = ctx.enter_context(nc.psum_tensor("c_ps", [P, 8, 512], F32))
        x1 = sb("x1", [P, NT, D])
        a_room = sb("a", [P, NT * D])
        a = a_room[:, :].rearrange("p (t d) -> p t d", t=NT)
        hT = a_room[:, :].bitcast(F16).rearrange("p (o v f t) -> p o v f t", o=2, v=2, f=FT)
        aT = sb("aT", [P, KC, S])
        xT = [sb("xT_hi", [P, KC, S], F16), sb("xT_lo", [P, KC, S], F16)]
        wo = sb("wo", [P, KC, D])
        wgs = sb("wgs", [P, KC, E])
        bob = sb("bob", [P, D])
        b2s = sb("b2s", [E, D])
        b1s = sb("b1s", [P, E, FT])
        ident = sb("ident", [P, P])
        stats = sb("stats", [P, 2, 6])
        mv = sb("mv", [P, NT, 2])
        std = sb("std", [P, NT])
        rstd = sb("rstd", [P, NT])
        lg = sb("lg", [P, NT, E])
        top = sb("top", [P, NT, 8])
        topi = sb("topi", [P, NT, 8], U32)
        topf = sb("topf", [P, NT, TOP])
        iota_i = sb("iota_i", [P, E], mybir.dt.int32)
        iota_f = sb("iota_f", [P, E])
        pw = sb("pw", [P, TOP, NT])
        w = sb("w", [P, NT, E])
        w_b = sb("w_b", [P, NT, E])
        wT = sb("wT", [E, S])
        w32 = sb("w32", [P, 2048])
        w1p = [sb(f"w1p{n}", [P, 2, KC, F], F16) for n in range(2)]
        w2p = [sb(f"w2p{n}", [P, 2, FT, D], F16) for n in range(2)]
        h32 = sb("h32", [P, 2, TB])

        names = ("x_in", "w_in", "zeroed", "ident_made", "iota_made", "dve_step", "var_done", "std_done", "xn_done",
                 "pe_job", "act_job", "dve_job", "xT_done", "top_done", "exp_done", "w_done",
                 "w32_in", "w_split", "relu_done", "h_split", "up_done", "down_done", "added", "stored")
        s = {n: sem(n) for n in names}

        kinds = ([("AT", j) for j in range(16)] + [("O", j) for j in range(16)] + [("XT", j) for j in range(16)]
                 + [("G", 0)] + [("WT", j) for j in range(8)] + [("B2", j) for j in range(16)])
        jobs = ["act" if k in ("AT", "XT") and j % 2 and k == "AT" else "dve" for k, j in kinds]
        freed = {"act": s["act_job"], "dve": s["dve_job"]}
        start = {k: next(n for n, (kk, _) in enumerate(kinds) if kk == k) for k, _ in kinds}

        def act_before(n):
            return sum(1 for e in jobs[:n] if e == "act")

        def dve_before(n):
            return sum(1 for e in jobs[:n] if e == "dve")

        N_W = 6
        block = ctx.enter_context(nc.Block())

        @block.sync
        def _(sp):
            for q in range(4):
                t = slice(8 * q, 8 * q + 8)
                sp.dma_start(a[:, t, :], att_dram.rearrange("t p d -> p t d")[:, t, :]).then_inc(s["x_in"], 16)
                sp.dma_start(x1[:, t, :], hidden.rearrange("o (t p) d -> p (o t) d", p=P)[:, t, :]).then_inc(s["x_in"], 16)
            for dst, src in ((wo[:, :, :], woT.rearrange("(c p) n -> p c n", p=P)),
                             (wgs[:, :, :], wg.rearrange("(c p) n -> p c n", p=P)),
                             (bob[:, :], bo.partition_broadcast(P)),
                             (b2s[:, :], b2),
                             (b1s[:, 0:E // 2, :], b1.rearrange("e (p f) -> p e f", f=FT)[:, 0:E // 2]),
                             (b1s[:, E // 2:E, :], b1.rearrange("e (p f) -> p e f", f=FT)[:, E // 2:E])):
                sp.dma_start(dst, src).then_inc(s["w_in"], 16)
            for e in range(E):
                for n, (dst, src) in enumerate(((w32[:, :].rearrange("p (c f) -> p c f", c=KC),
                                                 w1[e].rearrange("(c p) f -> p c f", p=P)),
                                                (w32[:, :].rearrange("p (f d) -> p f d", f=FT),
                                                 w2[e].rearrange("(p f) d -> p f d", f=FT)))):
                    if e + n > 0:
                        sp.wait_ge(s["w_split"], 2 * (2 * e + n))
                    sp.dma_start(dst, src).then_inc(s["w32_in"], 16)
            for t in range(4):
                sp.wait_ge(s["added"], (E - 1) * NT + 8 * t + 8)
                sp.dma_start(out.rearrange("o (t p) d -> p (o t) d", p=P)[:, 8 * t:8 * t + 8, :],
                             x1[:, 8 * t:8 * t + 8, :]).then_inc(s["stored"], 16)
            sp.wait_ge(s["stored"], 64)

        @block.gpsimd
        def _(pool):
            identity_into(nc, pool, ident[:, :], s["zeroed"], s["ident_made"])
            nc.gpsimd.iota(iota_i[:, :], pattern=[[1, E]], base=0, channel_multiplier=0).then_inc(s["iota_made"], 1)

        def add_result(dve, d):
            e, t = d // NT, d % NT
            dve.wait_ge(s["down_done"], d + 1)
            if e > 0:
                dve.wait_ge(s["added"], d - NT + 1)
            nc.vector.scalar_tensor_tensor(out=x1[:, t], in0=ps[:, 4 + d % 4, 0:D], scalar=w[:, t, e:e + 1],
                                           in1=x1[:, t], op0=ALU.mult, op1=ALU.add).then_inc(s["added"], 1)

        def split_weights(dve, e):
            for n, dst in enumerate((w1p[e % 2], w2p[e % 2])):
                dve.wait_ge(s["w32_in"], 16 * (2 * e + n + 1))
                hi = dst[:, 0].rearrange("p a b -> p (a b)")
                lo = dst[:, 1].rearrange("p a b -> p (a b)")
                nc.vector.tensor_copy(hi, w32[:, :]).then_inc(s["w_split"], 1)
                dve.wait_ge(s["w_split"], 2 * (2 * e + n) + 1)
                nc.vector.tensor_tensor(lo, w32[:, :], hi, ALU.subtract).then_inc(s["w_split"], 1)

        @block.vector
        def _(dve):
            chain = [0]

            def link(ins):
                chain[0] += 1
                ins.then_inc(s["dve_step"], 1)
                dve.wait_ge(s["dve_step"], chain[0])

            split_weights(dve, 0)
            dve.wait_ge(s["x_in"], 128)
            dve.wait_ge(s["w_in"], 16 * N_W)
            for n, (kind, j) in enumerate(kinds):
                if jobs[n] != "dve":
                    continue
                if n == start["XT"]:
                    dve.wait_ge(s["pe_job"], start["O"])
                    for t in range(NT):
                        link(nc.vector.bn_stats(stats[:, t % 2], x1[:, t]))
                        link(nc.vector.bn_aggr(mv[:, t], stats[:, t % 2]))
                    nc.vector.tensor_scalar(rstd[:, :], mv[:, :, 1], EPS, None, ALU.add).then_inc(s["var_done"], 1)
                    dve.wait_ge(s["std_done"], 1)
                    link(nc.vector.reciprocal(rstd[:, :], std[:, :]))
                    for t in range(NT):
                        nc.vector.tensor_scalar(a[:, t], x1[:, t], mv[:, t, 0:1], rstd[:, t:t + 1], ALU.subtract,
                                                ALU.mult).then_inc(s["xn_done"], 1)
                if n == start["WT"]:
                    for t in range(NT):
                        nc.vector.max(out=top[:, t], in_=lg[:, t]).then_inc(s["top_done"], 1)
                        dve.wait_ge(s["top_done"], 2 * t + 1)
                        nc.vector.max_index(topi[:, t], top[:, t], lg[:, t]).then_inc(s["top_done"], 1)
                    dve.wait_ge(s["top_done"], 2 * NT)
                    link(nc.vector.tensor_copy(topf[:, :, :], topi[:, :, 0:TOP]))
                    dve.wait_ge(s["iota_made"], 1)
                    link(nc.vector.tensor_copy(iota_f[:, :], iota_i[:, :]))
                    link(nc.vector.tensor_tensor(pw[:, 1], top[:, :, 1], top[:, :, 0], ALU.subtract))
                    dve.wait_ge(s["exp_done"], 1)
                    link(nc.vector.tensor_scalar(pw[:, 1], pw[:, 0], 1.0, None, ALU.add))
                    link(nc.vector.reciprocal(rstd[:, :], pw[:, 1]))
                    link(nc.vector.tensor_tensor(pw[:, 1], pw[:, 0], rstd[:, :], ALU.mult))
                    iota_b = iota_f[:, :].unsqueeze(1).broadcast_to([P, NT, E])
                    for r, dst, weight in ((0, w, rstd[:, :]), (1, w_b, pw[:, 1])):
                        link(nc.vector.tensor_tensor(dst[:, :, :], iota_b, topf[:, :, r:r + 1].broadcast_to([P, NT, E]),
                                                     ALU.is_equal))
                        link(nc.vector.tensor_tensor(dst[:, :, :], dst[:, :, :],
                                                     weight.unsqueeze(2).broadcast_to([P, NT, E]), ALU.mult))
                    nc.vector.tensor_tensor(w[:, :, :], w[:, :, :], w_b[:, :, :], ALU.add).then_inc(s["w_done"], 1)
                    dve.wait_ge(s["w_done"], 1)
                dve.wait_ge(s["pe_job"], n + 1)
                bank = ps[:, n % 8, :]
                if kind == "AT":
                    nc.vector.tensor_copy(aT[:, j % 2, (j // 2) * 512:(j // 2) * 512 + 512], bank).then_inc(s["dve_job"], 1)
                if kind == "O":
                    link(nc.vector.tensor_tensor(x1[:, 2 * j:2 * j + 2, :], x1[:, 2 * j:2 * j + 2, :],
                                                 bank.rearrange("p (t d) -> p t d", t=2), ALU.add))
                    nc.vector.tensor_tensor(x1[:, 2 * j:2 * j + 2, :], x1[:, 2 * j:2 * j + 2, :],
                                            bob[:, :].unsqueeze(1).broadcast_to([P, 2, D]), ALU.add).then_inc(s["dve_job"], 1)
                    dve.wait_ge(s["dve_job"], dve_before(n) + 1)
                if kind == "XT":
                    cols = slice((j // 2) * 512, (j // 2) * 512 + 512)
                    link(nc.vector.tensor_copy(aT[:, j % 2, cols], bank))
                    nc.vector.tensor_copy(xT[0][:, j % 2, cols], aT[:, j % 2, cols]).then_inc(s["dve_job"], 1)
                    dve.wait_ge(s["dve_job"], dve_before(n) + 1)
                    nc.vector.tensor_tensor(xT[1][:, j % 2, cols], aT[:, j % 2, cols], xT[0][:, j % 2, cols],
                                            ALU.subtract).then_inc(s["xT_done"], 1)
                if kind == "G":
                    nc.vector.tensor_copy(lg[:, :, :], bank[:, 0:NT * E].rearrange("p (t e) -> p t e", e=E)).then_inc(s["dve_job"], 1)
                    dve.wait_ge(s["dve_job"], dve_before(n) + 1)
                if kind == "WT":
                    nc.vector.tensor_copy(wT[:, j * 512:j * 512 + 512], ps[0:E, n % 8, :]).then_inc(s["dve_job"], 1)
                if kind == "B2":
                    nc.vector.tensor_tensor(x1[:, 2 * j:2 * j + 2, :], x1[:, 2 * j:2 * j + 2, :],
                                            bank.rearrange("p (t d) -> p t d", t=2), ALU.add).then_inc(s["dve_job"], 1)
            dve.wait_ge(s["dve_job"], dve_before(len(kinds)))
            for i in range(E * NTB + 1):
                if i < E * NTB:
                    e, tb = i // NTB, i % NTB
                    for f in range(FT):
                        n = i * FT + f
                        dve.wait_ge(s["relu_done"], n + 1)
                        if f == 0 and i >= 2:
                            dve.wait_ge(s["down_done"], 4 * (i - 1))
                        nc.vector.tensor_copy(hT[:, i % 2, 0, f], h32[:, n % 2]).then_inc(s["h_split"], 1)
                        dve.wait_ge(s["h_split"], 2 * n + 1)
                        nc.vector.tensor_tensor(hT[:, i % 2, 1, f], h32[:, n % 2], hT[:, i % 2, 0, f],
                                                ALU.subtract).then_inc(s["h_split"], 1)
                        if i >= 1 and f % 2:
                            d = 4 * (i - 1) + f // 2
                            add_result(dve, d)
                    if tb == 4 and e + 1 < E:
                        if e > 0:
                            dve.wait_ge(s["down_done"], 4 * (e * NTB))
                        split_weights(dve, e + 1)
                else:
                    for d in range(4 * (i - 1), 4 * i):
                        add_result(dve, d)

        @block.scalar
        def _(act):
            for n, (kind, j) in enumerate(kinds):
                if n == start["XT"]:
                    act.wait_ge(s["var_done"], 1)
                    nc.scalar.activation(std[:, :], rstd[:, :], ACT.Sqrt).then_inc(s["std_done"], 1)
                if n == start["WT"]:
                    act.wait_ge(s["dve_step"], 2 * NT + 1 + 16 + 16 + 3)
                    nc.scalar.activation(pw[:, 0], pw[:, 1], ACT.Exp).then_inc(s["exp_done"], 1)
                if jobs[n] != "act":
                    continue
                act.wait_ge(s["pe_job"], n + 1)
                nc.scalar.copy(aT[:, j % 2, (j // 2) * 512:(j // 2) * 512 + 512], ps[:, n % 8, :]).then_inc(s["act_job"], 1)
            for i in range(E * NTB):
                e = i // NTB
                for f in range(FT):
                    n = i * FT + f
                    act.wait_ge(s["up_done"], n + 1)
                    if n >= 2:
                        act.wait_ge(s["h_split"], 2 * (n - 1))
                    nc.scalar.activation(h32[:, n % 2], ps[:, n % 4, :], ACT.Relu, bias=b1s[:, e, f:f + 1]).then_inc(
                        s["relu_done"], 1)

        @block.tensor
        def _(pe):
            pe.wait_ge(s["w_in"], 16 * N_W)
            pe.wait_ge(s["x_in"], 128)
            pe.wait_ge(s["ident_made"], 1)
            for n, (kind, j) in enumerate(kinds):
                own = bank_owner(jobs, n)
                if own:
                    pe.wait_ge(freed[own[0]], own[1])
                if n in (start["O"], start["G"], start["B2"]):
                    if act_before(n):
                        pe.wait_ge(s["act_job"], act_before(n))
                    pe.wait_ge(s["dve_job"], dve_before(n))
                if kind in ("AT", "XT"):
                    c, tb = j % 2, j // 2
                    if kind == "XT":
                        pe.wait_ge(s["xn_done"], 4 * tb + 4)
                    for t in range(4):
                        ins = pe.transpose(ps[:, n % 8, t * P:t * P + P], a[:, 4 * tb + t, c * P:c * P + P], ident[:, :])
                if kind == "O":
                    for t in range(2):
                        tile = 2 * j + t
                        for c in range(KC):
                            ins = pe.matmul(ps[:, n % 8, t * D:t * D + D], aT[:, c, tile * P:tile * P + P], wo[:, c, :],
                                            start=(c == 0), stop=(c == KC - 1))
                if kind == "G":
                    for t in range(NT):
                        for c in range(KC):
                            ins = pe.matmul(ps[:, n % 8, t * E:t * E + E], aT[:, c, t * P:t * P + P], wgs[:, c, :],
                                            start=(c == 0), stop=(c == KC - 1))
                if kind == "WT":
                    pe.wait_ge(s["w_done"], 1)
                    for t in range(4):
                        ins = pe.transpose(ps[0:E, n % 8, t * P:t * P + P], w[:, 4 * j + t, :], ident[:, :])
                if kind == "B2":
                    for t in range(2):
                        tile = 2 * j + t
                        ins = pe.matmul(ps[:, n % 8, t * D:t * D + D], wT[:, tile * P:tile * P + P], b2s[:, :],
                                        start=True, stop=True)
                ins.then_inc(s["pe_job"], 1)
            pe.wait_ge(s["dve_job"], dve_before(len(kinds)))
            pe.wait_ge(s["xT_done"], 16)
            parts = ((0, 0), (1, 0), (0, 1))
            for i in range(E * NTB + 1):
                if i < E * NTB:
                    e, tb = i // NTB, i % NTB
                    if tb == 0:
                        pe.wait_ge(s["w_split"], 4 * e + 4)
                    for f in range(FT):
                        n = i * FT + f
                        if n >= 4:
                            pe.wait_ge(s["relu_done"], n - 3)
                        first = True
                        for c in range(KC):
                            for wp, xp in parts:
                                ins = pe.matmul(ps[:, n % 4, :], w1p[e % 2][:, wp, c, f:F:FT],
                                                xT[xp][:, c, tb * TB:tb * TB + TB], start=first,
                                                stop=(c == KC - 1 and xp == 1))
                                first = False
                        ins.then_inc(s["up_done"], 1)
                if i > 0:
                    e = (i - 1) // NTB
                    for t in range(4):
                        d = 4 * (i - 1) + t
                        if t == 0:
                            pe.wait_ge(s["h_split"], 2 * FT * i)
                        if d >= 4:
                            pe.wait_ge(s["added"], d - 3)
                        for f in range(FT):
                            for hp, wp in parts:
                                ins = pe.matmul(ps[:, 4 + d % 4, 0:D], hT[:, (i - 1) % 2, hp, f, t * P:t * P + P],
                                                w2p[e % 2][:, wp, f, :], start=(f == 0 and hp == 0 and wp == 0),
                                                stop=(f == FT - 1 and wp == 1))
                        ins.then_inc(s["down_done"], 1)


def preln_attention_moe_kernel(nc, hidden, wqT, bq, wkT, bk, wvT, bv, woT, bo, relT, rel_b, lbT, gwT, gate_b,
                               wg, w1, b1, w2, b2, out):
    with ExitStack() as ctx:
        def dram(name, shape, dt=F32):
            return nc.dram_tensor(name, shape, dt, kind="Internal").ap()

        q_dram = dram("q_stacks", (NT, 2, 64, PAIRS, P), F16)
        c_dram = dram("c_values", (NT, 3, 2, P, H), F16)
        dj_dram = dram("key_logits", (3, S))
        const_dram = dram("query_consts", (NT, P, H + 4))
        r_dram = dram("relation_parts", (NT, UNITS, 2, 2, P, JU), F16)
        m_dram = dram("row_maxima", (H, 3, P), F16)
        att_dram = dram("attention_out", (NT, P, D))
        with ExitStack() as attention:
            kst = attention.enter_context(nc.sbuf_tensor("kst", [P, PAIRS, S], F16))
            vp = attention.enter_context(nc.sbuf_tensor("vp", [P, NT, VPAD], F32))
            project_inputs(nc, kst, vp, hidden, wqT, bq, wkT, bk, wvT, bv, relT, rel_b, lbT, gwT, gate_b,
                           q_dram, c_dram, const_dram, dj_dram)
            attend(nc, kst, vp, dj_dram, q_dram, c_dram, const_dram, r_dram, m_dram, att_dram)
        experts(nc, hidden, woT, bo, wg, w1, b1, w2, b2, att_dram, out)


_INS = [("L0_attn_hidden_states", False), ("L0_attn_Wq", True), ("L0_attn_bq", False), ("L0_attn_Wk", True),
        ("L0_attn_bk", False), ("L0_attn_Wv", True), ("L0_attn_bv", False), ("L0_attn_Wo", True),
        ("L0_attn_bo", False), ("L0_attn_rel_W", True), ("L0_attn_rel_b", False), ("L0_attn_logical_bias", True),
        ("L0_attn_gate_W", True), ("L0_attn_gate_b", False), ("L0_ffn_Wg", False), ("L0_ffn_W1", False),
        ("L0_ffn_b1", False), ("L0_ffn_W2", False), ("L0_ffn_b2", False)]


def kernel(**inputs):
    import numpy as _np
    import concourse.bacc as _bacc
    from concourse import mybir as _mybir
    from concourse.bass_utils import run_bass_kernel_spmd as _run

    nc = _bacc.Bacc("TRN2", target_bir_lowering=False, num_devices=1)
    arrays, args = {}, []
    for name, turned in _INS:
        a = _np.asarray(inputs[name])
        a = _np.ascontiguousarray(a.T if turned else a)
        arrays[f"in_{name}_dram"] = a
        args.append(nc.dram_tensor(f"in_{name}_dram", a.shape, _mybir.dt.from_np(a.dtype), kind="ExternalInput").ap())
    args.append(nc.dram_tensor("out_0_dram", (1, S, D), _mybir.dt.float32, kind="ExternalOutput").ap())
    preln_attention_moe_kernel(nc, *args)
    r = _run(nc, [arrays], core_ids=[0])
    return r.results[0]["out_0_dram"]
```

```python
from contextlib import ExitStack

import concourse.bass as bass
from concourse import mybir

F32 = mybir.dt.float32
F16 = mybir.dt.float16
U32 = mybir.dt.uint32
I32 = mybir.dt.int32
ALU = mybir.AluOpType
ACT = mybir.ActivationFunctionType
AX = mybir.AxisListType

P = 128
S, D, H, HD = 4096, 256, 16, 16
NT = S // P
KC = D // P
PAIRS = H // 2
HH = H // 2
NB, BI = 8, 16
JU = 512
UNITS = S // JU
SPU = 2 * JU // P
STEPS = 2 * NT
VW = HD + 1
VPAD = H * VW + 15
E, F, TOP = 8, 1024, 2
FT = F // P
TB = 512
BT = TB // P
NBLK = (TOP * S - E) // TB + E
PAD = NT // 2
GT = 4
GROUPS = NT // GT
EPS = 1e-5
EXP_MAX = 43.0
ROWS = 6 * BI
MX_FIRST, MX_LAST = 2, 57
MXU = S // 512
MXN = H * MXU


def mx_units(m):
    m = min(max(m - MX_FIRST, 0), MX_LAST - MX_FIRST)
    return m * MXN // (MX_LAST - MX_FIRST)


def in_chunks(eng, chunk):
    with eng.Fori(0, (NT - 2) // 2) as pair:
        chunk(pair * 2, 0, pair + 1, False)
        chunk(pair * 2 + 1, 1, pair + 1, False)
    chunk(NT - 2, 0, NT // 2, False)
    chunk(NT - 1, 1, NT // 2, True)


def bank_owner(jobs, n, ring=8):
    if n < ring:
        return None
    eng = jobs[n - ring]
    return eng, sum(1 for e in jobs[:n - ring + 1] if e == eng)


def identity_into(nc, pool, t, zeroed, made):
    nc.gpsimd.memset(t, 0.0).then_inc(zeroed, 1)
    pool.wait_ge(zeroed, 1)
    nc.gpsimd.affine_select(out=t, in_=t, compare_op=ALU.not_equal, fill=1.0, base=0,
                            pattern=[[-1, P]], channel_multiplier=1).then_inc(made, 1)


def project_inputs(nc, kst, vp, hidden, wqT, bq, wkT, bk, wvT, bv, relT, rel_b, lbT, gwT, gate_b,
                   q_dram, c_dram, const_dram, dj_dram):
    with ExitStack() as ctx:
        def sb(name, shape, dt=F32):
            return ctx.enter_context(nc.sbuf_tensor("a_" + name, shape, dt))

        def sem(name):
            return ctx.enter_context(nc.semaphore("a_" + name))

        ps = ctx.enter_context(nc.psum_tensor("a_ps", [P, 8, 512], F32))
        x_room = sb("x_room", [P, NT * D])
        x = x_room[:, :].rearrange("p (t d) -> p t d", t=NT)
        part_lo = x_room[:, :].bitcast(F16).rearrange("p (m s) -> p m s", m=4)
        part_hi = sb("part_hi", [P, 2, S], F16)
        xnT = sb("xnT", [P, KC, S])
        stats = sb("stats", [P, NT // 4, 6])
        mv = sb("mv", [P, NT, 2])
        std = sb("std", [P, NT])
        rstd = sb("rstd", [P, NT])
        ident = sb("ident", [P, P])
        wq = sb("wq", [P, 2, KC, D])
        wv = sb("wv", [P, KC, D])
        rel = sb("rel", [P, 2, KC, 3])
        gw = sb("gw", [P, KC, H + 4])
        wdj = sb("wdj", [P, KC, 3])
        bqk = sb("bqk", [P, 4])
        bvb = sb("bvb", [P, D])
        gb = sb("gb", [P, H + 4])
        rb = sb("rb", [P, 3])
        lb = sb("lb", [P, 3, H])
        lbd = sb("lbd", [P, 2, H])
        mb = sb("mb", [P, H])
        qk32 = sb("qk32", [P, 2, 512])
        g = sb("g", [P, NT, H + 4])
        gate = sb("gate", [P, NT, H])
        consts = sb("consts", [P, NT, H + 4])
        chi = sb("chi", [P, 2, NT, H], F16)
        clo = sb("clo", [P, 2, NT, H], F16)
        zero16 = sb("zero16", [BI, PAIRS * P], F16)

        x_in = [sem(f"x_in{q}") for q in range(4)]
        w_in, zeroed, ident_made, zero_made, ones_made = (sem(n) for n in (
            "w_in", "zeroed", "ident_made", "zero_made", "ones_made"))
        dve_step, act_step = sem("dve_step"), sem("act_step")
        var_done, std_done, xn_done, wts_done = (sem(n) for n in ("var_done", "std_done", "xn_done", "wts_done"))
        pe_job, act_job, dve_job = sem("pe_job"), sem("act_job"), sem("dve_job")
        qk_split = sem("qk_split")
        dj_out = [sem("dj_out0"), sem("dj_out1")]
        ez_done, consts_done, c_done = sem("ez_done"), sem("consts_done"), sem("c_done")
        stored, k_filled, g_ready = sem("stored"), sem("k_filled"), sem("g_ready")

        kinds = ([("T", j) for j in range(16)] + [("G", j) for j in range(2)]
                 + [("QK", j) for j in range(32)] + [("DJ", j) for j in range(8)]
                 + [("V", j) for j in range(16)])
        jobs = ["act" if k == "T" and j % 2 or k in ("QK", "DJ") else "dve" for k, j in kinds]
        freed = {"act": act_job, "dve": dve_job}
        first_qk = next(n for n, (k, _) in enumerate(kinds) if k == "QK")
        last_t = 16
        N_W = 14

        block = ctx.enter_context(nc.Block())

        def act_before(n):
            return sum(1 for e in jobs[:n] if e == "act")

        def dve_before(n):
            return sum(1 for e in jobs[:n] if e == "dve")

        @block.sync
        def _(sp):
            for q in range(4):
                sp.dma_start(x[:, 8 * q:8 * q + 8, :],
                             hidden.rearrange("o (t p) d -> p (o t) d", p=P)[:, 8 * q:8 * q + 8, :]).then_inc(x_in[q], 16)
            for dst, src in ((wq[:, 0], wqT.rearrange("(c p) n -> p c n", p=P)),
                             (wq[:, 1], wkT.rearrange("(c p) n -> p c n", p=P)),
                             (wv[:, :, :], wvT.rearrange("(c p) n -> p c n", p=P)),
                             (rel[:, 0], relT.rearrange("(two c p) k -> two p c k", p=P, two=2)[0]),
                             (rel[:, 1], relT.rearrange("(two c p) k -> two p c k", p=P, two=2)[1]),
                             (gw[:, :, 0:H], gwT.rearrange("(c p) n -> p c n", p=P)),
                             (bqk[:, 0:2], bq.rearrange("(c p) -> p c", p=P)),
                             (bqk[:, 2:4], bk.rearrange("(c p) -> p c", p=P)),
                             (bvb[:, :], bv.partition_broadcast(P)),
                             (gb[:, 0:H], gate_b.partition_broadcast(P)),
                             (rb[:, :], rel_b.partition_broadcast(P)),
                             (lb[:, 0, :], lbT[0].partition_broadcast(P)),
                             (lb[:, 1, :], lbT[1].partition_broadcast(P)),
                             (lb[:, 2, :], lbT[2].partition_broadcast(P))):
                sp.dma_start(dst, src, allow_slow_non_contiguous=True).then_inc(w_in, 16)
            sp.wait_ge(zero_made, 1)
            for xc in range(NT):
                for ab in range(2):
                    sp.dma_start(q_dram[xc, ab, 32:48], zero16[:, :].rearrange("r (q t) -> r q t", q=PAIRS)).then_inc(stored, 16)
            sp.wait_ge(consts_done, 2)
            sp.dma_start(const_dram.rearrange("x p n -> p x n"), consts[:, :, :]).then_inc(stored, 16)
            sp.wait_ge(c_done, 2)
            for part, t in ((0, chi), (1, chi), (2, clo)):
                for k in range(2):
                    sp.dma_start(c_dram[:, part, k].rearrange("x p h -> p x h"), t[:, k]).then_inc(stored, 16)
            for m in range(4):
                sp.wait_ge(qk_split, 16 * (m + 1))
                for pp in range(4):
                    for ab in range(2):
                        r = 32 * pp + 16 * ab
                        pair = 4 * (m % 2) + pp
                        for row, part in ((0, "hi"), (16, "hi" if m < 2 else "lo"), (48, "lo" if m < 2 else "hi")):
                            src = part_hi[r:r + 16, m % 2, :] if part == "hi" else part_lo[r:r + 16, m, :]
                            if m < 2:
                                sp.dma_start(q_dram[:, ab, row:row + 16, pair, :].rearrange("x r t -> r x t"),
                                             src.rearrange("r (x t) -> r x t", t=P)).then_inc(stored, 16)
                            else:
                                sp.dma_start(kst[64 * ab + row:64 * ab + row + 16, pair, :], src).then_inc(k_filled, 16)
            first_dj = next(n for n, (k, _) in enumerate(kinds) if k == "DJ")
            for j in range(8):
                sp.wait_ge(act_job, act_before(first_dj + j) + 1)
                sp.dma_start(dj_dram[:, j * 512:j * 512 + 512], qk32[0:3, j % 2, :]).then_inc(dj_out[j % 2], 16)
            for q in dj_out:
                sp.wait_ge(q, 64)
            sp.wait_ge(k_filled, 16 * 48)
            sp.wait_ge(stored, 16 * (64 + 48 + 1 + 6))

        @block.gpsimd
        def _(pool):
            nc.gpsimd.memset(zero16[:, :], 0.0).then_inc(zero_made, 1)
            identity_into(nc, pool, ident[:, :], zeroed, ident_made)
            nc.gpsimd.memset(vp[:, :, :], 1.0).then_inc(ones_made, 1)
            for i, r in enumerate((32, 96)):
                pool.wait_ge(ones_made, i + 1)
                nc.gpsimd.memset(kst[r:r + 16, :, :], 1.0).then_inc(ones_made, 1)

        @block.vector
        def _(dve):
            chain = [0]

            def link(ins):
                chain[0] += 1
                ins.then_inc(dve_step, 1)
                dve.wait_ge(dve_step, chain[0])

            def normalise(q):
                dve.wait_ge(std_done, q + 1)
                link(nc.vector.reciprocal(rstd[:, 8 * q:8 * q + 8], std[:, 8 * q:8 * q + 8]))
                for t in range(8 * q, 8 * q + 8):
                    nc.vector.tensor_scalar(x[:, t], x[:, t], mv[:, t, 0:1], rstd[:, t:t + 1], ALU.subtract,
                                            ALU.mult).then_inc(xn_done, 1)

            for q in range(4):
                dve.wait_ge(x_in[q], 16)
                for t in range(8):
                    nc.vector.bn_stats(stats[:, t], x[:, 8 * q + t]).then_inc(dve_step, 1)
                chain[0] += 8
                dve.wait_ge(dve_step, chain[0])
                for t in range(8):
                    nc.vector.bn_aggr(mv[:, 8 * q + t], stats[:, t]).then_inc(dve_step, 1)
                chain[0] += 8
                dve.wait_ge(dve_step, chain[0])
                nc.vector.tensor_scalar(rstd[:, 8 * q:8 * q + 8], mv[:, 8 * q:8 * q + 8, 1], EPS, None,
                                        ALU.add).then_inc(var_done, 1)
                if q:
                    normalise(q - 1)
            normalise(3)
            for n, (kind, j) in enumerate(kinds):
                if n == last_t:
                    dve.wait_ge(w_in, 16 * N_W)
                    for i, (a, b) in enumerate(((1, 0), (2, 0), (0, 1), (2, 1))):
                        nc.vector.tensor_tensor(gw[:, :, H + i:H + i + 1], rel[:, 0, :, a:a + 1], rel[:, 0, :, b:b + 1],
                                                ALU.subtract).then_inc(wts_done, 1)
                        nc.vector.tensor_tensor(gb[:, H + i:H + i + 1], rb[:, a:a + 1], rb[:, b:b + 1],
                                                ALU.subtract).then_inc(wts_done, 1)
                    for i, (a, b) in enumerate(((1, 0), (2, 0), (2, 1))):
                        link(nc.vector.tensor_tensor(wdj[:, :, i:i + 1], rel[:, 1, :, a:a + 1], rel[:, 1, :, b:b + 1],
                                                     ALU.subtract))
                    for k in range(2):
                        nc.vector.tensor_tensor(lbd[:, k], lb[:, k], lb[:, 2], ALU.subtract).then_inc(wts_done, 1)
                    dve.wait_ge(wts_done, 10)
                    link(nc.vector.tensor_tensor(mb[:, :], lbd[:, 0], lbd[:, 1], ALU.max))
                    link(nc.vector.tensor_scalar(mb[:, :], mb[:, :], 0.0, None, ALU.max))
                if n == first_qk:
                    dve.wait_ge(ez_done, 1)
                    link(nc.vector.tensor_scalar(gate[:, :, :], gate[:, :, :], 1.0, None, ALU.add))
                    link(nc.vector.reciprocal(gate[:, :, :], gate[:, :, :]))
                    nc.vector.tensor_copy(consts[:, :, 0:4], g[:, :, H:H + 4]).then_inc(consts_done, 1)
                    nc.vector.tensor_tensor(consts[:, :, 4:4 + H], gate[:, :, :],
                                            mb[:, :].unsqueeze(1).broadcast_to([P, NT, H]), ALU.mult).then_inc(consts_done, 1)
                    for k in range(2):
                        link(nc.vector.tensor_tensor(g[:, :, 0:H], gate[:, :, :],
                                                     lbd[:, k].unsqueeze(1).broadcast_to([P, NT, H]), ALU.mult))
                        link(nc.vector.tensor_copy(chi[:, k], g[:, :, 0:H]))
                        nc.vector.tensor_tensor(clo[:, k], g[:, :, 0:H], chi[:, k], ALU.subtract).then_inc(c_done, 1)
                        dve.wait_ge(c_done, k + 1)
                if kind == "QK":
                    m, tb = j // 8, j % 8
                    dve.wait_ge(act_job, act_before(n) + 1)
                    if n == first_qk:
                        dve.wait_ge(pe_job, last_t)
                    if m == 2 and tb == 0:
                        dve.wait_ge(stored, 16 * (2 * NT + 7 + 48))
                    cols = slice(tb * 512, tb * 512 + 512)
                    nc.vector.tensor_copy(part_hi[:, m % 2, cols], qk32[:, j % 2, :]).then_inc(qk_split, 1)
                    dve.wait_ge(qk_split, 2 * j + 1)
                    nc.vector.tensor_tensor(part_lo[:, m, cols], qk32[:, j % 2, :], part_hi[:, m % 2, cols],
                                            ALU.subtract).then_inc(qk_split, 1)
                if jobs[n] != "dve":
                    continue
                dve.wait_ge(pe_job, n + 1)
                if kind == "T":
                    nc.vector.tensor_copy(xnT[:, j % 2, (j // 2) * 512:(j // 2) * 512 + 512], ps[:, n % 8, :]).then_inc(dve_job, 1)
                if kind == "V":
                    if j == 0:
                        dve.wait_ge(ones_made, 3)
                    dst = vp[:, 2 * j:2 * j + 2, 0:H * VW].rearrange("p t (h w) -> p t h w", w=VW)
                    for t in range(2):
                        ins = nc.vector.tensor_tensor(dst[:, t, :, 0:HD],
                                                      ps[:, n % 8, t * D:t * D + D].rearrange("p (h w) -> p h w", w=HD),
                                                      bvb[:, :].rearrange("p (h w) -> p h w", w=HD), ALU.add)
                    ins.then_inc(dve_job, 1)
                if kind == "G":
                    w = NT // 2 * (H + 4)
                    ins = nc.vector.tensor_tensor(g[:, j * 16:j * 16 + 16, :],
                                                  ps[:, n % 8, 0:w].rearrange("p (t n) -> p t n", n=H + 4),
                                                  gb[:, :].unsqueeze(1).broadcast_to([P, 16, H + 4]), ALU.add)
                    ins.then_inc(dve_job, 1)

        @block.scalar
        def _(act):
            for q in range(4):
                act.wait_ge(var_done, q + 1)
                nc.scalar.activation(std[:, 8 * q:8 * q + 8], rstd[:, 8 * q:8 * q + 8], ACT.Sqrt).then_inc(std_done, 1)
            for n, (kind, j) in enumerate(kinds):
                if n == first_qk:
                    act.wait_ge(dve_job, dve_before(first_qk))
                    nc.scalar.activation(gate[:, :, :], g[:, :, 0:H], ACT.Exp, scale=-1.0).then_inc(ez_done, 1)
                    act.wait_ge(w_in, 16 * N_W)
                    nc.scalar.mul(bqk[:, 0:2], bqk[:, 0:2], HD ** -0.5).then_inc(act_step, 1)
                    act.wait_ge(act_step, 1)
                if jobs[n] != "act":
                    continue
                act.wait_ge(pe_job, n + 1)
                if kind == "T":
                    nc.scalar.copy(xnT[:, j % 2, (j // 2) * 512:(j // 2) * 512 + 512], ps[:, n % 8, :]).then_inc(act_job, 1)
                if kind == "DJ":
                    if j == 0:
                        act.wait_ge(qk_split, 64)
                    if j >= 2:
                        act.wait_ge(dj_out[j % 2], 16 * (j // 2))
                    nc.scalar.copy(qk32[0:3, j % 2, :], ps[0:3, n % 8, :]).then_inc(act_job, 1)
                if kind == "QK":
                    if j >= 2:
                        act.wait_ge(qk_split, 2 * (j - 1))
                    m = j // 8
                    nc.scalar.activation(qk32[:, j % 2, :], ps[:, n % 8, :], ACT.Identity, bias=bqk[:, m:m + 1],
                                         scale=HD ** -0.5 if m < 2 else 1.0).then_inc(act_job, 1)

        @block.tensor
        def _(pe):
            pe.wait_ge(ident_made, 1)
            for n, (kind, j) in enumerate(kinds):
                own = bank_owner(jobs, n)
                if own:
                    pe.wait_ge(freed[own[0]], own[1])
                if kind == "T":
                    c, tb = j % 2, j // 2
                    pe.wait_ge(xn_done, 4 * tb + 4)
                    for t in range(4):
                        ins = pe.transpose(ps[:, n % 8, t * P:t * P + P], x[:, 4 * tb + t, c * P:c * P + P], ident[:, :])
                if n == last_t:
                    pe.wait_ge(w_in, 16 * N_W)
                    pe.wait_ge(wts_done, 10)
                    pe.wait_ge(act_job, act_before(n))
                    pe.wait_ge(dve_job, dve_before(n))
                if kind == "G":
                    for t in range(16):
                        tile = 16 * j + t
                        for c in range(KC):
                            ins = pe.matmul(ps[:, n % 8, t * (H + 4):(t + 1) * (H + 4)], xnT[:, c, tile * P:tile * P + P],
                                            gw[:, c, :], start=(c == 0), stop=(c == KC - 1))
                if kind == "QK":
                    m, tb = j // 8, j % 8
                    for c in range(KC):
                        ins = pe.matmul(ps[:, n % 8, :], wq[:, m // 2, c, (m % 2) * P:(m % 2) * P + P],
                                        xnT[:, c, tb * 512:tb * 512 + 512], start=(c == 0), stop=(c == KC - 1))
                if kind == "DJ":
                    for c in range(KC):
                        ins = pe.matmul(ps[0:3, n % 8, :], wdj[:, c, :], xnT[:, c, j * 512:j * 512 + 512],
                                        start=(c == 0), stop=(c == KC - 1))
                if kind == "V":
                    for t in range(2):
                        tile = 2 * j + t
                        for c in range(KC):
                            ins = pe.matmul(ps[:, n % 8, t * D:t * D + D], xnT[:, c, tile * P:tile * P + P],
                                            wv[:, c, :], start=(c == 0), stop=(c == KC - 1))
                ins.then_inc(pe_job, 1)


def attend(nc, kst, vp, dj_dram, q_dram, c_dram, const_dram, r_dram, m_dram, att_dram):
    with ExitStack() as ctx:
        def sb(name, shape, dt=F32):
            return ctx.enter_context(nc.sbuf_tensor("b_" + name, shape, dt))

        def sem(name):
            return ctx.enter_context(nc.semaphore("b_" + name))

        sc = ctx.enter_context(nc.psum_tensor("b_sc", [P, 2, 2, 512], F32))
        mx = ctx.enter_context(nc.psum_tensor("b_mx", [P, 2, 512], F32))
        acc = ctx.enter_context(nc.psum_tensor("b_acc", [P, 4, P], F32))
        tail = ctx.enter_context(nc.psum_tensor("b_tail", [P, 4, P], F32))

        dj = sb("dj", [P, 3, S])
        rst = sb("rst", [ROWS, 2, NB, JU], F16)
        pr = sb("pr", [P, 2, HH * P])
        qm = sb("qm", [P, 2, PAIRS, 2, P], F16)
        cm = sb("cm", [ROWS, 2, 2, NB, HH, BI], F16)
        cval = sb("cval", [ROWS, 2, NB, H], F16)
        eye = sb("eye", [ROWS, BI], F16)
        ident = sb("ident", [P, P])
        const = sb("const", [P, 2, H + 4])
        ex = sb("ex", [P, 2, 2, JU])
        rhi = sb("rhi", [P, 2, JU], F16)
        rlo = sb("rlo", [P, 2, JU], F16)
        mxp = sb("mxp", [P, H, MXU])
        mrow = sb("mrow", [P, H])
        mT = sb("mT", [H, P])
        mparts = sb("mparts", [H, 3, P], F16)
        oT = sb("oT", [P, 4, P])
        rl = sb("rl", [P, H])
        att = sb("att", [P, H, HD])

        names = ("zeroed", "ident_made", "eye_made", "dj_in", "q_zeroed", "att_zeroed",
                 "q_in", "m_in", "const_in0", "const_in1", "cval_in0", "cval_in1", "c_made",
                 "scores_ready", "p_ready", "pv_done", "mx_ready", "mx_used", "m_step", "m_neg", "m_turned", "m_parts",
                 "m_out", "d_ready", "e_ready", "sum_ready", "ln_ready", "r_ready", "hi_ready", "lo_ready",
                 "r_out00", "r_out01", "r_out10", "r_out11", "r_in0", "r_in1",
                 "acc_read", "o_turned", "att_step", "att_made", "att_out", "att_free", "sp_waited")
        s = {n: sem(n) for n in names}

        block = ctx.enter_context(nc.Block())

        def r_stored(eng, x, u, k):
            if u >= 0:
                eng.wait_ge(s[f"r_out{k}{u % 2}"], 32 * (UNITS // 2 * x + u // 2 + 1))
            elif not (isinstance(x, int) and x == 0):
                eng.wait_ge(s[f"r_out{k}1"], 32 * (UNITS // 2 * x))

        def waited(sp):
            sp.sem_inc(s["sp_waited"], 1)

        def sp_q(sp, x, par):
            for ab in range(2):
                sp.dma_start(qm[64 * ab:64 * ab + 64, par, :, ab, :],
                             q_dram[bass.ds(x, 1), ab].rearrange("o r q t -> r (o q) t")).then_inc(s["q_in"], 16)

        def sp_consts(sp, x, par):
            sp.dma_start(cval[:, par].rearrange("r b h -> r (b h)"),
                         c_dram[bass.ds(x, 1)].rearrange("o a k (i b) h -> (o a k i) (b h)", b=NB)).then_inc(s[f"cval_in{par}"], 16)
            sp.dma_start(const[:, par], const_dram[bass.ds(x, 1)].rearrange("o p n -> (o p) n")).then_inc(s[f"const_in{par}"], 16)

        def sp_write_r(sp, x, u):
            for k in range(2):
                sp.wait_ge(s["lo_ready"], 16 * x + 2 * u + k + 1)
                waited(sp)
                for part, t in ((0, rhi), (1, rlo)):
                    sp.dma_start(r_dram[bass.ds(x, 1), u, part, k].rearrange("o i j -> (o i) j"), t[:, k]).then_inc(
                        s[f"r_out{k}{u % 2}"], 16)

        def sp_read_r(sp, x, u, written):
            for k in range(2):
                sp.wait_ge(s[f"r_out{k}{u % 2}"], 32 * written)
            waited(sp)
            src = r_dram[bass.ds(x, 1), u].rearrange("o a k (i b) j -> (o a k i) (b j)", b=NB)
            dst = rst[:, u % 2].rearrange("r b j -> r (b j)")
            sp.dma_start(dst[0:64], src).then_inc(s[f"r_in{u % 2}"], 16)
            sp.dma_start(dst[64:96], src[0:32]).then_inc(s[f"r_in{u % 2}"], 16)

        def sp_m(sp, x, par):
            sp.wait_ge(s["m_parts"], 3 * x + 3)
            waited(sp)
            if not (isinstance(x, int) and x == 0):
                sp.wait_ge(s["m_in"], 32 * x)
            sp.dma_start(m_dram[:, :, :], mparts[:, :, :]).then_inc(s["m_out"], 16)
            sp.wait_ge(s["m_out"], 16 * x + 16)
            for ab in range(2):
                sp.dma_start(qm[64 * ab + 32:64 * ab + 35, par, :, ab, :],
                             m_dram.rearrange("(q ab) s i -> ab s q i", ab=2)[ab]).then_inc(s["m_in"], 16)

        @block.sync
        def _(sp):
            for d in range(3):
                sp.dma_start(dj[:, d, :], dj_dram[d].partition_broadcast(P)).then_inc(s["dj_in"], 16)
            sp.wait_ge(s["q_zeroed"], 1)
            for x in range(2):
                sp_consts(sp, x, x)
            sp_q(sp, 0, 0)
            sp.wait_ge(s["att_zeroed"], 1)
            sp.dma_start(att_dram[0], att[:, :, :].rearrange("p h w -> p (h w)")).then_inc(s["att_out"], 16)
            for u in range(UNITS):
                sp_write_r(sp, 0, u)
            sp_read_r(sp, 0, 0, UNITS // 2)
            sp_m(sp, 0, 0)
            sp_q(sp, 1, 1)

            def chunk(c, par, nth, last):
                more = not last and not (isinstance(c, int) and c + 2 >= NT)
                if more:
                    sp_consts(sp, c + 2, par)
                for u in range(UNITS):
                    if u + 1 < UNITS:
                        if u > 0:
                            sp.wait_ge(s["scores_ready"], STEPS * c + SPU * u)
                        sp_read_r(sp, c, u + 1, UNITS // 2 * (c + 1) + (0 if last else len(range((u + 1) % 2, u, 2))))
                    else:
                        sp.wait_ge(s["att_out"], 16 * c + 16)
                        sp.sem_inc(s["att_free"], 1)
                        if not last:
                            sp.wait_ge(s["scores_ready"], STEPS * c + SPU * u)
                            sp_read_r(sp, c + 1, 0, UNITS // 2 * (c + 2))
                    if not last:
                        if u + 1 == UNITS:
                            sp_m(sp, c + 1, 1 - par)
                        sp_write_r(sp, c + 1, u)
                if more:
                    sp.wait_ge(s["scores_ready"], STEPS * c + STEPS)
                    waited(sp)
                    sp_q(sp, c + 2, par)
                sp.wait_ge(s["att_made"], c + 1)
                waited(sp)
                sp.dma_start(att_dram[bass.ds(c, 1)].rearrange("o p n -> (o p) n"),
                             att[:, :, :].rearrange("p h w -> p (h w)")).then_inc(s["att_out"], 16)

            in_chunks(sp, chunk)
            sp.wait_ge(s["att_out"], 16 * NT + 16)

        def pool_c(pool, x, par, nth):
            pool.wait_ge(s[f"cval_in{par}"], 16 * nth)
            if not (isinstance(x, int) and x < 2):
                pool.wait_ge(s["scores_ready"], STEPS * (x - 1))
            for half in range(2):
                nc.gpsimd.tensor_tensor(cm[:, par, half],
                                        cval[:, par, :, HH * half:HH * half + HH].unsqueeze(3).broadcast_to([ROWS, NB, HH, BI]),
                                        eye[:, :].unsqueeze(1).unsqueeze(1).broadcast_to([ROWS, NB, HH, BI]),
                                        ALU.mult).then_inc(s["c_made"], 1)

        def pool_r(pool, x):
            for u in range(UNITS):
                for k in range(2):
                    g = 16 * x + 2 * u + k
                    pool.wait_ge(s["e_ready"], 2 * g + 2)
                    nc.gpsimd.tensor_tensor(ex[:, k, 0], ex[:, k, 0], ex[:, k, 1], ALU.add).then_inc(s["sum_ready"], 1)
                    pool.wait_ge(s["hi_ready"], g + 1)
                    nc.gpsimd.tensor_tensor(rlo[:, k], ex[:, k, 0], rhi[:, k], ALU.subtract).then_inc(s["lo_ready"], 1)

        @block.gpsimd
        def _(pool):
            identity_into(nc, pool, ident[:, :], s["zeroed"], s["ident_made"])
            nc.gpsimd.memset(qm[:, :, :, :, :], 0.0).then_inc(s["q_zeroed"], 1)
            nc.gpsimd.memset(att[:, :, :], 0.0).then_inc(s["att_zeroed"], 1)
            nc.gpsimd.memset(eye[:, :], 0.0).then_inc(s["eye_made"], 1)
            for n in range(ROWS // BI):
                pool.wait_ge(s["eye_made"], n + 1)
                nc.gpsimd.affine_select(out=eye[:, :], in_=eye[:, :], compare_op=ALU.not_equal, fill=1.0,
                                        base=-BI * n, pattern=[[-1, BI]], channel_multiplier=1).then_inc(s["eye_made"], 1)
            pool.wait_ge(s["eye_made"], ROWS // BI + 1)
            pool_c(pool, 0, 0, 1)
            pool_r(pool, 0)
            pool_c(pool, 1, 1, 1)

            def chunk(c, par, nth, last):
                if not last:
                    pool_r(pool, c + 1)
                if not last and not (isinstance(c, int) and c + 2 >= NT):
                    pool_c(pool, c + 2, par, nth + 1)

            in_chunks(pool, chunk)

        def act_r_exp(act, x, u, k):
            act.wait_ge(s["d_ready"], 2 * (16 * x + 2 * u + k) + 2)
            for n, sign in enumerate(((1.0, 1.0), (-1.0, 1.0))[k]):
                nc.scalar.activation(ex[:, k, n], ex[:, k, n], ACT.Exp, scale=sign).then_inc(s["e_ready"], 1)

        def act_r_inv(act, x, u, k):
            g = 16 * x + 2 * u + k
            act.wait_ge(s["sum_ready"], g + 1)
            nc.scalar.activation(ex[:, k, 0], ex[:, k, 0], ACT.Ln, bias=1.0).then_inc(s["ln_ready"], 1)
            act.wait_ge(s["ln_ready"], g + 1)
            nc.scalar.activation(ex[:, k, 0], ex[:, k, 0], ACT.Exp, scale=-1.0).then_inc(s["r_ready"], 1)

        @block.scalar
        def _(act):
            nc.scalar.preload_act_table_set("natural_log_exp_and_others")
            for u in range(UNITS):
                for k in range(2):
                    act_r_exp(act, 0, u, k)
                    act_r_inv(act, 0, u, k)

            def chunk(c, par, nth, last):
                for m in range(STEPS):
                    act.wait_ge(s["scores_ready"], STEPS * c + m + 1)
                    if m >= 2:
                        act.wait_ge(s["pv_done"], STEPS * c + m - 1)
                    nc.scalar.activation(pr[:, m % 2, :], sc[:, m % 2].rearrange("p a b -> p (a b)"),
                                         ACT.Exp).then_inc(s["p_ready"], 1)
                    if not last:
                        u, k, at = m // SPU, m % SPU // 4, m % 4
                        if at == 1:
                            act_r_exp(act, c + 1, u, k)
                        if at == 2:
                            act_r_inv(act, c + 1, u, k)

            in_chunks(act, chunk)

        def dve_max(dve, x, n):
            dve.wait_ge(s["mx_ready"], MXN * x + n + 1)
            nc.vector.tensor_reduce(mxp[:, n // MXU, n % MXU:n % MXU + 1], mx[:, n % 2, :], AX.X, ALU.max).then_inc(s["mx_used"], 1)

        def dve_r_diff(dve, x, par, nth, u, k):
            g = 16 * x + 2 * u + k
            if u == 0 and k == 0:
                dve.wait_ge(s[f"const_in{par}"], 16 * nth)
            if not (isinstance(g, int) and g < 2):
                dve.wait_ge(s["lo_ready"], g - 1)
            cols = slice(u * JU, u * JU + JU)
            for n, (d, b, limit, op) in enumerate((((0, 0, EXP_MAX, ALU.min), (1, 1, EXP_MAX, ALU.min)),
                                                   ((0, 0, -EXP_MAX, ALU.max), (2, 3, EXP_MAX, ALU.min)))[k]):
                nc.vector.tensor_scalar(ex[:, k, n], dj[:, d, cols], const[:, par, b:b + 1], limit, ALU.add,
                                        op).then_inc(s["d_ready"], 1)

        def dve_r_hi(dve, x, u, k):
            g = 16 * x + 2 * u + k
            dve.wait_ge(s["r_ready"], g + 1)
            r_stored(dve, x, u - 1, k)
            nc.vector.tensor_copy(rhi[:, k], ex[:, k, 0]).then_inc(s["hi_ready"], 1)

        def dve_m(dve, x, par):
            dve.wait_ge(s["mx_used"], MXN * x + MXN)
            nc.vector.tensor_reduce(mrow[:, :], mxp[:, :, :], AX.X, ALU.max).then_inc(s["m_step"], 1)
            dve.wait_ge(s["m_step"], 4 * x + 1)
            nc.vector.scalar_tensor_tensor(out=mrow[:, :], in0=mrow[:, :], scalar=-1.0, in1=const[:, par, 4:4 + H],
                                           op0=ALU.mult, op1=ALU.subtract).then_inc(s["m_neg"], 1)
            dve.wait_ge(s["m_turned"], x + 1)
            nc.vector.tensor_copy(mT[:, :], tail[0:H, 0, :]).then_inc(s["m_step"], 1)
            dve.wait_ge(s["m_step"], 4 * x + 2)
            if not (isinstance(x, int) and x == 0):
                dve.wait_ge(s["m_out"], 16 * x)
            nc.vector.tensor_copy(mparts[:, 0], mT[:, :]).then_inc(s["m_parts"], 1)
            dve.wait_ge(s["m_parts"], 3 * x + 1)
            nc.vector.tensor_tensor(mT[:, :], mT[:, :], mparts[:, 0], ALU.subtract).then_inc(s["m_step"], 1)
            dve.wait_ge(s["m_step"], 4 * x + 3)
            nc.vector.tensor_copy(mparts[:, 1], mT[:, :]).then_inc(s["m_parts"], 1)
            dve.wait_ge(s["m_parts"], 3 * x + 2)
            nc.vector.tensor_tensor(mT[:, :], mT[:, :], mparts[:, 1], ALU.subtract).then_inc(s["m_step"], 1)
            dve.wait_ge(s["m_step"], 4 * x + 4)
            nc.vector.tensor_copy(mparts[:, 2], mT[:, :]).then_inc(s["m_parts"], 1)
            dve.wait_ge(s["m_parts"], 3 * x + 3)

        def dve_out(dve, c):
            dve.wait_ge(s["pv_done"], STEPS * c + STEPS)
            nc.vector.tensor_copy(oT[:, :, :], acc[:, :, :]).then_inc(s["acc_read"], 1)
            dve.wait_ge(s["o_turned"], c + 1)
            t = tail[:, :, :].rearrange("p g (c w) -> p (g c) w", w=32)
            nc.vector.reciprocal(rl[:, :], t[:, :, HD]).then_inc(s["att_step"], 1)
            dve.wait_ge(s["att_step"], c + 1)
            dve.wait_ge(s["att_free"], c + 1)
            nc.vector.tensor_tensor(att[:, :, :], t[:, :, 0:HD], rl[:, :].unsqueeze(2).broadcast_to([P, H, HD]),
                                    ALU.mult).then_inc(s["att_made"], 1)

        @block.vector
        def _(dve):
            dve.wait_ge(s["dj_in"], 48)
            for m in range(STEPS):
                u, k, at = m // SPU, m % SPU // 4, m % 4
                if at == 0:
                    dve_r_diff(dve, 0, 0, 1, u, k)
                for n in range(2 * m, 2 * m + 2):
                    dve_max(dve, 0, n)
                if at == 3:
                    dve_r_hi(dve, 0, u, k)
            dve_m(dve, 0, 0)

            def chunk(c, par, nth, last):
                for m in range(STEPS):
                    if last:
                        break
                    u, k, at = m // SPU, m % SPU // 4, m % 4
                    if at == 0:
                        dve_r_diff(dve, c + 1, 1 - par, nth + par, u, k)
                    for n in range(mx_units(m), mx_units(m + 1)):
                        dve_max(dve, c + 1, n)
                    if at == 3:
                        dve_r_hi(dve, c + 1, u, k)
                    if m == MX_LAST:
                        dve_m(dve, c + 1, 1 - par)
                dve_out(dve, c)

            in_chunks(dve, chunk)

        def pe_scores(pe, c, par, m, between=lambda: None):
            jt, half = m // 2, m % 2
            if m == 0:
                pe.wait_ge(s["m_in"], 32 * c + 32)
                pe.wait_ge(s["c_made"], 2 * c + 2)
            if m % SPU == 0:
                u = m // SPU
                pe.wait_ge(s[f"r_in{u % 2}"], 32 * (UNITS // 2 * c + u // 2 + 1))
            if m >= 2:
                pe.wait_ge(s["p_ready"], STEPS * c + m - 1)
            u, j0 = m // SPU, jt % 4 * P
            for p in range(4):
                pair = 4 * half + p
                pe.matmul(sc[:, half, p // 2, (p % 2) * 256:(p % 2) * 256 + 256], kst[:, pair, jt * P:jt * P + P],
                          qm[:, par, pair].rearrange("r a t -> r (a t)"), start=(p % 2 == 0), stop=False,
                          skip_group_check=True)
            between()
            for b in range(NB):
                for bank in range(2):
                    out = sc[:, half, bank, :].rearrange("p (h i b) -> p h i b", h=4, b=NB)[:, :, :, b]
                    ins = pe.matmul(out, rst[:, u % 2, b, j0:j0 + P], cm[:, par, half, b, 4 * bank:4 * bank + 4, :],
                                    start=False, stop=(b == NB - 1), skip_group_check=True)
            ins.then_inc(s["scores_ready"], 1)

        def pe_max(pe, x, par, n):
            head, j0 = n // MXU, n % MXU * 512
            if not (isinstance(x, int) and x == 0 and n < 2):
                pe.wait_ge(s["mx_used"], MXN * x + n - 1)
            pe.matmul(mx[:, n % 2, :], qm[:, par, head // 2, head % 2, :], kst[:, head // 2, j0:j0 + 512],
                      start=True, stop=True).then_inc(s["mx_ready"], 1)

        def pe_pv(pe, c, m):
            jt, half = m // 2, m % 2
            pe.wait_ge(s["p_ready"], STEPS * c + m + 1)
            for k in range(HH):
                h = HH * half + k
                ins = pe.matmul(acc[32 * (h % 4):32 * (h % 4) + 32, h // 4, :], vp[:, jt, VW * h:VW * h + 32],
                                pr[:, half, k * P:k * P + P], start=(m == 0 and k < 4), stop=(jt == NT - 1),
                                skip_group_check=True)
            ins.then_inc(s["pv_done"], 1)

        def pe_m(pe, x):
            pe.wait_ge(s["m_neg"], x + 1)
            pe.transpose(tail[0:H, 0, :], mrow[:, :], ident[:, :]).then_inc(s["m_turned"], 1)

        @block.tensor
        def _(pe):
            pe.wait_ge(s["ident_made"], 1)
            pe.wait_ge(s["q_in"], 32)
            for n in range(MXN):
                pe_max(pe, 0, 0, n)
            pe_m(pe, 0)
            pe_scores(pe, 0, 0, 0)
            pe_scores(pe, 0, 0, 1)

            def chunk(c, par, nth, last):
                for m in range(STEPS):
                    units = [] if last else list(range(mx_units(m), mx_units(m + 1)))

                    def max_unit():
                        if units:
                            if units[0] == 0:
                                pe.wait_ge(s["q_in"], 32 * c + 64)
                            pe_max(pe, c + 1, 1 - par, units.pop(0))

                    if 0 < m < STEPS - 1:
                        pe_scores(pe, c, par, m + 1, max_unit)
                    elif m > 0 and not last:
                        pe_scores(pe, c + 1, 1 - par, 0)
                    max_unit()
                    pe_pv(pe, c, m)
                    max_unit()
                    if m == MX_LAST and not last:
                        pe_m(pe, c + 1)
                if not last:
                    pe_scores(pe, c + 1, 1 - par, 1)
                pe.wait_ge(s["acc_read"], c + 1)
                for g in range(4):
                    ins = pe.transpose(tail[:, g, :], oT[:, g, :], ident[:, :])
                ins.then_inc(s["o_turned"], 1)

            in_chunks(pe, chunk)


def experts(nc, hidden, woT, bo, wg, w1, b1, w2, b2, att_dram, xs_dram, ys_dram, out):
    with ExitStack() as ctx:
        def sb(name, shape, dt=F32):
            return ctx.enter_context(nc.sbuf_tensor("c_" + name, shape, dt))

        def sem(name):
            return ctx.enter_context(nc.semaphore("c_" + name))

        ps = ctx.enter_context(nc.psum_tensor("c_ps", [P, 8, 512], F32))
        x1 = sb("x1", [P, NT, D])
        a_room = sb("a", [P, NT * D])
        a = a_room[:, :].rearrange("p (t d) -> p t d", t=NT)
        hT = a_room[:, :].bitcast(F16).rearrange("p (o v f t) -> p o v f t", o=2, v=2, f=FT)
        aT_room = sb("aT", [P, KC * S])
        aT = aT_room[:, :].rearrange("p (c s) -> p c s", c=KC)
        picked = (aT_room[:, :].rearrange("p (t d) -> p t d", t=NT), a)
        wo = sb("wo", [P, KC, D])
        wgs = sb("wgs", [P, KC, E])
        bob = sb("bob", [P, D])
        ident = sb("ident", [P, P])
        earlier = sb("earlier", [P, P])
        ones = sb("ones", [P, P])
        zeros = sb("zeros", [P, D])
        stats = sb("stats", [P, NT, 6])
        mv = sb("mv", [P, NT, 2])
        std = sb("std", [P, NT])
        rstd = sb("rstd", [P, NT])
        lg = sb("lg", [P, NT, E])
        top = sb("top", [P, NT, 8])
        topi = sb("topi", [P, NT, 8], U32)
        topf = sb("topf", [P, NT, TOP])
        iota_i = sb("iota_i", [P, NBLK], I32)
        iota_f = sb("iota_f", [P, NBLK])
        diff = sb("diff", [P, NT])
        e_diff = sb("e_diff", [P, NT])
        pw = sb("pw", [P, TOP, NT])
        chosen = sb("chosen", [P, TOP, NT, E])
        mask = sb("mask", [P, NT, E])
        upto = [sb(f"upto{n}", [P, PAD + NT, E]) for n in range(2)]
        steps8 = sb("steps8", [P, 8])
        cmp = sb("cmp", [P, E, 8])
        below = sb("below", [P, E, E])
        nblk = sb("nblk", [P, E])
        first_blk = sb("first_blk", [P, E])
        slot = sb("slot", [P, NT, E])
        slot_r = sb("slot_r", [P, TOP, NT, E])
        pos_f = sb("pos_f", [P, TOP, NT])
        pos = sb("pos", [P, TOP, NT], U32)
        blk_cmp = sb("blk_cmp", [1, NBLK, E])
        blk_f = sb("blk_f", [1, NBLK])
        blk_e = sb("blk_e", [1, NBLK], I32)
        w1r = sb("w1r", [P, KC * F])
        w2r = sb("w2r", [P, FT * D])
        w1p = sb("w1p", [P, 2, 2, KC, F], F16)
        w2p = sb("w2p", [P, 2, 2, FT, D], F16)
        b1b = sb("b1b", [P, 4, FT])
        b2b = sb("b2b", [P, 4, D])
        xb = sb("xb", [P, 2, BT, D])
        xT = sb("xT", [P, 2, 2, KC, TB], F16)
        h32 = sb("h32", [P, 2, TB])
        y = sb("y", [P, 2, BT, D])

        names = ("w_in", "zeroed", "ident_made", "iota_made", "consts", "ones_made", "tri_made", "dve_step", "bias_added",
                 "var_done", "std_done", "xn_done", "pe_job", "act_job", "dve_job", "top_done", "diff_made", "exp_done",
                 "mask_made", "ranks_done", "pos_made", "blk_made", "zero_out", "xs_out", "x_turned", "x_hi", "x_lo",
                 "w1_hi", "w1_lo", "w2_hi", "w2_lo", "up_done", "relu_done", "h_split", "down_done", "y_done",
                 "added", "stored")
        s = {n: sem(n) for n in names}
        for q in range(4):
            s[f"a_in{q}"] = sem(f"a_in{q}")
            s[f"h_in{q}"] = sem(f"h_in{q}")
        for par in range(2):
            for n in ("w1_in", "w2_in", "x_in", "y_out"):
                s[f"{n}{par}"] = sem(f"{n}{par}")
        for g in range(GROUPS):
            s[f"picked_in{g}"] = sem(f"picked_in{g}")

        kinds = ([("AT", j) for j in range(16)] + [("O", j) for j in range(16)] + [("XT", j) for j in range(16)]
                 + [("G", 0)])
        jobs = ["act" if k == "XT" or (k == "AT" and j % 2) else "dve" for k, j in kinds]
        freed = {"act": s["act_job"], "dve": s["dve_job"]}
        start = {k: next(n for n, (kk, _) in enumerate(kinds) if kk == k) for k, _ in kinds}

        def before(eng, n):
            return sum(1 for e in jobs[:n] if e == eng)

        N_W = 3
        block = ctx.enter_context(nc.Block())

        def fetch_x(sp, b):
            if b >= 2:
                sp.wait_ge(s["x_turned"], KC * (b - 1))
            sp.dma_start(xb[:, b % 2].rearrange("p t d -> p (t d)"),
                         xs_dram[b * TB:b * TB + TB].rearrange("(p t) d -> p (t d)", t=BT)).then_inc(s[f"x_in{b % 2}"], 16)

        def fetch_first(sp, b):
            par = b % 2
            e = sp.value_load(blk_e[0:1, b:b + 1], min_val=0, max_val=E - 1)
            if b >= 1:
                sp.wait_ge(s["w1_lo"], b)
            if b >= 4:
                sp.wait_ge(s["relu_done"], FT * (b - 3))
            sp.dma_start(w1r[:, :].rearrange("p (c f) -> p c f", c=KC),
                         w1[bass.ds(e, 1)].rearrange("o (c p) f -> p (o c) f", p=P)).then_inc(s[f"w1_in{par}"], 16)
            sp.dma_start(b1b[:, b % 4], b1[bass.ds(e, 1)].rearrange("o (p f) -> (o p) f", f=FT)).then_inc(s[f"w1_in{par}"], 16)

        def fetch_second(sp, b):
            par = b % 2
            e = sp.value_load(blk_e[0:1, b:b + 1], min_val=0, max_val=E - 1)
            if b >= 1:
                sp.wait_ge(s["w2_lo"], b)
            if b >= 4:
                sp.wait_ge(s["y_done"], BT * (b - 3))
            sp.dma_start(w2r[:, :], w2[bass.ds(e, 1)].rearrange("o (p f) d -> (o p) (f d)", f=FT)).then_inc(s[f"w2_in{par}"], 16)
            sp.dma_start(b2b[:, b % 4], b2[bass.ds(e, 1)].broadcast_to([P, D])).then_inc(s[f"w2_in{par}"], 16)

        def store(sp, b):
            sp.wait_ge(s["y_done"], BT * (b + 1))
            sp.dma_start(ys_dram[b * TB:b * TB + TB].rearrange("(p t) d -> p (t d)", t=BT),
                         y[:, b % 2].rearrange("p t d -> p (t d)")).then_inc(s[f"y_out{b % 2}"], 16)

        @block.sync
        def _(sp):
            for dst, src in ((wo[:, :, :], woT.rearrange("(c p) n -> p c n", p=P)),
                             (wgs[:, :, :], wg.rearrange("(c p) n -> p c n", p=P)),
                             (bob[:, :], bo.partition_broadcast(P))):
                sp.dma_start(dst, src).then_inc(s["w_in"], 16)
            for q in range(4):
                t = slice(8 * q, 8 * q + 8)
                sp.dma_start(a[:, t, :], att_dram.rearrange("t p d -> p t d")[:, t, :]).then_inc(s[f"a_in{q}"], 16)
                sp.dma_start(x1[:, t, :], hidden.rearrange("o (t p) d -> p (o t) d", p=P)[:, t, :]).then_inc(s[f"h_in{q}"], 16)
            sp.wait_ge(s["zeroed"], 1)
            for b in range(NBLK):
                sp.dma_start(xs_dram[b * TB:b * TB + TB].rearrange("(p t) d -> p t d", t=BT),
                             zeros[:, :].unsqueeze(1).broadcast_to([P, BT, D])).then_inc(s["zero_out"], 16)
            sp.wait_ge(s["blk_made"], 1)
            fetch_first(sp, 0)
            fetch_second(sp, 0)
            sp.wait_ge(s["xs_out"], 16 * TOP * NT)
            for b in range(NBLK + 3):
                if b < NBLK:
                    fetch_x(sp, b)
                if 1 <= b < NBLK:
                    fetch_first(sp, b)
                if 2 <= b <= NBLK:
                    fetch_second(sp, b - 1)
                if b >= 3:
                    store(sp, b - 3)
            for g in range(GROUPS):
                t = slice(g * GT, g * GT + GT)
                sp.wait_ge(s["added"], TOP * GT * (g + 1))
                sp.dma_start(out.rearrange("o (t p) d -> p (o t) d", p=P)[:, t, :], x1[:, t, :]).then_inc(s["stored"], 16)
            sp.wait_ge(s["stored"], 16 * GROUPS)

        def split_lo(eng, unit, b, raw, parts, hi, lo):
            eng.wait_ge(s[hi], b + 1)
            unit.tensor_tensor(parts[:, b % 2, 1].rearrange("p a b -> p (a b)"), raw[:, :],
                                    parts[:, b % 2, 0].rearrange("p a b -> p (a b)"), ALU.subtract).then_inc(s[lo], 1)

        @block.gpsimd
        def _(pool):
            nc.gpsimd.memset(zeros[:, :], 0.0).then_inc(s["zeroed"], 1)
            nc.gpsimd.memset(ident[:, :], 0.0).then_inc(s["consts"], 1)
            nc.gpsimd.memset(ones[:, :], 1.0).then_inc(s["ones_made"], 1)
            for n in range(2):
                nc.gpsimd.memset(upto[n][:, 0:PAD, :], 0.0).then_inc(s["ones_made"], 1)
            nc.gpsimd.iota(iota_i[:, :], pattern=[[1, NBLK]], base=0, channel_multiplier=0).then_inc(s["iota_made"], 1)
            pool.wait_ge(s["consts"], 1)
            nc.gpsimd.affine_select(out=ident[:, :], in_=ident[:, :], compare_op=ALU.not_equal, fill=1.0, base=0,
                                    pattern=[[-1, P]], channel_multiplier=1).then_inc(s["ident_made"], 1)
            pool.wait_ge(s["ones_made"], 3)
            nc.gpsimd.affine_select(out=earlier[:, :], in_=ones[:, :], compare_op=ALU.is_gt, fill=0.0, base=0,
                                    pattern=[[1, P]], channel_multiplier=-1).then_inc(s["tri_made"], 1)
            pool.wait_ge(s["w_in"], 16 * N_W)
            for t in range(0, NT, 4):
                if t % 8 == 0:
                    pool.wait_ge(s[f"h_in{t // 8}"], 16)
                nc.gpsimd.tensor_tensor(x1[:, t:t + 4, :], x1[:, t:t + 4, :],
                                        bob[:, :].unsqueeze(1).broadcast_to([P, 4, D]), ALU.add).then_inc(s["bias_added"], 1)
            pool.wait_ge(s["pos_made"], 1)
            pool.wait_ge(s["xn_done"], NT)
            pool.wait_ge(s["zero_out"], 16 * NBLK)
            for t in range(NT):
                for r in range(TOP):
                    nc.gpsimd.indirect_dma_start(
                        out=xs_dram, out_offset=bass.IndirectOffsetOnAxis(ap=pos[:, r, t:t + 1], axis=0),
                        in_=a[:, t, :], in_offset=None).then_inc(s["xs_out"], 16)
            for b in range(NBLK):
                if b + 1 < NBLK:
                    if b == 0:
                        pool.wait_ge(s["w1_lo"], 1)
                    split_lo(pool, nc.gpsimd, b + 1, w1r, w1p, "w1_hi", "w1_lo")
                split_lo(pool, nc.gpsimd, b, w2r, w2p, "w2_hi", "w2_lo")
            pool.wait_ge(s["down_done"], BT * NBLK)
            pool.wait_ge(s["y_out0"], 16 * ((NBLK + 1) // 2))
            pool.wait_ge(s["y_out1"], 16 * (NBLK // 2))
            for t in range(NT):
                for r in range(TOP):
                    nc.gpsimd.indirect_dma_start(
                        out=picked[r][:, t, :], out_offset=None, in_=ys_dram,
                        in_offset=bass.IndirectOffsetOnAxis(ap=pos[:, r, t:t + 1], axis=0)).then_inc(
                            s[f"picked_in{t // GT}"], 16)

        def choose(dve, link):
            for t in range(NT):
                nc.vector.max(out=top[:, t], in_=lg[:, t]).then_inc(s["top_done"], 1)
            dve.wait_ge(s["top_done"], NT)
            nc.vector.tensor_tensor(diff[:, :], top[:, :, 1], top[:, :, 0], ALU.subtract).then_inc(s["diff_made"], 1)
            for t in range(NT):
                nc.vector.max_index(topi[:, t], top[:, t], lg[:, t]).then_inc(s["top_done"], 1)
            dve.wait_ge(s["iota_made"], 1)
            link(nc.vector.tensor_copy(iota_f[:, :], iota_i[:, :]))
            dve.wait_ge(s["top_done"], 2 * NT)
            link(nc.vector.tensor_copy(topf[:, :, :], topi[:, :, 0:TOP]))
            experts_b = iota_f[:, 0:E].unsqueeze(1).broadcast_to([P, NT, E])
            for r in range(TOP):
                ins = nc.vector.tensor_tensor(chosen[:, r], experts_b, topf[:, :, r:r + 1].broadcast_to([P, NT, E]), ALU.is_equal)
                link(ins)
            nc.vector.tensor_tensor(mask[:, :, :], chosen[:, 0], chosen[:, 1], ALU.add).then_inc(s["mask_made"], 1)
            dve.wait_ge(s["exp_done"], 1)
            link(nc.vector.tensor_scalar(diff[:, :], e_diff[:, :], 1.0, None, ALU.add))
            link(nc.vector.reciprocal(pw[:, 0], diff[:, :]))
            link(nc.vector.tensor_tensor(pw[:, 1], e_diff[:, :], pw[:, 0], ALU.mult))
            link(nc.vector.tensor_scalar(steps8[:, :], iota_f[:, 0:8], float(TB), None, ALU.mult))
            link(nc.vector.tensor_tensor(below[:, :, :], iota_f[:, 0:E].unsqueeze(2).broadcast_to([P, E, E]),
                                         iota_f[:, 0:E].unsqueeze(1).broadcast_to([P, E, E]), ALU.is_gt))
            dve.wait_ge(s["ranks_done"], 1)
            within = ps[:, 0, 0:NT * E].rearrange("p (t e) -> p t e", e=E)
            totals = ps[:, 1, 0:NT * E].rearrange("p (t e) -> p t e", e=E)
            link(nc.vector.tensor_copy(upto[0][:, PAD:, :], totals))
            src, k = 0, 1
            while k < NT:
                link(nc.vector.tensor_tensor(upto[1 - src][:, PAD:, :], upto[src][:, PAD:, :],
                                             upto[src][:, PAD - k:PAD + NT - k, :], ALU.add))
                src, k = 1 - src, 2 * k
            summed = upto[src]
            link(nc.vector.tensor_tensor(cmp[:, :, :], summed[:, PAD + NT - 1, :].unsqueeze(2).broadcast_to([P, E, 8]),
                                         steps8[:, :].unsqueeze(1).broadcast_to([P, E, 8]), ALU.is_gt))
            link(nc.vector.tensor_reduce(nblk[:, :], cmp[:, :, :], AX.X, ALU.add))
            link(nc.vector.tensor_tensor(below[:, :, :], below[:, :, :],
                                         nblk[:, :].unsqueeze(1).broadcast_to([P, E, E]), ALU.mult))
            link(nc.vector.tensor_reduce(first_blk[:, :], below[:, :, :], AX.X, ALU.add))
            link(nc.vector.tensor_tensor(slot[:, :, :], summed[:, PAD - 1:PAD + NT - 1, :], within, ALU.add))
            link(nc.vector.scalar_tensor_tensor(out=slot[:, :, :], in0=first_blk[:, :].unsqueeze(1).broadcast_to([P, NT, E]),
                                                scalar=float(TB), in1=slot[:, :, :], op0=ALU.mult, op1=ALU.add))
            for r in range(TOP):
                link(nc.vector.tensor_tensor(slot_r[:, r], chosen[:, r], slot[:, :, :], ALU.mult))
            for r in range(TOP):
                link(nc.vector.tensor_reduce(pos_f[:, r], slot_r[:, r], AX.X, ALU.add))
            nc.vector.tensor_copy(pos[:, :, :], pos_f[:, :, :]).then_inc(s["pos_made"], 1)
            link(nc.vector.tensor_tensor(blk_cmp[:, :, :], iota_f[0:1, :].unsqueeze(2).broadcast_to([1, NBLK, E]),
                                         first_blk[0:1, :].unsqueeze(1).broadcast_to([1, NBLK, E]), ALU.is_ge))
            link(nc.vector.tensor_reduce(blk_f[:, :], blk_cmp[:, :, :], AX.X, ALU.add))
            link(nc.vector.tensor_scalar(blk_f[:, :], blk_f[:, :], -1.0, None, ALU.add))
            nc.vector.tensor_copy(blk_e[:, :], blk_f[:, :]).then_inc(s["blk_made"], 1)

        def split_x(dve, b):
            for c in range(KC):
                dve.wait_ge(s["x_hi"], KC * b + c + 1)
                nc.vector.tensor_tensor(xT[:, b % 2, 1, c], ps[:, 6 + c, :], xT[:, b % 2, 0, c],
                                        ALU.subtract).then_inc(s["x_lo"], 1)

        @block.vector
        def _(dve):
            chain = [0]

            def link(ins):
                chain[0] += 1
                ins.then_inc(s["dve_step"], 1)
                dve.wait_ge(s["dve_step"], chain[0])

            def layer_stats(j):
                for t in (2 * j, 2 * j + 1):
                    nc.vector.bn_stats(stats[:, t], x1[:, t]).then_inc(s["dve_step"], 1)
                    chain[0] += 1

            for n, (kind, j) in enumerate(kinds):
                if n == start["XT"]:
                    dve.wait_ge(s["dve_job"], before("dve", n))
                    layer_stats(15)
                    dve.wait_ge(s["dve_step"], chain[0])
                    for t in range(NT):
                        nc.vector.bn_aggr(mv[:, t], stats[:, t]).then_inc(s["dve_step"], 1)
                        chain[0] += 1
                    dve.wait_ge(s["dve_step"], chain[0])
                    nc.vector.tensor_scalar(rstd[:, :], mv[:, :, 1], EPS, None, ALU.add).then_inc(s["var_done"], 1)
                    dve.wait_ge(s["std_done"], 1)
                    link(nc.vector.reciprocal(rstd[:, :], std[:, :]))
                    for t in range(NT):
                        nc.vector.tensor_scalar(a[:, t], x1[:, t], mv[:, t, 0:1], rstd[:, t:t + 1], ALU.subtract,
                                                ALU.mult).then_inc(s["xn_done"], 1)
                if jobs[n] != "dve":
                    continue
                if kind == "O" and j % 2 == 0:
                    dve.wait_ge(s["bias_added"], j // 2 + 1)
                dve.wait_ge(s["pe_job"], n + 1)
                bank = ps[:, n % 8, :]
                if kind == "AT":
                    nc.vector.tensor_copy(aT[:, j % 2, (j // 2) * 512:(j // 2) * 512 + 512], bank).then_inc(s["dve_job"], 1)
                if kind == "O":
                    nc.vector.tensor_tensor(x1[:, 2 * j:2 * j + 2, :], x1[:, 2 * j:2 * j + 2, :],
                                            bank.rearrange("p (t d) -> p t d", t=2), ALU.add).then_inc(s["dve_job"], 1)
                    if j:
                        dve.wait_ge(s["dve_job"], before("dve", n))
                        layer_stats(j - 1)
                if kind == "G":
                    nc.vector.tensor_copy(lg[:, :, :], bank[:, 0:NT * E].rearrange("p (t e) -> p t e", e=E)).then_inc(s["dve_job"], 1)
                    dve.wait_ge(s["dve_job"], before("dve", n) + 1)
            choose(dve, link)
            split_lo(dve, nc.vector, 0, w1r, w1p, "w1_hi", "w1_lo")
            split_x(dve, 0)
            for b in range(NBLK + 1):
                if b < NBLK:
                    if b >= 2:
                        dve.wait_ge(s["down_done"], BT * (b - 1))
                    for f in range(FT):
                        n = b * FT + f
                        dve.wait_ge(s["relu_done"], n + 1)
                        nc.vector.tensor_copy(hT[:, b % 2, 0, f], h32[:, n % 2]).then_inc(s["h_split"], 1)
                        dve.wait_ge(s["h_split"], 2 * n + 1)
                        nc.vector.tensor_tensor(hT[:, b % 2, 1, f], h32[:, n % 2], hT[:, b % 2, 0, f],
                                                ALU.subtract).then_inc(s["h_split"], 1)
                    if b + 1 < NBLK:
                        split_x(dve, b + 1)
                if b > 0:
                    par, nth = (b - 1) % 2, (b - 1) // 2
                    dve.wait_ge(s[f"w2_in{par}"], 32 * nth + 32)
                    if nth:
                        dve.wait_ge(s[f"y_out{par}"], 16 * nth)
                    for t in range(BT):
                        d = BT * (b - 1) + t
                        dve.wait_ge(s["down_done"], d + 1)
                        nc.vector.tensor_tensor(y[:, par, t], ps[:, 4 + d % 2, 0:D], b2b[:, (b - 1) % 4],
                                                ALU.add).then_inc(s["y_done"], 1)
            for g in range(GROUPS):
                dve.wait_ge(s[f"picked_in{g}"], 16 * TOP * GT)
                for r in range(TOP):
                    if r:
                        dve.wait_ge(s["added"], TOP * GT * g + GT)
                    for t in range(g * GT, g * GT + GT):
                        nc.vector.scalar_tensor_tensor(out=x1[:, t], in0=picked[r][:, t], scalar=pw[:, r, t:t + 1],
                                                       in1=x1[:, t], op0=ALU.mult, op1=ALU.add).then_inc(s["added"], 1)

        def split_hi(act, b, raw, parts, arrived, hi):
            act.wait_ge(s[f"{arrived}{b % 2}"], 32 * (b // 2) + 32)
            nc.scalar.copy(parts[:, b % 2, 0].rearrange("p a b -> p (a b)"), raw[:, :]).then_inc(s[hi], 1)

        def take_x(act, b):
            if b >= 2:
                act.wait_ge(s["up_done"], FT * (b - 1))
            for c in range(KC):
                act.wait_ge(s["x_turned"], KC * b + c + 1)
                nc.scalar.copy(xT[:, b % 2, 0, c], ps[:, 6 + c, :]).then_inc(s["x_hi"], 1)

        @block.scalar
        def _(act):
            for n, (kind, j) in enumerate(kinds):
                if n == start["XT"]:
                    act.wait_ge(s["var_done"], 1)
                    nc.scalar.activation(std[:, :], rstd[:, :], ACT.Sqrt).then_inc(s["std_done"], 1)
                if jobs[n] != "act":
                    continue
                act.wait_ge(s["pe_job"], n + 1)
                nc.scalar.copy(aT[:, j % 2, (j // 2) * 512:(j // 2) * 512 + 512], ps[:, n % 8, :]).then_inc(s["act_job"], 1)
            act.wait_ge(s["diff_made"], 1)
            nc.scalar.activation(e_diff[:, :], diff[:, :], ACT.Exp).then_inc(s["exp_done"], 1)
            split_hi(act, 0, w1r, w1p, "w1_in", "w1_hi")
            take_x(act, 0)
            for b in range(NBLK):
                for f in range(FT):
                    n = b * FT + f
                    act.wait_ge(s["up_done"], n + 1)
                    if n >= 2:
                        act.wait_ge(s["h_split"], 2 * (n - 1))
                    nc.scalar.activation(h32[:, n % 2], ps[:, n % 4, :], ACT.Relu, bias=b1b[:, b % 4, f:f + 1]).then_inc(
                        s["relu_done"], 1)
                    if f == 3 and b + 1 < NBLK:
                        if b >= 1:
                            act.wait_ge(s["up_done"], FT * b)
                        split_hi(act, b + 1, w1r, w1p, "w1_in", "w1_hi")
                    if f == 5:
                        if b >= 2:
                            act.wait_ge(s["down_done"], BT * (b - 1))
                        split_hi(act, b, w2r, w2p, "w2_in", "w2_hi")
                if b + 1 < NBLK:
                    take_x(act, b + 1)

        def turn_x(pe, b):
            pe.wait_ge(s[f"x_in{b % 2}"], 16 * (b // 2) + 16)
            if b >= 1:
                pe.wait_ge(s["x_lo"], KC * b)
            for c in range(KC):
                for t in range(BT):
                    ins = pe.transpose(ps[:, 6 + c, t * P:t * P + P], xb[:, b % 2, t, c * P:c * P + P], ident[:, :])
                ins.then_inc(s["x_turned"], 1)

        @block.tensor
        def _(pe):
            pe.wait_ge(s["w_in"], 16 * N_W)
            pe.wait_ge(s["ident_made"], 1)
            for n, (kind, j) in enumerate(kinds):
                own = bank_owner(jobs, n)
                if own:
                    pe.wait_ge(freed[own[0]], own[1])
                if n in (start["O"], start["G"]):
                    pe.wait_ge(s["act_job"], before("act", n))
                    pe.wait_ge(s["dve_job"], before("dve", n))
                if kind in ("AT", "XT"):
                    c, tb = j % 2, j // 2
                    if kind == "XT":
                        pe.wait_ge(s["xn_done"], 4 * tb + 4)
                    elif j % 4 == 0:
                        pe.wait_ge(s[f"a_in{j // 4}"], 16)
                    for t in range(4):
                        ins = pe.transpose(ps[:, n % 8, t * P:t * P + P], a[:, 4 * tb + t, c * P:c * P + P], ident[:, :])
                if kind == "O":
                    for t in range(2):
                        tile = 2 * j + t
                        for c in range(KC):
                            ins = pe.matmul(ps[:, n % 8, t * D:t * D + D], aT[:, c, tile * P:tile * P + P], wo[:, c, :],
                                            start=(c == 0), stop=(c == KC - 1))
                if kind == "G":
                    for t in range(NT):
                        for c in range(KC):
                            ins = pe.matmul(ps[:, n % 8, t * E:t * E + E], aT[:, c, t * P:t * P + P], wgs[:, c, :],
                                            start=(c == 0), stop=(c == KC - 1))
                ins.then_inc(s["pe_job"], 1)
            pe.wait_ge(s["dve_job"], before("dve", len(kinds)))
            pe.wait_ge(s["act_job"], before("act", len(kinds)))
            pe.wait_ge(s["tri_made"], 1)
            pe.wait_ge(s["mask_made"], 1)
            flat = mask[:, :, :].rearrange("p t e -> p (t e)")
            pe.matmul(ps[:, 0, 0:NT * E], earlier[:, :], flat, start=True, stop=True)
            pe.matmul(ps[:, 1, 0:NT * E], ones[:, :], flat, start=True, stop=True).then_inc(s["ranks_done"], 1)
            parts = ((0, 0), (1, 0), (0, 1))
            turn_x(pe, 0)
            pe.wait_ge(s["pos_made"], 1)
            for b in range(NBLK + 1):
                if b < NBLK:
                    pe.wait_ge(s["w1_lo"], b + 1)
                    pe.wait_ge(s["x_lo"], KC * (b + 1))
                    for f in range(FT):
                        n = b * FT + f
                        if n >= 4:
                            pe.wait_ge(s["relu_done"], n - 3)
                        for c in range(KC):
                            for wp, xp in parts:
                                ins = pe.matmul(ps[:, n % 4, :], w1p[:, b % 2, wp, c, f:F:FT], xT[:, b % 2, xp, c],
                                                start=(c == 0 and wp == 0 and xp == 0), stop=(c == KC - 1 and xp == 1))
                        ins.then_inc(s["up_done"], 1)
                    if b + 1 < NBLK:
                        turn_x(pe, b + 1)
                if b > 0:
                    pe.wait_ge(s["w2_lo"], b)
                    pe.wait_ge(s["h_split"], 2 * FT * b)
                    for t in range(BT):
                        d = BT * (b - 1) + t
                        if d >= 2:
                            pe.wait_ge(s["y_done"], d - 1)
                        for f in range(FT):
                            for hp, wp in parts:
                                ins = pe.matmul(ps[:, 4 + d % 2, 0:D], hT[:, (b - 1) % 2, hp, f, t * P:t * P + P],
                                                w2p[:, (b - 1) % 2, wp, f, :], start=(f == 0 and hp == 0 and wp == 0),
                                                stop=(f == FT - 1 and wp == 1))
                        ins.then_inc(s["down_done"], 1)


def preln_attention_moe_kernel(nc, hidden, wqT, bq, wkT, bk, wvT, bv, woT, bo, relT, rel_b, lbT, gwT, gate_b,
                               wg, w1, b1, w2, b2, out):
    with ExitStack() as ctx:
        def dram(name, shape, dt=F32):
            return nc.dram_tensor(name, shape, dt, kind="Internal").ap()

        q_dram = dram("q_stacks", (NT, 2, 64, PAIRS, P), F16)
        c_dram = dram("c_values", (NT, 3, 2, P, H), F16)
        dj_dram = dram("key_logits", (3, S))
        const_dram = dram("query_consts", (NT, P, H + 4))
        r_dram = dram("relation_parts", (NT, UNITS, 2, 2, P, JU), F16)
        m_dram = dram("row_maxima", (H, 3, P), F16)
        att_dram = dram("attention_out", (NT, P, D))
        with ExitStack() as attention:
            kst = attention.enter_context(nc.sbuf_tensor("kst", [P, PAIRS, S], F16))
            vp = attention.enter_context(nc.sbuf_tensor("vp", [P, NT, VPAD], F32))
            project_inputs(nc, kst, vp, hidden, wqT, bq, wkT, bk, wvT, bv, relT, rel_b, lbT, gwT, gate_b,
                           q_dram, c_dram, const_dram, dj_dram)
            attend(nc, kst, vp, dj_dram, q_dram, c_dram, const_dram, r_dram, m_dram, att_dram)
        xs_dram = dram("expert_tokens", (NBLK * TB, D))
        ys_dram = dram("expert_results", (NBLK * TB, D))
        experts(nc, hidden, woT, bo, wg, w1, b1, w2, b2, att_dram, xs_dram, ys_dram, out)


_INS = [("L0_attn_hidden_states", False), ("L0_attn_Wq", True), ("L0_attn_bq", False), ("L0_attn_Wk", True),
        ("L0_attn_bk", False), ("L0_attn_Wv", True), ("L0_attn_bv", False), ("L0_attn_Wo", True),
        ("L0_attn_bo", False), ("L0_attn_rel_W", True), ("L0_attn_rel_b", False), ("L0_attn_logical_bias", True),
        ("L0_attn_gate_W", True), ("L0_attn_gate_b", False), ("L0_ffn_Wg", False), ("L0_ffn_W1", False),
        ("L0_ffn_b1", False), ("L0_ffn_W2", False), ("L0_ffn_b2", False)]


def kernel(**inputs):
    import numpy as _np
    import concourse.bacc as _bacc
    from concourse import mybir as _mybir
    from concourse.bass_utils import run_bass_kernel_spmd as _run

    nc = _bacc.Bacc("TRN2", target_bir_lowering=False, num_devices=1)
    arrays, args = {}, []
    for name, turned in _INS:
        a = _np.asarray(inputs[name])
        a = _np.ascontiguousarray(a.T if turned else a)
        arrays[f"in_{name}_dram"] = a
        args.append(nc.dram_tensor(f"in_{name}_dram", a.shape, _mybir.dt.from_np(a.dtype), kind="ExternalInput").ap())
    args.append(nc.dram_tensor("out_0_dram", (1, S, D), _mybir.dt.float32, kind="ExternalOutput").ap())
    preln_attention_moe_kernel(nc, *args)
    r = _run(nc, [arrays], core_ids=[0])
    return r.results[0]["out_0_dram"]
```
